# Optimizing a Trainium2 kernel written in Bass

```python
import numpy as np
import jax
import jax.numpy as jnp

def _softmax(x, axis=-1):
    return jax.nn.softmax(x, axis=axis)

def _gelu(x):
    return jax.nn.gelu(x, approximate=True)

def _silu(x):
    return jax.nn.silu(x)

def _sigmoid(x):
    return jax.nn.sigmoid(x)

def _layernorm(x, axis=-1, eps=1e-05):
    m = jnp.mean(x, axis=axis, keepdims=True)
    v = jnp.var(x, axis=axis, keepdims=True)
    return (x - m) / jnp.sqrt(v + eps)

def _scatter_add(tgt, idx, src, axis=0):
    return tgt.at[idx].add(src)

def _segment_sum(src, seg, n):
    return jax.ops.segment_sum(src, seg, n)
kernel_name = 'mk_vit_tower_d1_tok_img768_r4_f3a22c'

def setup_inputs(seed: int=0):
    np.random.seed(seed)
    _w = jnp.asarray

    def _rec_inputs():
        import jax
        import jax.numpy as jnp
        _rk = jax.random.key(seed)
        x = 7.57192e-06 + 1.00007 * jax.random.normal(jax.random.fold_in(_rk, 1), (8, 3, 96, 96), jnp.float32)
        return x
    x = _rec_inputs()

    def _L0_tok_setup():
        import jax, jax.numpy as jnp
        import numpy as np
        QMAX = 127.0

        def fake_quant(v):
            s = jnp.maximum(jnp.max(jnp.abs(v)), 1e-08) / QMAX
            return jnp.round(jnp.clip(v / s, -QMAX, QMAX)) * s
        key = jax.random.key(seed)
        k1, k2, k3 = jax.random.split(key, 3)
        B, C, H, W = (64, 3, 224, 224)
        D, P = (192, 8)
        x = jax.random.normal(k1, (B, C, H, W), dtype=jnp.float32)
        w = jax.random.normal(k2, (D, C, P, P), dtype=jnp.float32) * 0.02
        b = jax.random.normal(k3, (D,), dtype=jnp.float32) * 0.02
        return {'x': x, 'w': w, 'b': b}
    _L0_tok_all = _L0_tok_setup()
    _L0_tok_in = {k: v for k, v in _L0_tok_all.items() if k in ('w', 'b')}
    del _L0_tok_all

    def _L0_attn_setup():
        import jax, jax.numpy as jnp
        import numpy as np
        from jax import lax
        D_MODEL = 192
        D_STATE = 64
        D_CONV = 4
        EXPAND = 2
        HEADDIM = 64
        D_INNER = EXPAND * D_MODEL
        NHEADS = D_INNER // HEADDIM
        NGROUPS = 1
        CONV_DIM = D_INNER + 2 * NGROUPS * D_STATE
        D_IN_PROJ = 2 * D_INNER + 2 * NGROUPS * D_STATE + NHEADS
        EPS = 1e-05

        def _mamba2(x, W_in, conv_w, conv_b, dt_bias, A_log, D, norm_w, W_out):
            B, L, _ = x.shape
            zxbcdt = x @ W_in
            z = zxbcdt[..., :D_INNER]
            xBC = zxbcdt[..., D_INNER:D_INNER + CONV_DIM]
            dt = zxbcdt[..., D_INNER + CONV_DIM:]
            dt = jax.nn.softplus(dt + dt_bias)
            xp = jnp.pad(xBC, ((0, 0), (D_CONV - 1, 0), (0, 0)))
            conv = sum((xp[:, k:k + L, :] * conv_w[:, k] for k in range(D_CONV)))
            xBC = jax.nn.silu(conv + conv_b)
            xs = xBC[..., :D_INNER].reshape(B, L, NHEADS, HEADDIM)
            Bm = xBC[..., D_INNER:D_INNER + D_STATE]
            Cm = xBC[..., D_INNER + D_STATE:]
            A = -jnp.exp(A_log)
            dA = jnp.exp(dt * A)

            def step(h, inp):
                dA_t, dt_t, x_t, B_t, C_t = inp
                h = h * dA_t[:, :, None, None] + (dt_t[:, :, None] * x_t)[..., None] * B_t[:, None, None, :]
                y = jnp.einsum('bhpn,bn->bhp', h, C_t)
                return (h, y)
            inps = (jnp.moveaxis(dA, 1, 0), jnp.moveaxis(dt, 1, 0), jnp.moveaxis(xs, 1, 0), jnp.moveaxis(Bm, 1, 0), jnp.moveaxis(Cm, 1, 0))
            h0 = jnp.zeros((B, NHEADS, HEADDIM, D_STATE), x.dtype)
            _, ys = lax.scan(step, h0, inps)
            y = jnp.moveaxis(ys, 0, 1) + D[None, None, :, None] * xs
            y = y.reshape(B, L, D_INNER)
            y = y * jax.nn.silu(z)
            y = y * lax.rsqrt(jnp.mean(y * y, axis=-1, keepdims=True) + EPS) * norm_w
            return y @ W_out
        key = jax.random.key(seed)
        ks = jax.random.split(key, 8)
        B, L = (2, 1024)
        x = jax.random.normal(ks[0], (B, L, D_MODEL), jnp.float32)
        W_in = jax.random.normal(ks[1], (D_MODEL, D_IN_PROJ), jnp.float32) * D_MODEL ** (-0.5)
        conv_w = jax.random.normal(ks[2], (CONV_DIM, D_CONV), jnp.float32) * 0.2
        conv_b = jnp.zeros((CONV_DIM,), jnp.float32)
        dt = jax.random.uniform(ks[3], (NHEADS,), jnp.float32, 0.001, 0.1)
        dt_bias = dt + jnp.log(-jnp.expm1(-dt))
        A_log = jnp.log(jax.random.uniform(ks[4], (NHEADS,), jnp.float32, 1.0, 16.0))
        D = jnp.ones((NHEADS,), jnp.float32)
        norm_w = jnp.ones((D_INNER,), jnp.float32)
        W_out = jax.random.normal(ks[5], (D_INNER, D_MODEL), jnp.float32) * D_INNER ** (-0.5)
        return {'x': x, 'W_in': W_in, 'conv_w': conv_w, 'conv_b': conv_b, 'dt_bias': dt_bias, 'A_log': A_log, 'D': D, 'norm_w': norm_w, 'W_out': W_out}
    _L0_attn_all = _L0_attn_setup()
    _L0_attn_in = {k: v for k, v in _L0_attn_all.items() if k in ('W_in', 'conv_w', 'conv_b', 'dt_bias', 'A_log', 'D', 'norm_w', 'W_out')}
    del _L0_attn_all

    def _L0_ffn_setup():
        import math
        import jax, jax.numpy as jnp
        import numpy as np
        N_HEAD = 12
        N_EXP = 8
        TOP_K = 2
        TRAIN_CAPACITY = 1.25
        MIN_CAPACITY = 4
        LN_EPS = 1e-05
        NEG_INF = -1e+30

        def _layer_norm(x, w, b):
            mu = jnp.mean(x, axis=-1, keepdims=True)
            var = jnp.var(x, axis=-1, keepdims=True)
            return (x - mu) * jax.lax.rsqrt(var + LN_EPS) * w + b

        def _attention(x, qkv_w, qkv_b, proj_w, proj_b):
            B, T, C = x.shape
            H, D = (N_HEAD, C // N_HEAD)
            qkv = x @ qkv_w + qkv_b
            q, k, v = jnp.split(qkv, 3, axis=-1)
            q = q.reshape(B, T, H, D).transpose(0, 2, 1, 3)
            k = k.reshape(B, T, H, D).transpose(0, 2, 1, 3)
            v = v.reshape(B, T, H, D).transpose(0, 2, 1, 3)
            scores = jnp.einsum('bhqd,bhkd->bhqk', q, k) / math.sqrt(D)
            causal = jnp.tril(jnp.ones((T, T), bool))
            scores = jnp.where(causal, scores, NEG_INF)
            attn = jax.nn.softmax(scores, axis=-1)
            y = jnp.einsum('bhqk,bhkd->bhqd', attn, v)
            y = y.transpose(0, 2, 1, 3).reshape(B, T, C)
            return y @ proj_w + proj_b

        def _moe(x, w_g, fc_w, fc_b, pj_w, pj_b):
            B, T, C = x.shape
            N, E, K = (B * T, N_EXP, TOP_K)
            cap = int(math.floor(K * TRAIN_CAPACITY * N / E))
            cap += cap % 2
            cap = max(cap, MIN_CAPACITY)
            logits = (x @ w_g).reshape(N, E)
            _, topk_idx = jax.lax.top_k(logits, K)
            hot = jax.nn.one_hot(topk_idx, E, dtype=jnp.int32)
            sel = hot.sum(axis=1) > 0
            router_probs = jax.nn.softmax(jnp.where(sel, logits, NEG_INF), axis=-1)
            exp_mask = hot.transpose(1, 0, 2)
            exp_rank = jnp.cumsum(exp_mask.reshape(K * N, E), axis=0) - 1
            exp_rank = exp_rank.reshape(K, N, E)
            exp_mask = exp_mask * (exp_rank < cap).astype(jnp.int32)
            exp_rank = jnp.sum(exp_mask * exp_rank, axis=-1)
            exp_weights = exp_mask.astype(x.dtype) * router_probs[None]
            rank_sc = jax.nn.one_hot(exp_rank, cap, dtype=x.dtype)
            cb_weight = jnp.einsum('kne,knc->nec', exp_weights, rank_sc)
            sec_mask = (cb_weight != 0).astype(x.dtype)
            xf = x.reshape(N, C)
            xb = jnp.einsum('nec,nd->ecd', sec_mask, xf)
            h = jax.nn.gelu(jnp.einsum('ecd,edf->ecf', xb, fc_w) + fc_b, approximate=False)
            out = jnp.einsum('ecf,efd->ecd', h, pj_w) + pj_b
            y = jnp.einsum('nec,ecd->nd', cb_weight, out)
            return y.reshape(B, T, C)
        key = jax.random.key(seed)
        ks = jax.random.split(key, 12)
        B, T, C = (4, 256, 192)
        E, F = (N_EXP, 4 * C)
        s = 0.02
        return {'x': jax.random.normal(ks[0], (B, T, C), jnp.float32), 'ln1_w': jnp.ones((C,), jnp.float32), 'ln1_b': jnp.zeros((C,), jnp.float32), 'ln2_w': jnp.ones((C,), jnp.float32), 'ln2_b': jnp.zeros((C,), jnp.float32), 'attn_qkv_w': jax.random.normal(ks[1], (C, 3 * C), jnp.float32) * s, 'attn_qkv_b': jnp.zeros((3 * C,), jnp.float32), 'attn_proj_w': jax.random.normal(ks[2], (C, C), jnp.float32) * s, 'attn_proj_b': jnp.zeros((C,), jnp.float32), 'w_g': jax.random.normal(ks[3], (C, E), jnp.float32) * s, 'exp_fc_w': jax.random.normal(ks[4], (E, C, F), jnp.float32) * s, 'exp_fc_b': jnp.zeros((E, 1, F), jnp.float32), 'exp_proj_w': jax.random.normal(ks[5], (E, F, C), jnp.float32) * s, 'exp_proj_b': jnp.zeros((E, 1, C), jnp.float32)}
    _L0_ffn_all = _L0_ffn_setup()
    _L0_ffn_in = {k: v for k, v in _L0_ffn_all.items() if k in ('ln1_w', 'ln1_b', 'ln2_w', 'ln2_b', 'attn_qkv_w', 'attn_qkv_b', 'attn_proj_w', 'attn_proj_b', 'w_g', 'exp_fc_w', 'exp_fc_b', 'exp_proj_w', 'exp_proj_b')}
    del _L0_ffn_all
    return {'x': x, 'L0_tok_w': _L0_tok_in['w'], 'L0_tok_b': _L0_tok_in['b'], 'L0_attn_W_in': _L0_attn_in['W_in'], 'L0_attn_conv_w': _L0_attn_in['conv_w'], 'L0_attn_conv_b': _L0_attn_in['conv_b'], 'L0_attn_dt_bias': _L0_attn_in['dt_bias'], 'L0_attn_A_log': _L0_attn_in['A_log'], 'L0_attn_D': _L0_attn_in['D'], 'L0_attn_norm_w': _L0_attn_in['norm_w'], 'L0_attn_W_out': _L0_attn_in['W_out'], 'L0_ffn_ln1_w': _L0_ffn_in['ln1_w'], 'L0_ffn_ln1_b': _L0_ffn_in['ln1_b'], 'L0_ffn_ln2_w': _L0_ffn_in['ln2_w'], 'L0_ffn_ln2_b': _L0_ffn_in['ln2_b'], 'L0_ffn_attn_qkv_w': _L0_ffn_in['attn_qkv_w'], 'L0_ffn_attn_qkv_b': _L0_ffn_in['attn_qkv_b'], 'L0_ffn_attn_proj_w': _L0_ffn_in['attn_proj_w'], 'L0_ffn_attn_proj_b': _L0_ffn_in['attn_proj_b'], 'L0_ffn_w_g': _L0_ffn_in['w_g'], 'L0_ffn_exp_fc_w': _L0_ffn_in['exp_fc_w'], 'L0_ffn_exp_fc_b': _L0_ffn_in['exp_fc_b'], 'L0_ffn_exp_proj_w': _L0_ffn_in['exp_proj_w'], 'L0_ffn_exp_proj_b': _L0_ffn_in['exp_proj_b']}

def reference(x, L0_tok_w, L0_tok_b, L0_attn_W_in, L0_attn_conv_w, L0_attn_conv_b, L0_attn_dt_bias, L0_attn_A_log, L0_attn_D, L0_attn_norm_w, L0_attn_W_out, L0_ffn_ln1_w, L0_ffn_ln1_b, L0_ffn_ln2_w, L0_ffn_ln2_b, L0_ffn_attn_qkv_w, L0_ffn_attn_qkv_b, L0_ffn_attn_proj_w, L0_ffn_attn_proj_b, L0_ffn_w_g, L0_ffn_exp_fc_w, L0_ffn_exp_fc_b, L0_ffn_exp_proj_w, L0_ffn_exp_proj_b):
    import jax
    import jax.numpy as jnp

    def _L0_tok_ref(x, w, b):
        import jax, jax.numpy as jnp
        import numpy as np
        QMAX = 127.0

        def fake_quant(v):
            s = jnp.maximum(jnp.max(jnp.abs(v)), 1e-08) / QMAX
            return jnp.round(jnp.clip(v / s, -QMAX, QMAX)) * s
        B, C, H, W = x.shape
        D, _, P, _ = w.shape
        gh, gw = (H // P, W // P)
        xq = fake_quant(x)
        wq = fake_quant(w)
        xp = xq.reshape(B, C, gh, P, gw, P)
        out = jnp.einsum('bchpwq,dchq->bhwd', xp.transpose(0, 1, 2, 3, 4, 5), wq, optimize=True) if False else jnp.einsum('bcxpyq,dcpq->bxyd', xp, wq)
        out = out + b
        out = out.reshape(B, gh * gw, D)
        return out

    def _L0_attn_ref(x, W_in, conv_w, conv_b, dt_bias, A_log, D, norm_w, W_out):
        import jax, jax.numpy as jnp
        import numpy as np
        from jax import lax
        D_MODEL = 192
        D_STATE = 64
        D_CONV = 4
        EXPAND = 2
        HEADDIM = 64
        D_INNER = EXPAND * D_MODEL
        NHEADS = D_INNER // HEADDIM
        NGROUPS = 1
        CONV_DIM = D_INNER + 2 * NGROUPS * D_STATE
        D_IN_PROJ = 2 * D_INNER + 2 * NGROUPS * D_STATE + NHEADS
        EPS = 1e-05

        def _mamba2(x, W_in, conv_w, conv_b, dt_bias, A_log, D, norm_w, W_out):
            B, L, _ = x.shape
            zxbcdt = x @ W_in
            z = zxbcdt[..., :D_INNER]
            xBC = zxbcdt[..., D_INNER:D_INNER + CONV_DIM]
            dt = zxbcdt[..., D_INNER + CONV_DIM:]
            dt = jax.nn.softplus(dt + dt_bias)
            xp = jnp.pad(xBC, ((0, 0), (D_CONV - 1, 0), (0, 0)))
            conv = sum((xp[:, k:k + L, :] * conv_w[:, k] for k in range(D_CONV)))
            xBC = jax.nn.silu(conv + conv_b)
            xs = xBC[..., :D_INNER].reshape(B, L, NHEADS, HEADDIM)
            Bm = xBC[..., D_INNER:D_INNER + D_STATE]
            Cm = xBC[..., D_INNER + D_STATE:]
            A = -jnp.exp(A_log)
            dA = jnp.exp(dt * A)

            def step(h, inp):
                dA_t, dt_t, x_t, B_t, C_t = inp
                h = h * dA_t[:, :, None, None] + (dt_t[:, :, None] * x_t)[..., None] * B_t[:, None, None, :]
                y = jnp.einsum('bhpn,bn->bhp', h, C_t)
                return (h, y)
            inps = (jnp.moveaxis(dA, 1, 0), jnp.moveaxis(dt, 1, 0), jnp.moveaxis(xs, 1, 0), jnp.moveaxis(Bm, 1, 0), jnp.moveaxis(Cm, 1, 0))
            h0 = jnp.zeros((B, NHEADS, HEADDIM, D_STATE), x.dtype)
            _, ys = lax.scan(step, h0, inps)
            y = jnp.moveaxis(ys, 0, 1) + D[None, None, :, None] * xs
            y = y.reshape(B, L, D_INNER)
            y = y * jax.nn.silu(z)
            y = y * lax.rsqrt(jnp.mean(y * y, axis=-1, keepdims=True) + EPS) * norm_w
            return y @ W_out
        return _mamba2(x, W_in, conv_w, conv_b, dt_bias, A_log, D, norm_w, W_out)

    def _L0_ffn_ref(x, ln1_w, ln1_b, ln2_w, ln2_b, attn_qkv_w, attn_qkv_b, attn_proj_w, attn_proj_b, w_g, exp_fc_w, exp_fc_b, exp_proj_w, exp_proj_b):
        import math
        import jax, jax.numpy as jnp
        import numpy as np
        N_HEAD = 12
        N_EXP = 8
        TOP_K = 2
        TRAIN_CAPACITY = 1.25
        MIN_CAPACITY = 4
        LN_EPS = 1e-05
        NEG_INF = -1e+30

        def _layer_norm(x, w, b):
            mu = jnp.mean(x, axis=-1, keepdims=True)
            var = jnp.var(x, axis=-1, keepdims=True)
            return (x - mu) * jax.lax.rsqrt(var + LN_EPS) * w + b

        def _attention(x, qkv_w, qkv_b, proj_w, proj_b):
            B, T, C = x.shape
            H, D = (N_HEAD, C // N_HEAD)
            qkv = x @ qkv_w + qkv_b
            q, k, v = jnp.split(qkv, 3, axis=-1)
            q = q.reshape(B, T, H, D).transpose(0, 2, 1, 3)
            k = k.reshape(B, T, H, D).transpose(0, 2, 1, 3)
            v = v.reshape(B, T, H, D).transpose(0, 2, 1, 3)
            scores = jnp.einsum('bhqd,bhkd->bhqk', q, k) / math.sqrt(D)
            causal = jnp.tril(jnp.ones((T, T), bool))
            scores = jnp.where(causal, scores, NEG_INF)
            attn = jax.nn.softmax(scores, axis=-1)
            y = jnp.einsum('bhqk,bhkd->bhqd', attn, v)
            y = y.transpose(0, 2, 1, 3).reshape(B, T, C)
            return y @ proj_w + proj_b

        def _moe(x, w_g, fc_w, fc_b, pj_w, pj_b):
            B, T, C = x.shape
            N, E, K = (B * T, N_EXP, TOP_K)
            cap = int(math.floor(K * TRAIN_CAPACITY * N / E))
            cap += cap % 2
            cap = max(cap, MIN_CAPACITY)
            logits = (x @ w_g).reshape(N, E)
            _, topk_idx = jax.lax.top_k(logits, K)
            hot = jax.nn.one_hot(topk_idx, E, dtype=jnp.int32)
            sel = hot.sum(axis=1) > 0
            router_probs = jax.nn.softmax(jnp.where(sel, logits, NEG_INF), axis=-1)
            exp_mask = hot.transpose(1, 0, 2)
            exp_rank = jnp.cumsum(exp_mask.reshape(K * N, E), axis=0) - 1
            exp_rank = exp_rank.reshape(K, N, E)
            exp_mask = exp_mask * (exp_rank < cap).astype(jnp.int32)
            exp_rank = jnp.sum(exp_mask * exp_rank, axis=-1)
            exp_weights = exp_mask.astype(x.dtype) * router_probs[None]
            rank_sc = jax.nn.one_hot(exp_rank, cap, dtype=x.dtype)
            cb_weight = jnp.einsum('kne,knc->nec', exp_weights, rank_sc)
            sec_mask = (cb_weight != 0).astype(x.dtype)
            xf = x.reshape(N, C)
            xb = jnp.einsum('nec,nd->ecd', sec_mask, xf)
            h = jax.nn.gelu(jnp.einsum('ecd,edf->ecf', xb, fc_w) + fc_b, approximate=False)
            out = jnp.einsum('ecf,efd->ecd', h, pj_w) + pj_b
            y = jnp.einsum('nec,ecd->nd', cb_weight, out)
            return y.reshape(B, T, C)
        x = x + _attention(_layer_norm(x, ln1_w, ln1_b), attn_qkv_w, attn_qkv_b, attn_proj_w, attn_proj_b)
        x = x + _moe(_layer_norm(x, ln2_w, ln2_b), w_g, exp_fc_w, exp_fc_b, exp_proj_w, exp_proj_b)
        return x
    h = _L0_tok_ref(x, L0_tok_w, L0_tok_b)
    h = h + _L0_attn_ref(_layernorm(h, axis=-1), L0_attn_W_in, L0_attn_conv_w, L0_attn_conv_b, L0_attn_dt_bias, L0_attn_A_log, L0_attn_D, L0_attn_norm_w, L0_attn_W_out)
    h = h + _L0_ffn_ref(_layernorm(h, axis=-1), L0_ffn_ln1_w, L0_ffn_ln1_b, L0_ffn_ln2_w, L0_ffn_ln2_b, L0_ffn_attn_qkv_w, L0_ffn_attn_qkv_b, L0_ffn_attn_proj_w, L0_ffn_attn_proj_b, L0_ffn_w_g, L0_ffn_exp_fc_w, L0_ffn_exp_fc_b, L0_ffn_exp_proj_w, L0_ffn_exp_proj_b)
    return h

_drawn_inputs = setup_inputs


def setup_inputs(seed=0):
    import zlib

    import numpy as np

    out = dict(_drawn_inputs(seed))
    spreads = {'L0_attn_conv_b': (0.0, 0.1),
     'L0_attn_D': (1.0, 0.2),
     'L0_attn_norm_w': (1.0, 0.2),
     'L0_ffn_ln1_w': (1.0, 0.6),
     'L0_ffn_ln1_b': (0.0, 0.8),
     'L0_ffn_ln2_w': (1.0, 0.6),
     'L0_ffn_ln2_b': (0.0, 0.585),
     'L0_ffn_attn_qkv_b': (0.0, 0.505),
     'L0_ffn_attn_proj_b': (0.0, 0.1),
     'L0_ffn_exp_fc_b': (0.0, 0.766),
     'L0_ffn_exp_proj_b': (0.0, 0.364)}
    factors = {'L0_ffn_attn_qkv_w': 5.379, 'L0_ffn_attn_proj_w': 3.09}
    for name, (base, spread) in spreads.items():
        noise = np.random.default_rng([zlib.crc32(name.encode()), seed]).standard_normal(out[name].shape)
        drawn = base * np.exp(spread * noise) if base else spread * noise
        out[name] = jnp.asarray(drawn.astype(out[name].dtype))
    for name, factor in factors.items():
        out[name] = (out[name] * factor).astype(out[name].dtype)
    return out
```

```python
from contextlib import ExitStack

import concourse.bass as bass
from concourse import mybir

ALU = mybir.AluOpType
ACT = mybir.ActivationFunctionType
F32 = mybir.dt.float32
BF16 = mybir.dt.bfloat16
I32 = mybir.dt.int32
AX = mybir.AxisListType

IMAGES = 8
CHANNELS, SIDE, PATCH = 3, 96, 8
GRID = SIDE // PATCH
TOKENS = GRID * GRID
T = TOKENS // 2
TILES = 2 * IMAGES
D = 192
HALF = D // 2
NTOK = IMAGES * TOKENS
D_INNER = 2 * D
HEADS, HEAD = 6, 64
STATE = 64
NCH = (D_INNER + 2 * STATE) // 128
TAPS = 4
D_PROJ = 2 * D_INNER + 2 * STATE + HEADS
AHEADS, AHEAD = 12, 16
PAD = 32
GROUPS = AHEADS // 4
EXPERTS = 8
CAP = 360
CHUNK = CAP // 3
FF = 4 * D
FT = FF // 128
ROW = D + EXPERTS + 1
GATE0, TOKCOL = D, D + EXPERTS
SLOTS = EXPERTS * CAP
OUT_OF_RANGE = 8192.0
EPS = 1e-5
QMAX = 127.0
MAGIC = 12582912.0
assert CAP == int(2 * 1.25 * NTOK // EXPERTS) and CAP % 2 == 0 and NTOK == TILES * T


def tower(nc, a, out):
    with ExitStack() as ctx:
        def sb(name, shape, dt=F32):
            return ctx.enter_context(nc.sbuf_tensor(name, shape, dt))

        def over(arena, at, shape, dt=F32):
            names = "abcdef"[:len(shape) - 1]
            size = 1
            for n in shape[1:]:
                size *= n
            end = at + (size if dt == F32 else size // 2)
            view = arena[0:shape[0], at:end]
            if dt != F32:
                view = view.bitcast(dt)
            return view.rearrange(f"p ({' '.join(names)}) -> p {' '.join(names)}", **dict(zip(names, shape[1:]))), end

        def sem(name):
            return ctx.enter_context(nc.semaphore(name))

        xslots = nc.dram_tensor("xslots", [SLOTS, ROW], F32, kind="Internal").ap()
        ysum = nc.dram_tensor("ysum", [NTOK + CAP, D], F32, kind="Internal").ap()

        ps = ctx.enter_context(nc.psum_tensor("ps", [128, 8, 512], F32))

        arena_p = sb("arena_p", [128, 2 * GROUPS * 12 * T])
        xin, n = over(arena_p, 0, [HALF, 2, NTOK])
        rnd = arena_p[0:HALF, n:2 * n]
        probs, n = over(arena_p, 0, [T, GROUPS, 4, 3, T])
        probsT, _ = over(arena_p, n, [T, GROUPS, 4, 3, T])
        hid, n = over(arena_p, 0, [128, FT, CAP])
        xsT, _ = over(arena_p, n, [HALF, 2, 2, CAP])
        arena_m = sb("arena_m", [128, 3 * 3 * HEADS * T])
        mix, n = over(arena_m, 0, [T, 2, 3, HEADS, T])
        decay, _ = over(arena_m, n, [T, 3, HEADS, T])
        dtT = arena_m[0:HEADS, 0:NTOK]
        fcw, _ = over(arena_m, 0, [HALF, 2, 2, FF])
        arena_x = sb("arena_x", [128, 2 * NCH * TOKENS + 2 * 2 * D_INNER])
        xc, n = over(arena_x, 0, [128, 2, NCH, TOKENS])
        dtx, _ = over(arena_x, n, [T, 2, 2, HEADS, HEAD])
        pjw, _ = over(arena_x, 0, [128, 2, FT, D])
        arena_q = sb("arena_q", [128, TILES * ROW])
        xqT, _ = over(arena_q, 0, [HALF, 2, NTOK], BF16)
        xd, _ = over(arena_q, 0, [T, TILES, ROW])
        ident = sb("ident", [128, 128])
        identb = sb("identb", [128, 128], BF16)
        r_le_t = sb("r_le_t", [T, T], BF16)
        r_gt_s = sb("r_gt_s", [T, T], BF16)
        r_lt_t = sb("r_lt_t", [T, T], BF16)
        onesb = sb("onesb", [T, T], BF16)
        onecol = sb("onecol", [128, 1])
        causal = sb("causal", [T, 3, T])
        maskneg = sb("maskneg", [T, 3, T], BF16)
        minus_half = sb("minus_half", [T, TILES])
        revw = sb("revw", [T, TILES, EXPERTS])
        restart = sb("restart", [T, EXPERTS * 2 * TILES])
        win = sb("win", [HALF, 2, D_PROJ])
        cw = sb("cw", [128, NCH, TAPS])
        cb = sb("cb", [128, NCH])
        dtb = sb("dtb", [T, HEADS])
        alog = sb("alog", [T, HEADS])
        dskip = sb("dskip", [128, 3])
        normw = sb("normw", [128, 3])
        wout = sb("wout", [128, 3, D])
        ln1w = sb("ln1w", [HALF, 2])
        ln1b = sb("ln1b", [HALF, 2])
        ln2w = sb("ln2w", [T, D])
        ln2b = sb("ln2b", [T, D])
        wqkv = sb("wqkv", [HALF, 2, 3 * D])
        wqk = sb("wqk", [HALF, 2, 2, AHEADS, PAD])
        qkb = sb("qkb", [128, 2, GROUPS])
        vb = sb("vb", [T, D])
        projw = sb("projw", [HALF, 2, D])
        projb = sb("projb", [T, D])
        wg = sb("wg", [HALF, 2, EXPERTS])
        tokb = sb("tokb", [T, D])
        fcb = sb("fcb", [128, EXPERTS * FT])
        pjb = sb("pjb", [CHUNK, EXPERTS * D])
        win_tok = sb("win_tok", [HALF, 2, D])
        rndw = sb("rndw", [HALF, 2 * D])
        wqT = sb("wqT", [HALF, 2, D], BF16)
        absmax = sb("absmax", [128, 2])
        absall = sb("absall", [128, 2])
        scales = sb("scales", [128, 2])
        inv = sb("inv", [128, 2])
        sxw = sb("sxw", [128, 1])
        h = sb("h", [T, TILES, D])
        hn = sb("hn", [T, TILES, D])
        u = hn
        stats_all = sb("stats_all", [T, TILES, 6])
        mv_all = sb("mv_all", [T, TILES, 2])
        veps_all = sb("veps_all", [T, TILES])
        rstd_all = sb("rstd_all", [T, TILES])
        hnT = sb("hnT", [HALF, 2, NTOK])
        stats = sb("stats", [T, 2, 6])
        spare = sb("spare", [1, 1])
        sparep = sb("sparep", [1, 1])
        mv = sb("mv", [T, 2, 2])
        veps = sb("veps", [T, 2])
        rstd = sb("rstd", [T, 2])
        dpre = sb("dpre", [T, TILES, HEADS])
        dabs = sb("dabs", [T, TILES, HEADS])
        dlost = sb("dlost", [T, TILES, HEADS])
        dpos = sb("dpos", [T, TILES, HEADS])
        donep = sb("donep", [T, TILES, HEADS])
        aexp = sb("aexp", [T, HEADS])
        dexp = sb("dexp", [T, TILES, HEADS])
        dlog = sb("dlog", [T, TILES, HEADS])
        dt = sb("dt", [T, TILES, HEADS])
        amat = sb("amat", [T, TILES, HEADS])
        arest = sb("arest", [T, TILES, HEADS])
        asplit = sb("asplit", [T, 3, TILES, HEADS], BF16)
        xpad = sb("xpad", [128, NCH, TAPS - 1 + TOKENS])
        conv = sb("conv", [128, NCH, TOKENS])
        cT = sb("cT", [STATE, TOKENS])
        sz = sb("sz", [128, 2, 3, TOKENS])
        amask = sb("amask", [T, 3, 2, HEADS, T], BF16)
        cbm = sb("cbm", [T, 3, T])
        yg = sb("yg", [128, 3, TOKENS])
        ysq = sb("ysq", [128, 3, TOKENS])
        msq = sb("msq", [T, 2])
        rms = sb("rms", [T, 2])
        xh = sb("xh", [T, 2, 2, D])
        xT = sb("xT", [HALF, 2, TOKENS])
        qs = sb("qs", [128, GROUPS, TOKENS])
        ks = sb("ks", [128, GROUPS, TOKENS])
        vaug = sb("vaug", [T, 2, AHEADS, AHEAD + 1])
        smax = sb("smax", [T, 4, 2])
        rden = sb("rden", [T, 2 * AHEADS])
        ao = sb("ao", [T, 2, D])
        aoT = sb("aoT", [HALF, 2, TOKENS])
        x1 = sb("x1", [T, 2, D])
        xh2 = sb("xh2", [T, 2, D])
        x2 = sb("x2", [T, 2, D])
        x2T = sb("x2T", [HALF, 2, TOKENS])
        base = sb("base", [T, 2, D])
        lg = sb("lg", [T, TILES, EXPERTS])
        top = sb("top", [T, 2, TILES])
        cand = sb("cand", [T, TILES, EXPERTS])
        cand2 = sb("cand2", [T, TILES, EXPERTS])
        lg2 = sb("lg2", [T, TILES, EXPERTS])
        pick = sb("pick", [T, 2, TILES])
        hotb = sb("hotb", [T, 2, TILES, EXPERTS], BF16)
        tot = sb("tot", [T, EXPERTS, 2 * TILES])
        incl = sb("incl", [T, EXPERTS, 2 * TILES])
        before = sb("before", [T, EXPERTS, 2 * TILES])
        rankm = sb("rankm", [T, 2 * TILES, EXPERTS])
        rank = sb("rank", [T, 2 * TILES])
        late = sb("late", [T, 2 * TILES])
        slotf = sb("slotf", [T, 2 * TILES])
        slot = sb("slot", [T, 2 * TILES], I32)
        pdiff = sb("pdiff", [T, TILES])
        pexp = sb("pexp", [T, TILES])
        psum1 = sb("psum1", [T, TILES])
        p1 = sb("p1", [T, TILES])
        p2 = sb("p2", [T, TILES])
        g1 = sb("g1", [T, TILES, EXPERTS])
        g2 = sb("g2", [T, TILES, EXPERTS])
        fill = sb("fill", [CHUNK, 3, ROW])
        xs = sb("xs", [CHUNK, 2, 3, ROW])
        ob = sb("ob", [CHUNK, 3, D])
        og = sb("og", [CHUNK, 2, 3, D])

        s_x = sem("s_x")
        s_w = sem("s_w")
        s_par = sem("s_par")
        s_part = sem("s_part")
        s_moeb = sem("s_moeb")
        s_fillx = sem("s_fillx")
        s_const = sem("s_const")
        s_pad = sem("s_pad")
        s_padb = sem("s_padb")
        s_prep = sem("s_prep")
        s_fcbT = sem("s_fcbT")
        s_fcb = sem("s_fcb")
        s_absmax = sem("s_absmax")
        s_absall = sem("s_absall")
        s_scale = sem("s_scale")
        s_rnd = sem("s_rnd")
        s_q = sem("s_q")
        s_qT = sem("s_qT")
        s_qTe = sem("s_qTe")
        s_qTd = sem("s_qTd")
        s_tok = sem("s_tok")
        s_h = sem("s_h")
        s_var = sem("s_var")
        s_rstd = sem("s_rstd")
        s_hn = sem("s_hn")
        s_hnT = sem("s_hnT")
        s_hnTe = sem("s_hnTe")
        s_a0 = sem("s_a0")
        s_dtT = sem("s_dtT")
        s_dtTe = sem("s_dtTe")
        s_dtp = sem("s_dtp")
        s_dabs = sem("s_dabs")
        s_dexp = sem("s_dexp")
        s_donep = sem("s_donep")
        s_dlog = sem("s_dlog")
        s_aexp = sem("s_aexp")
        s_as = sem("s_as")
        s_proj = sem("s_proj")
        s_xpad = sem("s_xpad")
        s_conv = sem("s_conv")
        s_xc = sem("s_xc")
        s_cT = sem("s_cT")
        s_z = sem("s_z")
        s_amask = sem("s_amask")
        s_seg = sem("s_seg")
        s_decay = sem("s_decay")
        s_xsT = sem("s_xsT")
        s_cb = sem("s_cb")
        s_cbm = sem("s_cbm")
        s_dtx = sem("s_dtx")
        s_mix = sem("s_mix")
        s_y = sem("s_y")
        s_yg = sem("s_yg")
        s_ysq = sem("s_ysq")
        s_wo = sem("s_wo")
        s_msq = sem("s_msq")
        s_rms = sem("s_rms")
        s_h1 = sem("s_h1")
        s_conv_step = sem("s_conv_step")
        s_y_step = sem("s_y_step")
        s_var1 = sem("s_var1")
        s_rstd1 = sem("s_rstd1")
        s_xh = sem("s_xh")
        s_xhT = sem("s_xhT")
        s_xT = sem("s_xT")
        s_qk = sem("s_qk")
        s_v = sem("s_v")
        s_qkv = sem("s_qkv")
        s_s = sem("s_s")
        s_sub = sem("s_sub")
        s_exp = sem("s_exp")
        s_pT = sem("s_pT")
        s_pTe = sem("s_pTe")
        s_pv = sem("s_pv")
        s_ao = sem("s_ao")
        s_aoT = sem("s_aoT")
        s_aoTe = sem("s_aoTe")
        s_pr = sem("s_pr")
        s_x1 = sem("s_x1")
        s_base = sem("s_base")
        s_based = sem("s_based")
        s_var2 = sem("s_var2")
        s_rstd2 = sem("s_rstd2")
        s_x2 = sem("s_x2")
        s_xd = sem("s_xd")
        s_x2T = sem("s_x2T")
        s_x2Te = sem("s_x2Te")
        s_lgp = sem("s_lgp")
        s_lg = sem("s_lg")
        s_ln_step = sem("s_ln_step")
        s_max_step = sem("s_max_step")
        s_x1_step = sem("s_x1_step")
        s_ao_step = sem("s_ao_step")
        s_hot = sem("s_hot")
        s_pre = sem("s_pre")
        s_slot = sem("s_slot")
        s_pd = sem("s_pd")
        s_pe = sem("s_pe")
        s_gate = sem("s_gate")
        s_r_step = sem("s_r_step")
        s_scat = sem("s_scat")
        s_et = sem("s_et")
        s_ete = sem("s_ete")
        s_fc = sem("s_fc")
        s_gelu = sem("s_gelu")
        s_pj = sem("s_pj")
        s_ob = sem("s_ob")
        s_og = sem("s_og")
        s_add = sem("s_add")
        s_out = sem("s_out")
        s_rmsp = sem("s_rmsp")
        s_ln2p = sem("s_ln2p")
        s_lnp = sem("s_lnp")
        s_ap = sem("s_ap")
        s_tokcol = sem("s_tokcol")
        s_relay = sem("s_relay")
        s_ew = [sem("s_ew0"), sem("s_ew1")]
        s_ex = [sem("s_ex0"), sem("s_ex1")]

        def bc(ap, n):
            return ap.unsqueeze(len(ap.shape)).to_broadcast(list(ap.shape) + [n])

        def bc_at(ap, at, n):
            v = ap.unsqueeze(at)
            s = list(v.shape)
            s[at] = n
            return v.to_broadcast(s)

        def imgs(t, i):
            return t[:, bass.ds(i * 2, 2), :]

        def tile(t, i, j):
            return t[:, bass.ds(i * 2 + j, 1), :].rearrange("t o d -> t (o d)")

        def run_slots(eng, slot):
            slot(0, 0, True, False)
            with eng.Fori(1, IMAGES - 2, 2) as i:
                slot(i, 1, False, False)
                slot(i + 1, 0, False, False)
            slot(7, 1, False, True)

        class Chain:

            def __init__(self, eng, s, i, per):
                self.eng, self.s, self.i, self.per, self.n = eng, s, i, per, 0

            def __call__(self, ins):
                self.n += 1
                ins.then_inc(self.s, 1)
                self.eng.wait_ge(self.s, self.i * self.per + self.n)

            def close(self):
                assert self.n == self.per, (self.n, self.per)

        block = ctx.enter_context(nc.Block())
        NPAR, NPART = 6, 11

        @block.sync
        def _(sp):
            def load(dst, src, s):
                sp.dma_start(dst, src).then_inc(s, 16)

            for c in range(2):
                load(xin[:, c, 0:NTOK // 2], a["patches"][c * HALF:(c + 1) * HALF, 0:NTOK // 2], s_x)
            load(win[:], a["L0_attn_W_in"].rearrange("(c p) n -> p c n", p=HALF), s_par)
            load(cw[:], a["L0_attn_conv_w"].rearrange("(c p) k -> p c k", p=128), s_par)
            load(cb[:], a["conv_b"], s_par)
            load(dskip[:], a["d_skip"], s_par)
            load(normw[:], a["norm_w"], s_par)
            load(wout[:], a["L0_attn_W_out"].rearrange("(c p) n -> p c n", p=128), s_par)
            load(wqkv[:], a["L0_ffn_attn_qkv_w"].rearrange("(c p) n -> p c n", p=HALF), s_part)
            sp.wait_ge(s_const, 1)
            load(ysum[NTOK:NTOK + CAP, :].rearrange("(c p) d -> p c d", p=CHUNK), fill[:, :, 0:D], s_based)
            sp.wait_ge(s_padb, 1)
            for g in range(4):
                load(qkb[PAD * g:PAD * g + AHEAD, :, :], a["qk_b"][g], s_part)
            load(ln1w[:], a["ln1_w"], s_part)
            load(ln1b[:], a["ln1_b"], s_part)
            load(fcb[:], a["fc_b"], s_part)
            load(projw[:], a["L0_ffn_attn_proj_w"].rearrange("(c p) n -> p c n", p=HALF), s_part)
            load(wg[:], a["L0_ffn_w_g"].rearrange("(c p) n -> p c n", p=HALF), s_part)
            load(vb[:], a["L0_ffn_attn_qkv_b"][2 * D:3 * D].rearrange("(o d) -> o d", o=1).to_broadcast([T, D]), s_part)
            load(pjb[:], a["L0_ffn_exp_proj_b"].rearrange("e o d -> o (e d)").to_broadcast([CHUNK, EXPERTS * D]), s_moeb)

            def load_weights(e, p):
                load(fcw[:, p, :, :], a["L0_ffn_exp_fc_w"][e].rearrange("(c p) f -> p c f", p=HALF), s_ew[p])
                load(pjw[:, p, :, :], a["L0_ffn_exp_proj_w"][e].rearrange("(f p) d -> p f d", p=128), s_ew[p])

            with sp.Fori(0, IMAGES - 1, 2) as i:
                for p in range(2):
                    sp.wait_ge(s_xc, i + p + 1)
                    load(cT[:, :], xc[STATE:128, p, NCH - 1, :], s_cT)

            sp.wait_ge(s_wo, IMAGES)
            load_weights(0, 0)
            load_weights(1, 1)

            with sp.Fori(0, IMAGES - 1, 2) as i:
                for p in range(2):
                    sp.wait_ge(s_base, i + p + 1)
                    load(ysum[bass.ds((i + p) * TOKENS, TOKENS), :].rearrange("(j t) d -> t j d", t=T), base[:], s_based)

            def load_rows(e, p):
                load(xs[:, p, :, :], xslots[bass.ds(e * CAP, CAP), :].rearrange("(c p) n -> p c n", p=CHUNK), s_ex[p])

            sp.wait_ge(s_scat, 16 * 2 * TILES)
            load_rows(0, 0)
            load_rows(1, 1)
            with sp.Fori(0, EXPERTS - 3, 2) as e:
                for p in range(2):
                    sp.wait_ge(s_pj, e + p + 1)
                    fw = a["L0_ffn_exp_fc_w"][bass.ds(e + (p + 2), 1)].rearrange("o (c p) f -> p (o c) f", p=HALF)
                    pw = a["L0_ffn_exp_proj_w"][bass.ds(e + (p + 2), 1)].rearrange("o (f p) d -> p (o f) d", p=128)
                    load(fcw[:, p, :, :], fw, s_ew[p])
                    load(pjw[:, p, :, :], pw, s_ew[p])
                    sp.wait_ge(s_add, (e + p + 1) * 48)
                    load_rows(e + (p + 2), p)
            sp.wait_ge(s_add, EXPERTS * 48)
            load(out.rearrange("b t d -> (b t) d"), ysum[0:NTOK, :], s_out)
            sp.wait_ge(s_out, 16)

        @block.scalar
        def _(act):
            def load(dst, src, s):
                act.dma_start(dst, src).then_inc(s, 16)

            act_f = nc.scalar.activation
            for c in range(2):
                load(xin[:, c, NTOK // 2:], a["patches"][c * HALF:(c + 1) * HALF, NTOK // 2:], s_x)
            load(win_tok[:], a["patch_w"].rearrange("(c p) d -> p c d", p=HALF), s_w)
            for dst, name in ((tokb, "L0_tok_b"), (dtb, "L0_attn_dt_bias"), (alog, "L0_attn_A_log"),
                              (ln2w, "L0_ffn_ln2_w"), (ln2b, "L0_ffn_ln2_b"), (projb, "L0_ffn_attn_proj_b")):
                load(dst[:], a[name].rearrange("(o d) -> o d", o=1).to_broadcast(list(dst.shape)), s_w)
            act.wait_ge(s_w, 16 * 7)
            act_f(aexp[:], alog[:], ACT.Exp).then_inc(s_aexp, 1)

            act.wait_ge(s_rnd, 1)
            act_f(wqT[:].rearrange("p c k -> p (c k)"), rndw[:], ACT.Copy, bias=-MAGIC)
            act_f(xqT[:].rearrange("p c t -> p (c t)"), rnd, ACT.Copy, bias=-MAGIC).then_inc(s_q, 1)

            for b in range(IMAGES):
                act.wait_ge(s_hnT, b + 1)
                act_f(hnT[:, :, b * TOKENS:(b + 1) * TOKENS],
                      ps[0:HALF, b % 2, 0:2 * TOKENS].rearrange("k (c t) -> k c t", c=2), ACT.Copy).then_inc(s_hnTe, 1)
            act.wait_ge(s_dtT, 1)
            act_f(dtT[:].rearrange("h (n t) -> h n t", n=3), ps[0:HEADS, 2:5, 0:NTOK // 3], ACT.Copy).then_inc(s_dtTe, 1)
            act.wait_ge(s_dabs, 1)
            act_f(dexp[:], dabs[:], ACT.Exp, scale=-1.0).then_inc(s_dexp, 1)
            act.wait_ge(s_donep, 1)
            act_f(dlog[:], donep[:], ACT.Ln).then_inc(s_dlog, 1)

            def square(m):
                act.wait_ge(s_yg, m + 1)
                act_f(ysq[:], yg[:], ACT.Square).then_inc(s_ysq, 1)

            def ssm_slot(i, p, first, last):
                act.wait_ge(s_proj, i * 3 + 2)
                act.wait_ge(s_conv, i)
                act_f(xpad[:, 0:3, TAPS - 1:], ps[:, 1, 0:3 * TOKENS].rearrange("k (c t) -> k c t", c=3), ACT.Copy)
                act_f(xpad[:, 3, TAPS - 1:], ps[:, 2, 0:TOKENS], ACT.Copy).then_inc(s_xpad, 1)
                act.wait_ge(s_seg, i + 1)
                act.wait_ge(s_mix, i)
                act_f(decay[:].rearrange("s k h t -> s k (h t)"), ps[0:T, 5:8, 0:HEADS * T], ACT.Exp).then_inc(s_decay, 1)
                if not first:
                    square(i - 1)
                act.wait_ge(s_proj, i * 3 + 3)
                act_f(sz[:, p, :, :].rearrange("k c t -> k (c t)"), ps[:, 0, 0:3 * TOKENS], ACT.Silu).then_inc(s_z, 1)
                act.wait_ge(s_conv, i + 1)
                act_f(xc[:, p, :, :], conv[:], ACT.Silu).then_inc(s_xc, 1)

            run_slots(act, ssm_slot)
            square(IMAGES - 1)

            act.wait_ge(s_part, 16 * NPART)

            def att_ao(m):
                act.wait_ge(s_aoT, m + 1)
                act_f(aoT[:], ps[0:HALF, 4, 0:2 * TOKENS].rearrange("k (c t) -> k c t", c=2), ACT.Copy).then_inc(s_aoTe, 1)

            def att_x2(m):
                act.wait_ge(s_x2T, m + 1)
                act_f(x2T[:], ps[0:HALF, 4, 0:2 * TOKENS].rearrange("k (c t) -> k c t", c=2), ACT.Copy).then_inc(s_x2Te, 1)

            def att_slot(i, p, first, last):
                act.wait_ge(s_xhT, i + 1)
                for c in range(2):
                    ins = act_f(xT[:, c, :], ps[0:HALF, 4, c * TOKENS:(c + 1) * TOKENS], ACT.Identity,
                                bias=ln1b[:, c:c + 1], scale=ln1w[:, c:c + 1])
                ins.then_inc(s_xT, 1)
                if not first:
                    att_ao(i - 1)
                for c in range(GROUPS):
                    act.wait_ge(s_sub, i * 3 + (c + 1))
                    act_f(probs[:, c], probs[:, c], ACT.Exp).then_inc(s_exp, 1)
                    act.wait_ge(s_pT, i * 3 + (c + 1))
                    act_f(probsT[:, c].rearrange("s (b g) k t -> s b (g k t)", b=2),
                          ps[0:T, 5:7, 0:6 * T], ACT.Copy).then_inc(s_pTe, 1)
                    if c == 0 and not first:
                        att_x2(i - 1)

            run_slots(act, att_slot)
            att_ao(IMAGES - 1)
            att_x2(IMAGES - 1)

            act.wait_ge(s_pd, 1)
            act_f(pexp[:], pdiff[:], ACT.Exp).then_inc(s_pe, 1)

            def exp_slot(e, p, first, last):
                for f in range(FT):
                    if f == 0:
                        act.wait_ge(s_pj, e)
                    act.wait_ge(s_fc, e * FT + (f + 1))
                    act_f(hid[:, f, :], ps[:, 2 + (2 * p + f) % 4, 0:CAP], ACT.Gelu,
                          bias=fcb[:, bass.ds(e * FT + f, 1)]).then_inc(s_gelu, 1)

            run_slots(act, exp_slot)

        @block.gpsimd
        def _(pool):
            g = nc.gpsimd
            g.memset(ident[:], 0.0)
            g.memset(identb[:], 0.0)
            g.memset(r_le_t[:], 1.0)
            g.memset(r_gt_s[:], 1.0)
            g.memset(r_lt_t[:], 1.0)
            g.memset(causal[:], 1.0)
            g.memset(maskneg[:], 0.0)
            g.memset(restart[:], 1.0)
            g.memset(fill[:], 0.0)
            g.memset(onesb[:], 1.0)
            g.memset(onecol[:], 1.0)
            g.memset(minus_half[:], -0.5)
            g.memset(xpad[:, :, 0:TAPS - 1], 0.0)
            g.memset(vaug[:], 1.0)
            g.memset(wqk[:], 0.0)
            g.memset(qkb[:], 0.0).then_inc(s_padb, 1)
            pool.wait_ge(s_padb, 1)
            for m in (ident, identb):
                g.affine_select(out=m[:], in_=m[:], compare_op=ALU.not_equal, fill=1.0, base=0,
                                pattern=[[-1, 128]], channel_multiplier=1)
            g.affine_select(out=r_le_t[:], in_=r_le_t[:], compare_op=ALU.is_ge, fill=0.0, base=0,
                            pattern=[[1, T]], channel_multiplier=-1)
            g.affine_select(out=r_gt_s[:], in_=r_gt_s[:], compare_op=ALU.is_gt, fill=0.0, base=0,
                            pattern=[[-1, T]], channel_multiplier=1)
            g.affine_select(out=r_lt_t[:], in_=r_lt_t[:], compare_op=ALU.is_gt, fill=0.0, base=0,
                            pattern=[[1, T]], channel_multiplier=-1)
            g.affine_select(out=causal[:, 0:3:2, :], in_=causal[:, 0:3:2, :], compare_op=ALU.is_ge, fill=0.0,
                            base=0, pattern=[[0, 2], [1, T]], channel_multiplier=-1)
            g.affine_select(out=maskneg[:, 0:3:2, :], in_=maskneg[:, 0:3:2, :], compare_op=ALU.is_ge, fill=-1e30,
                            base=0, pattern=[[0, 2], [-1, T]], channel_multiplier=1)
            g.affine_select(out=restart[:], in_=restart[:], compare_op=ALU.not_equal, fill=0.0,
                            base=0, pattern=[[0, EXPERTS], [1, 2 * TILES]], channel_multiplier=0)
            for e in range(EXPERTS):
                g.memset(revw[:, :, e], float(EXPERTS - e))
            g.iota(fill[:, :, TOKCOL].bitcast(I32), pattern=[[CHUNK, 3]], base=NTOK, channel_multiplier=1
                   ).then_inc(s_const, 1)
            pool.wait_ge(s_const, 1)
            for e in range(EXPERTS):
                pool.dma_start(xslots[e * CAP:(e + 1) * CAP, :].rearrange("(c p) n -> p c n", p=CHUNK), fill[:]
                               ).then_inc(s_fillx, 16)
            pool.wait_ge(s_absmax, 2)
            g.partition_all_reduce(absall[0:HALF, :], absmax[0:HALF, :], HALF, bass.bass_isa.ReduceOp.absmax
                                   ).then_inc(s_absall, 1)
            pool.wait_ge(s_var, 1)
            g.tensor_tensor(rstd_all[:], veps_all[:], minus_half[:], ALU.pow).then_inc(s_rstd, 1)
            pool.wait_ge(s_par, 16 * NPAR)
            g.tensor_tensor(wout[:], wout[:], bc(normw[:], D), ALU.mult)
            pool.wait_ge(s_part, 16 * NPART)
            scale = float(AHEAD) ** -0.5
            for k in range(2):
                for c in range(2):
                    src = wqkv[:, c, k * D:(k + 1) * D].rearrange("p (h d) -> p h d", d=AHEAD)
                    g.tensor_scalar(wqk[:, c, k, :, 0:AHEAD], src, 1.0 if k else scale, None, ALU.mult)
            g.tensor_scalar(qkb[:, 0, :], qkb[:, 0, :], scale, None, ALU.mult).then_inc(s_prep, 1)

            def pow_rms(m):
                pool.wait_ge(s_msq, m + 1)
                g.tensor_tensor(rms[:], msq[:], minus_half[:, 0:2], ALU.pow).then_inc(s_rms, 1)

            pool.wait_ge(s_as, 1)

            def ssm_slot(i, p, first, last):
                pool.wait_ge(s_seg, i)
                for k in range(3):
                    ins = g.tensor_tensor(amask[:, k], bc_at(bc_at(r_le_t[:], 1, HEADS), 1, 2),
                                          bc(asplit[:, k, bass.ds(i * 2, 2), :], T), ALU.mult)
                ins.then_inc(s_amask, 1)
                if not first:
                    pow_rms(i - 1)

            run_slots(pool, ssm_slot)
            pow_rms(IMAGES - 1)

            def rstd_ln(i):
                for n in range(2):
                    pool.wait_ge(s_var1, i * 2 + (n + 1))
                    g.tensor_tensor(rstd[:], veps[:], minus_half[:, 0:2], ALU.pow).then_inc(s_rstd1, 1)

            def after_attention(m):
                pool.wait_ge(s_x1, m + 1)
                pool.wait_ge(s_based, (m + 1) * 16)
                g.tensor_tensor(base[:], x1[:], imgs(h, m), ALU.add).then_inc(s_base, 1)
                pool.wait_ge(s_var2, m + 1)
                g.tensor_tensor(rstd[:], veps[:], minus_half[:, 0:2], ALU.pow).then_inc(s_rstd2, 1)
                pool.wait_ge(s_x2, m + 1)
                g.tensor_copy(xd[:, bass.ds(m * 2, 2), 0:D], x2[:]).then_inc(s_xd, 1)

            rstd_ln(0)
            g.iota(xd[:, :, TOKCOL].bitcast(I32), pattern=[[T, TILES]], base=0, channel_multiplier=1).then_inc(s_tokcol, 1)

            def att_slot(i, p, first, last):
                if not first:
                    after_attention(i - 1)
                if not last:
                    rstd_ln(i + 1)

            run_slots(pool, att_slot)
            after_attention(IMAGES - 1)

            pool.wait_ge(s_gate, 1)
            pool.wait_ge(s_slot, 1)
            pool.wait_ge(s_xd, IMAGES)
            pool.wait_ge(s_tokcol, 1)
            pool.wait_ge(s_fillx, 16 * EXPERTS)
            for n in range(2 * TILES):
                g.indirect_dma_start(out=xslots[:, :],
                                     out_offset=bass.IndirectOffsetOnAxis(ap=slot[:, n:n + 1], axis=0),
                                     in_=xd[:, n % TILES, :], in_offset=None,
                                     bounds_check=SLOTS - 1, oob_is_err=False).then_inc(s_scat, 16)

            pool.wait_ge(s_based, 16 * (IMAGES + 1))

            def exp_slot(e, p, first, last):
                pool.wait_ge(s_relay, e)
                pool.wait_ge(s_og, e + 1)
                pool.wait_ge(s_add, e * 48)
                g.tensor_tensor(sparep[:], onecol[0:1, :], onecol[0:1, :], ALU.mult).then_inc(s_relay, 1)
                for c in range(3):
                    g.indirect_dma_start(out=ysum[:, :],
                                         out_offset=bass.IndirectOffsetOnAxis(
                                             ap=xs[:, p, c, TOKCOL:TOKCOL + 1].bitcast(I32), axis=0),
                                         in_=og[:, p, c, :], in_offset=None, compute_op=ALU.add).then_inc(s_add, 16)

            run_slots(pool, exp_slot)

        @block.vector
        def _(dve):
            v = nc.vector

            dve.wait_ge(s_x, 16 * 4)
            v.tensor_reduce(absmax[0:HALF, 0:1], xin.rearrange("x c t -> x (c t)"), AX.X, ALU.max,
                            apply_absolute_value=True).then_inc(s_absmax, 1)
            dve.wait_ge(s_w, 16 * 7)
            v.tensor_reduce(absmax[0:HALF, 1:2], win_tok[:].rearrange("p j k -> p (j k)"), AX.X, ALU.max,
                            apply_absolute_value=True).then_inc(s_absmax, 1)
            dve.wait_ge(s_absall, 1)
            link = Chain(dve, s_a0, 0, 99)
            link(v.tensor_scalar(scales[0:HALF, :], absall[0:HALF, :], 1e-8, 1.0 / QMAX, ALU.max, ALU.mult))
            v.tensor_tensor(sxw[0:HALF, :], scales[0:HALF, 0:1], scales[0:HALF, 1:2], ALU.mult)
            link(v.reciprocal(inv[0:HALF, :], scales[0:HALF, :]))
            link(v.tensor_scalar(rnd, xin.rearrange("x c t -> x (c t)"), inv[0:HALF, 0:1], MAGIC,
                                 ALU.mult, ALU.add))
            v.tensor_scalar(rnd, rnd, MAGIC - QMAX, MAGIC + QMAX, ALU.max, ALU.min)
            link(v.tensor_scalar(rndw[:], win_tok[:].rearrange("p j k -> p (j k)"), inv[0:HALF, 1:2], MAGIC,
                                 ALU.mult, ALU.add))
            v.tensor_scalar(rndw[:], rndw[:], MAGIC - QMAX, MAGIC + QMAX, ALU.max, ALU.min).then_inc(s_rnd, 1)
            for b in range(IMAGES):
                dve.wait_ge(s_tok, b + 1)
                v.scalar_tensor_tensor(out=h[:, 2 * b:2 * b + 2, :],
                                       in0=ps[0:T, 5 + b % 2, 0:2 * D].rearrange("t (j d) -> t j d", j=2),
                                       scalar=sxw[0:T, :], in1=bc_at(tokb[:], 1, 2), op0=ALU.mult, op1=ALU.add
                                       ).then_inc(s_h, 1)
                if b:
                    for j in range(2 * b - 2, 2 * b):
                        dve.wait_ge(s_h, b)
                        v.bn_stats(stats_all[:, j, :], h[:, j, :])
            dve.wait_ge(s_h, IMAGES)
            v.bn_stats(stats_all[:, TILES - 2, :], h[:, TILES - 2, :])
            link(v.bn_stats(stats_all[:, TILES - 1, :], h[:, TILES - 1, :]))
            for j in range(TILES):
                ins = v.bn_aggr(mv_all[:, j, :], stats_all[:, j, :])
            link(ins)
            v.tensor_scalar_add(veps_all[:], mv_all[:, :, 1], EPS).then_inc(s_var, 1)
            dve.wait_ge(s_rstd, 1)
            for j in range(TILES):
                v.tensor_scalar(hn[:, j, :], h[:, j, :], mv_all[:, j, 0:1], rstd_all[:, j:j + 1],
                                ALU.subtract, ALU.mult).then_inc(s_hn, 1)

            dve.wait_ge(s_dtp, 1)
            link(v.tensor_tensor(dpre[:], ps[0:T, 5, 0:TILES * HEADS].rearrange("t (j h) -> t j h", h=HEADS),
                                 bc_at(dtb[:], 1, TILES), ALU.add))
            link(v.tensor_scalar(dpos[:], dpre[:], 0.0, None, ALU.max))
            v.scalar_tensor_tensor(out=dabs[:], in0=dpos[:], scalar=2.0, in1=dpre[:], op0=ALU.mult, op1=ALU.subtract
                                   ).then_inc(s_dabs, 1)
            dve.wait_ge(s_dexp, 1)
            v.tensor_scalar_add(donep[:], dexp[:], 1.0).then_inc(s_donep, 1)
            dve.wait_ge(s_donep, 1)
            link(v.scalar_tensor_tensor(out=dlost[:], in0=donep[:], scalar=-1.0, in1=dexp[:],
                                        op0=ALU.add, op1=ALU.subtract))
            link(v.tensor_tensor(dpos[:], dpos[:], dlost[:], ALU.subtract))
            dve.wait_ge(s_dlog, 1)
            link(v.tensor_tensor(dt[:], dpos[:], dlog[:], ALU.add))
            dve.wait_ge(s_aexp, 1)
            link(v.scalar_tensor_tensor(out=amat[:], in0=dt[:], scalar=-1.0, in1=bc_at(aexp[:], 1, TILES),
                                        op0=ALU.mult, op1=ALU.mult))
            link(v.tensor_copy(asplit[:, 0], amat[:]))
            link(v.tensor_tensor(arest[:], amat[:], asplit[:, 0], ALU.subtract))
            link(v.tensor_copy(asplit[:, 1], arest[:]))
            link(v.tensor_tensor(arest[:], arest[:], asplit[:, 1], ALU.subtract))
            v.tensor_copy(asplit[:, 2], arest[:]).then_inc(s_as, 1)
            dve.wait_ge(s_par, 16 * NPAR)
            dve.wait_ge(s_const, 1)

            def gate_y(m, q):
                step = Chain(dve, s_y_step, m, 1)
                dve.wait_ge(s_y, m + 1)
                for c in range(3):
                    ins = v.scalar_tensor_tensor(out=yg[:, c, :], in0=xc[:, q, c, :], scalar=dskip[:, c:c + 1],
                                                 in1=ps[:, 3, c * TOKENS:(c + 1) * TOKENS], op0=ALU.mult, op1=ALU.add)
                step(ins)
                v.tensor_tensor(yg[:], yg[:], sz[:, q], ALU.mult).then_inc(s_yg, 1)

            def residual(m):
                dve.wait_ge(s_wo, m + 1)
                v.tensor_scalar(msq[:], ps[0:T, 4, 400:402], 1.0 / D_INNER, EPS, ALU.mult, ALU.add).then_inc(s_msq, 1)
                dve.wait_ge(s_rms, m + 1)
                for j in range(2):
                    ins = v.scalar_tensor_tensor(out=tile(h, m, j), in0=ps[0:T, 4, j * D:(j + 1) * D],
                                                 scalar=rms[:, j:j + 1], in1=tile(h, m, j), op0=ALU.mult, op1=ALU.add)
                ins.then_inc(s_h1, 1)

            def ssm_slot(i, p, first, last):
                step = Chain(dve, s_conv_step, i, TAPS - 1)
                dve.wait_ge(s_xpad, i + 1)
                dve.wait_ge(s_xc, i)
                for k in range(TAPS):
                    for c in range(NCH):
                        if k == 0:
                            ins = v.tensor_scalar(conv[:, c, :], xpad[:, c, 0:TOKENS], cw[:, c, 0:1], cb[:, c:c + 1],
                                                  ALU.mult, ALU.add)
                        else:
                            ins = v.scalar_tensor_tensor(out=conv[:, c, :], in0=xpad[:, c, k:k + TOKENS],
                                                         scalar=cw[:, c, k:k + 1], in1=conv[:, c, :],
                                                         op0=ALU.mult, op1=ALU.add)
                    if k < TAPS - 1:
                        step(ins)
                step.close()
                ins.then_inc(s_conv, 1)
                if not first:
                    gate_y(i - 1, 1 - p)
                    residual(i - 1)
                dve.wait_ge(s_xsT, i + 1)
                for j in range(2):
                    ins = v.tensor_tensor(dtx[:, p, j], ps[0:T, j, 0:D_INNER].rearrange("t (h d) -> t h d", h=HEADS),
                                          bc(tile(dt, i, j), HEAD), ALU.mult)
                ins.then_inc(s_dtx, 1)
                dve.wait_ge(s_cb, i + 1)
                v.tensor_tensor(cbm[:], ps[0:T, 2, TOKENS:TOKENS + 3 * T].rearrange("s (k t) -> s k t", k=3),
                                causal[:], ALU.mult).then_inc(s_cbm, 1)
                dve.wait_ge(s_cbm, i + 1)
                dve.wait_ge(s_decay, i + 1)
                v.tensor_tensor(mix[:, p], decay[:], bc_at(cbm[:], 2, HEADS), ALU.mult).then_inc(s_mix, 1)

            run_slots(dve, ssm_slot)
            gate_y(IMAGES - 1, 1)
            residual(IMAGES - 1)

            def normalise(step, src, dst, s_var_, s_rstd_, count):
                v.memset(spare[:], 0.0)
                v.bn_stats(stats[:, 0, :], src(0))
                step(v.bn_stats(stats[:, 1, :], src(1)))
                v.memset(spare[:], 0.0)
                v.bn_aggr(mv[:, 0, :], stats[:, 0, :])
                step(v.bn_aggr(mv[:, 1, :], stats[:, 1, :]))
                v.tensor_scalar_add(veps[:], mv[:, :, 1], EPS).then_inc(s_var_, 1)
                dve.wait_ge(s_rstd_, count)
                for j in range(2):
                    ins = v.tensor_scalar(dst(j), src(j), mv[:, j, 0:1], rstd[:, j:j + 1], ALU.subtract, ALU.mult)
                return ins

            def enter(i, p):
                step = Chain(dve, s_ln_step, i, 5)
                step(normalise(step, lambda j: tile(h, i, j), lambda j: tile(u, i, j), s_var1, s_rstd1, i * 2 + 1))
                normalise(step, lambda j: tile(u, i, j), lambda j: xh[:, p, j, :], s_var1, s_rstd1, i * 2 + 2
                          ).then_inc(s_xh, 1)
                step.close()

            def after_attention(m):
                step = Chain(dve, s_x1_step, m, 5)
                dve.wait_ge(s_pr, m + 1)
                step(v.tensor_tensor(x1[:], ps[0:T, 4, 0:2 * D].rearrange("t (j d) -> t j d", j=2),
                                     bc_at(projb[:], 1, 2), ALU.add))
                v.tensor_tensor(x1[:], x1[:], imgs(u, m), ALU.add).then_inc(s_x1, 1)
                dve.wait_ge(s_x1, m + 1)
                step(normalise(step, lambda j: x1[:, j, :], lambda j: xh2[:, j, :], s_var2, s_rstd2, m + 1))
                step(v.tensor_tensor(xh2[:], xh2[:], bc_at(ln2w[:], 1, 2), ALU.mult))
                v.tensor_tensor(x2[:], xh2[:], bc_at(ln2b[:], 1, 2), ALU.add).then_inc(s_x2, 1)
                step.close()

            def logits(m):
                dve.wait_ge(s_lgp, m + 1)
                v.tensor_copy(imgs(lg, m), ps[0:T, 4, 0:2 * EXPERTS].rearrange("t (j e) -> t j e", j=2)).then_inc(s_lg, 1)

            def att_slot(i, p, first, last):
                dve.wait_ge(s_qk, i + 1)
                for k, dst in ((0, qs), (1, ks)):
                    v.tensor_tensor(dst[:], ps[:, 5 + k, 0:GROUPS * TOKENS].rearrange("p (c t) -> p c t", c=GROUPS),
                                    bc(qkb[:, k, :], TOKENS), ALU.add)
                dve.wait_ge(s_v, i + 1)
                v.tensor_tensor(vaug[:, :, :, 0:AHEAD],
                                ps[0:T, 7, 0:2 * D].rearrange("t (j h d) -> t j h d", j=2, d=AHEAD),
                                bc_at(vb[:], 1, 2).rearrange("t j (h d) -> t j h d", d=AHEAD), ALU.add).then_inc(s_qkv, 1)
                step = Chain(dve, s_max_step, i, GROUPS)
                for c in range(GROUPS):
                    dve.wait_ge(s_s, i * 3 + (c + 1))
                    v.tensor_reduce(smax[:, :, 0], ps[0:T, 0:4, 0:T], AX.X, ALU.max)
                    step(v.tensor_reduce(smax[:, :, 1], ps[0:T, 0:4, T:3 * T], AX.X, ALU.max))
                    v.tensor_tensor(probs[:, c, :, 0, :], ps[0:T, 0:4, 0:T], bc(smax[:, :, 0], T), ALU.subtract)
                    v.tensor_tensor(probs[:, c, :, 1:3, :].rearrange("t g k s -> t g (k s)"), ps[0:T, 0:4, T:3 * T],
                                    bc(smax[:, :, 1], 2 * T), ALU.subtract).then_inc(s_sub, 1)
                    if c == 0 and not first:
                        after_attention(i - 1)
                step.close()
                if not first:
                    logits(i - 1)
                if not last:
                    enter(i + 1, 1 - p)
                dve.wait_ge(s_pv, i + 1)
                step = Chain(dve, s_ao_step, i, 1)
                pv = ps[0:T, 7, 0:2 * AHEADS * (AHEAD + 1)].rearrange("t (n e) -> t n e", e=AHEAD + 1)
                step(v.reciprocal(rden[:], pv[:, :, AHEAD]))
                v.tensor_tensor(ao[:].rearrange("t j (h d) -> t (j h) d", d=AHEAD), pv[:, :, 0:AHEAD],
                                bc(rden[:], AHEAD), ALU.mult).then_inc(s_ao, 1)

            dve.wait_ge(s_prep, 1)
            dve.wait_ge(s_part, 16 * NPART)
            dve.wait_ge(s_h1, IMAGES)
            enter(0, 0)
            run_slots(dve, att_slot)
            after_attention(IMAGES - 1)
            logits(IMAGES - 1)

            link = Chain(dve, s_r_step, 0, 99)
            dve.wait_ge(s_lg, IMAGES)
            src = lg
            for k in range(2):
                link(v.tensor_reduce(top[:, k, :], src[:], AX.X, ALU.max))
                link(v.tensor_tensor(cand[:], src[:], bc(top[:, k, :], EXPERTS), ALU.is_equal))
                link(v.tensor_tensor(cand2[:], cand[:], revw[:], ALU.mult))
                link(v.tensor_reduce(pick[:, k, :], cand2[:], AX.X, ALU.max))
                link(v.tensor_tensor(hotb[:, k], revw[:], bc(pick[:, k, :], EXPERTS), ALU.is_equal))
                if k == 0:
                    link(v.scalar_tensor_tensor(out=lg2[:], in0=hotb[:, 0], scalar=-3e38, in1=lg[:],
                                                op0=ALU.mult, op1=ALU.add))
                    src = lg2
            v.tensor_tensor(pdiff[:], top[:, 1, :], top[:, 0, :], ALU.subtract).then_inc(s_pd, 1)
            dve.wait_ge(s_pre, 1)
            prev = ps[0:T, 0, 0:2 * TILES * EXPERTS].rearrange("t (n e) -> t e n", e=EXPERTS)
            totv = ps[0:T, 1, 0:2 * TILES * EXPERTS].rearrange("t (n e) -> t e n", e=EXPERTS)
            link(v.tensor_copy(tot[:], totv))
            link(v.tensor_tensor_scan(incl[:].rearrange("t e n -> t (e n)"), restart[:],
                                      tot[:].rearrange("t e n -> t (e n)"), 0.0, ALU.mult, ALU.add))
            link(v.tensor_tensor(before[:], incl[:], tot[:], ALU.subtract))
            link(v.tensor_tensor(before[:], before[:], prev, ALU.add))
            link(v.tensor_tensor(rankm[:], before[:].rearrange("t e n -> t n e"),
                                 hotb[:].rearrange("t k j e -> t (k j) e"), ALU.mult))
            link(v.tensor_reduce(rank[:], rankm[:], AX.X, ALU.add))
            v.tensor_scalar(late[:], rank[:], float(CAP), OUT_OF_RANGE, ALU.is_ge, ALU.mult)
            link(v.scalar_tensor_tensor(out=slotf[:], in0=pick[:].rearrange("t k j -> t (k j)"), scalar=-float(CAP),
                                        in1=rank[:], op0=ALU.mult, op1=ALU.add))
            link(v.scalar_tensor_tensor(out=slotf[:], in0=slotf[:], scalar=float(EXPERTS * CAP), in1=late[:],
                                        op0=ALU.add, op1=ALU.add))
            v.tensor_copy(slot[:], slotf[:]).then_inc(s_slot, 1)
            dve.wait_ge(s_pe, 1)
            link(v.tensor_scalar_add(psum1[:], pexp[:], 1.0))
            link(v.reciprocal(p1[:], psum1[:]))
            link(v.tensor_tensor(p2[:], p1[:], pexp[:], ALU.mult))
            v.tensor_tensor(g1[:], hotb[:, 0], bc(p1[:], EXPERTS), ALU.mult)
            link(v.tensor_tensor(g2[:], hotb[:, 1], bc(p2[:], EXPERTS), ALU.mult))
            v.tensor_tensor(xd[:, :, GATE0:GATE0 + EXPERTS], g1[:], g2[:], ALU.add).then_inc(s_gate, 1)

            def rows_out(e, p):
                dve.wait_ge(s_et, e + 1)
                for c in range(2):
                    ins = v.tensor_copy(xsT[:, p, c, :], ps[0:HALF, c, 0:CAP])
                ins.then_inc(s_ete, 1)

            rows_out(0, 0)
            dve.wait_ge(s_moeb, 16)

            def exp_slot(e, p, first, last):
                if not last:
                    rows_out(e + 1, 1 - p)
                dve.wait_ge(s_og, e)
                dve.wait_ge(s_pj, e + 1)
                bias = pjb[:, bass.ds(e * D, D)]
                v.tensor_tensor(ob[:, 0:2, :], ps[0:CHUNK, 6, 0:2 * D].rearrange("s (c d) -> s c d", c=2),
                                bc_at(bias, 1, 2), ALU.add)
                v.tensor_tensor(ob[:, 2, :], ps[0:CHUNK, 7, 0:D], bias, ALU.add).then_inc(s_ob, 1)
                dve.wait_ge(s_ob, e + 1)
                dve.wait_ge(s_relay, e)
                for c in range(3):
                    ins = v.tensor_scalar(og[:, p, c, :], ob[:, c, :], xs[:, p, c, bass.ds(e + GATE0, 1)], None, ALU.mult)
                ins.then_inc(s_og, 1)

            run_slots(dve, exp_slot)

        @block.tensor
        def _(pe):
            mm, tr = nc.tensor.matmul, nc.tensor.transpose
            pe.wait_ge(s_const, 1)

            pe.wait_ge(s_q, 1)
            for b in range(IMAGES):
                if b >= 2:
                    pe.wait_ge(s_h, b - 1)
                for j in range(2):
                    at = b * TOKENS + j * T
                    for c in range(2):
                        ins = mm(ps[0:T, 5 + b % 2, j * D:(j + 1) * D], xqT[:, c, at:at + T], wqT[:, c, :],
                                 start=c == 0, stop=c == 1)
                ins.then_inc(s_tok, 1)
            for b in range(IMAGES):
                pe.wait_ge(s_hn, 2 * b + 2)
                if b >= 2:
                    pe.wait_ge(s_hnTe, b - 1)
                for c in range(2):
                    for j in range(2):
                        at = c * TOKENS + j * T
                        ins = tr(ps[0:HALF, b % 2, at:at + T], hn[:, 2 * b + j, c * HALF:(c + 1) * HALF], ident[0:T, 0:T])
                ins.then_inc(s_hnT, 1)

            pe.wait_ge(s_par, 16 * NPAR)
            pe.wait_ge(s_hnTe, IMAGES)
            n3 = NTOK // 3
            for n in range(3):
                for c in range(2):
                    ins = mm(ps[0:HEADS, 2 + n, 0:n3], win[:, c, D_PROJ - HEADS:D_PROJ], hnT[:, c, n * n3:(n + 1) * n3],
                             start=c == 0, stop=c == 1)
            ins.then_inc(s_dtT, 1)
            pe.wait_ge(s_dtTe, 1)
            for j in range(TILES):
                ins = tr(ps[0:T, 5, j * HEADS:(j + 1) * HEADS], dtT[:, j * T:(j + 1) * T], ident[0:HEADS, 0:HEADS])
            ins.then_inc(s_dtp, 1)

            pe.wait_ge(s_as, 1)

            def scan_out(m, q):
                pe.wait_ge(s_mix, m + 1)
                for hd in range(HEADS):
                    r = slice(64 * (hd % 2), 64 * (hd % 2) + 64)
                    at = (hd // 2) * TOKENS
                    mm(ps[r, 3, at:at + TOKENS], dtx[:, q, 0, hd, :], mix[:, q, 0:2, hd, :], start=True, stop=False)
                    ins = mm(ps[r, 3, at + T:at + TOKENS], dtx[:, q, 1, hd, :], mix[:, q, 2, hd, :], start=False, stop=True)
                ins.then_inc(s_y, 1)
                pe.wait_ge(s_yg, m + 1)
                for j in range(2):
                    for c in range(3):
                        mm(ps[0:T, 4, j * D:(j + 1) * D], yg[:, c, j * T:(j + 1) * T], wout[:, c, :],
                           start=c == 0, stop=c == 2)
                pe.wait_ge(s_ysq, m + 1)
                for j in range(2):
                    for c in range(3):
                        ins = mm(ps[0:T, 4, 400 + j:401 + j], ysq[:, c, j * T:(j + 1) * T], onecol[:, :],
                                 start=c == 0, stop=c == 2)
                ins.then_inc(s_wo, 1)

            def ssm_slot(i, p, first, last):
                pe.wait_ge(s_dtx, i)
                pe.wait_ge(s_cbm, i)

                def project(bank, n, c0):
                    for c in range(n):
                        w = (c0 + c) * 128
                        for k in range(2):
                            ins = mm(ps[:, bank, c * TOKENS:(c + 1) * TOKENS], win[:, k, w:w + 128],
                                     hnT[:, k, bass.ds(i * TOKENS, TOKENS)], start=k == 0, stop=k == 1)
                    ins.then_inc(s_proj, 1)

                project(1, 3, 3)
                project(2, 1, 6)
                project(0, 3, 0)
                pe.wait_ge(s_amask, i + 1)
                pe.wait_ge(s_decay, i)
                for k in range(3):
                    mm(ps[0:T, 5, 0:HEADS * T], r_gt_s[:], amask[:, k, 0], start=k == 0, stop=k == 2)
                for k in range(3):
                    mm(ps[0:T, 7, 0:HEADS * T], r_gt_s[:], amask[:, k, 1], start=k == 0, stop=k == 2)
                for k in range(3):
                    mm(ps[0:T, 6, 0:HEADS * T], r_gt_s[:],
                       amask[:, k, 0, :, T - 1:T].to_broadcast([T, HEADS, T]), start=k == 0, stop=False)
                for k in range(3):
                    ins = mm(ps[0:T, 6, 0:HEADS * T], onesb[:], amask[:, k, 1], start=False, stop=k == 2)
                ins.then_inc(s_seg, 1)
                if not first:
                    scan_out(i - 1, 1 - p)
                pe.wait_ge(s_xc, i + 1)
                pe.wait_ge(s_z, i + 1)
                for j in range(2):
                    for c in range(3):
                        ins = tr(ps[0:T, j, c * 128:(c + 1) * 128], xc[:, p, c, j * T:(j + 1) * T], ident[:])
                ins.then_inc(s_xsT, 1)
                pe.wait_ge(s_cT, (i + 1) * 16)
                mm(ps[0:T, 2, TOKENS:2 * TOKENS], xc[0:STATE, p, 3, 0:T], cT[:, :], start=True, stop=True)
                mm(ps[0:T, 2, 2 * TOKENS:2 * TOKENS + T], xc[0:STATE, p, 3, T:TOKENS], cT[:, T:TOKENS],
                   start=True, stop=True).then_inc(s_cb, 1)

            run_slots(pe, ssm_slot)
            scan_out(IMAGES - 1, 1)

            pe.wait_ge(s_prep, 1)
            pe.wait_ge(s_part, 16 * NPART)
            pe.wait_ge(s_h1, IMAGES)

            def att_out_T(m):
                pe.wait_ge(s_ao, m + 1)
                for c in range(2):
                    for j in range(2):
                        at = c * TOKENS + j * T
                        ins = tr(ps[0:HALF, 4, at:at + T], ao[:, j, c * HALF:(c + 1) * HALF], ident[0:T, 0:T])
                ins.then_inc(s_aoT, 1)

            def att_project(m):
                pe.wait_ge(s_aoTe, m + 1)
                for j in range(2):
                    for c in range(2):
                        ins = mm(ps[0:T, 4, j * D:(j + 1) * D], aoT[:, c, j * T:(j + 1) * T], projw[:, c, :],
                                 start=c == 0, stop=c == 1)
                ins.then_inc(s_pr, 1)

            def router_T(m):
                pe.wait_ge(s_x2, m + 1)
                for c in range(2):
                    for j in range(2):
                        at = c * TOKENS + j * T
                        ins = tr(ps[0:HALF, 4, at:at + T], x2[:, j, c * HALF:(c + 1) * HALF], ident[0:T, 0:T])
                ins.then_inc(s_x2T, 1)

            def router(m):
                pe.wait_ge(s_x2Te, m + 1)
                for j in range(2):
                    for c in range(2):
                        ins = mm(ps[0:T, 4, j * EXPERTS:(j + 1) * EXPERTS], x2T[:, c, j * T:(j + 1) * T], wg[:, c, :],
                                 start=c == 0, stop=c == 1)
                ins.then_inc(s_lgp, 1)

            def att_slot(i, p, first, last):
                pe.wait_ge(s_xh, i + 1)
                for c in range(2):
                    for j in range(2):
                        at = c * TOKENS + j * T
                        ins = tr(ps[0:HALF, 4, at:at + T], xh[:, p, j, c * HALF:(c + 1) * HALF], ident[0:T, 0:T])
                ins.then_inc(s_xhT, 1)
                pe.wait_ge(s_xT, i + 1)
                if not first:
                    att_out_T(i - 1)
                    pe.wait_ge(s_pTe, i * 3)
                for k in range(2):
                    for c in range(GROUPS):
                        for f in range(2):
                            w = wqk[:, f, k, 4 * c:4 * c + 4, :].rearrange("p h d -> p (h d)")
                            ins = mm(ps[:, 5 + k, c * TOKENS:(c + 1) * TOKENS], w, xT[:, f, :], start=f == 0, stop=f == 1)
                ins.then_inc(s_qk, 1)
                for j in range(2):
                    for f in range(2):
                        ins = mm(ps[0:T, 7, j * D:(j + 1) * D], xT[:, f, j * T:(j + 1) * T], wqkv[:, f, 2 * D:3 * D],
                                 start=f == 0, stop=f == 1)
                ins.then_inc(s_v, 1)
                if not first:
                    att_project(i - 1)

                def scores(c):
                    pe.wait_ge(s_sub, i * 3 + c)
                    for g in range(4):
                        mm(ps[0:T, g, 0:3 * T], identb[0:T, 0:T], maskneg[:].rearrange("t k s -> t (k s)"),
                           start=True, stop=False)
                    for g in range(4):
                        r = slice(PAD * g, PAD * g + PAD)
                        mm(ps[0:T, g, 0:T], qs[r, c, 0:T], ks[r, c, 0:T], start=False, stop=False)
                        ins = mm(ps[0:T, g, T:3 * T], qs[r, c, T:TOKENS], ks[r, c, :], start=False, stop=True)
                    ins.then_inc(s_s, 1)

                def weigh(c):
                    pe.wait_ge(s_exp, i * 3 + (c + 1))
                    if c:
                        pe.wait_ge(s_pTe, i * 3 + c)
                    for g in range(4):
                        for k in range(3):
                            at = ((g % 2) * 3 + k) * T
                            ins = tr(ps[0:T, 5 + g // 2, at:at + T], probs[:, c, g, k, :], ident[0:T, 0:T])
                    ins.then_inc(s_pT, 1)
                    pe.wait_ge(s_pTe, i * 3 + (c + 1))
                    for g in range(4):
                        hd = 4 * c + g
                        E1 = AHEAD + 1
                        mm(ps[0:T, 7, hd * E1:(hd + 1) * E1], probsT[:, c, g, 0, :], vaug[:, 0, hd, :], start=True, stop=True)
                        at = (AHEADS + hd) * E1
                        mm(ps[0:T, 7, at:at + E1], probsT[:, c, g, 1, :], vaug[:, 0, hd, :], start=True, stop=False)
                        ins = mm(ps[0:T, 7, at:at + E1], probsT[:, c, g, 2, :], vaug[:, 1, hd, :], start=False, stop=True)
                    if c == GROUPS - 1:
                        ins.then_inc(s_pv, 1)

                pe.wait_ge(s_qkv, i + 1)
                scores(0)
                scores(1)
                weigh(0)
                if not first:
                    router_T(i - 1)
                scores(2)
                weigh(1)
                if not first:
                    router(i - 1)
                weigh(2)

            run_slots(pe, att_slot)
            att_out_T_wait = IMAGES - 1
            pe.wait_ge(s_lg, IMAGES - 1)
            att_out_T(att_out_T_wait)
            att_project(IMAGES - 1)
            router_T(IMAGES - 1)
            router(IMAGES - 1)

            pe.wait_ge(s_pd, 1)
            hot = hotb[:].rearrange("t k j e -> t (k j e)")
            mm(ps[0:T, 0, 0:2 * TILES * EXPERTS], r_lt_t[:], hot, start=True, stop=True)
            mm(ps[0:T, 1, 0:2 * TILES * EXPERTS], onesb[:], hot, start=True, stop=True).then_inc(s_pre, 1)

            def rows_in(e, p, n):
                pe.wait_ge(s_ex[p], n * 16)
                for c in range(2):
                    for k in range(3):
                        ins = tr(ps[0:HALF, c, k * CHUNK:(k + 1) * CHUNK], xs[:, p, k, c * HALF:(c + 1) * HALF],
                                 ident[0:CHUNK, 0:CHUNK])
                ins.then_inc(s_et, 1)

            pe.wait_ge(s_slot, 1)
            rows_in(0, 0, 1)

            def exp_slot(e, p, first, last):
                half = 1 if first else 4 if last else None
                n = half if half else (e + (1 if p else 2)) // 2
                pe.wait_ge(s_ew[p], n * 32)
                pe.wait_ge(s_ete, e + 1)
                for f in range(FT):
                    if not first or f > 3:
                        pe.wait_ge(s_gelu, e * FT + (f - 3))
                    for c in range(2):
                        ins = mm(ps[:, 2 + (2 * p + f) % 4, 0:CAP], fcw[:, p, c, f * 128:(f + 1) * 128], xsT[:, p, c, :],
                                 start=c == 0, stop=c == 1)
                    ins.then_inc(s_fc, 1)
                if not last:
                    rows_in(e + 1, 1 - p, 1 if first else (e + (3 if p else 2)) // 2)
                pe.wait_ge(s_gelu, e * FT + FT)
                pe.wait_ge(s_ob, e)
                for k in range(3):
                    for f in range(FT):
                        ins = mm(ps[0:CHUNK, 6 + k // 2, (k % 2) * D:(k % 2) * D + D],
                                 hid[:, f, k * CHUNK:(k + 1) * CHUNK], pjw[:, p, f, :], start=f == 0, stop=f == FT - 1)
                ins.then_inc(s_pj, 1)

            run_slots(pe, exp_slot)


def _layouts(v):
    import numpy as np

    g = {n: np.asarray(x) for n, x in v.items()}
    x, w = g.pop("x"), g.pop("L0_tok_w")
    g["patches"] = x.reshape(IMAGES, CHANNELS, GRID, PATCH, GRID, PATCH).transpose(1, 3, 5, 0, 2, 4).reshape(D, NTOK)
    g["patch_w"] = w.reshape(D, D).T
    g["conv_b"] = g.pop("L0_attn_conv_b").reshape(NCH, 128).T
    g["norm_w"] = g.pop("L0_attn_norm_w").reshape(3, 128).T
    g["d_skip"] = np.repeat(g.pop("L0_attn_D").reshape(3, 2).T, HEAD, axis=0)
    g["ln1_w"] = g.pop("L0_ffn_ln1_w").reshape(2, HALF).T
    g["ln1_b"] = g.pop("L0_ffn_ln1_b").reshape(2, HALF).T
    g["qk_b"] = g["L0_ffn_attn_qkv_b"][:2 * D].reshape(2, GROUPS, 4, AHEAD).transpose(2, 3, 0, 1)
    g["fc_b"] = g.pop("L0_ffn_exp_fc_b").reshape(EXPERTS * FT, 128).T
    return g


_INS = ["x", "L0_tok_w", "L0_tok_b", "L0_attn_W_in", "L0_attn_conv_w", "L0_attn_conv_b", "L0_attn_dt_bias",
        "L0_attn_A_log", "L0_attn_D", "L0_attn_norm_w", "L0_attn_W_out", "L0_ffn_ln1_w", "L0_ffn_ln1_b",
        "L0_ffn_ln2_w", "L0_ffn_ln2_b", "L0_ffn_attn_qkv_w", "L0_ffn_attn_qkv_b", "L0_ffn_attn_proj_w",
        "L0_ffn_attn_proj_b", "L0_ffn_w_g", "L0_ffn_exp_fc_w", "L0_ffn_exp_fc_b", "L0_ffn_exp_proj_w",
        "L0_ffn_exp_proj_b"]
_OUTS = [((IMAGES, TOKENS, D), "float32")]


def kernel(**inputs):
    import numpy as _np
    import concourse.bacc as _bacc
    from concourse import mybir as _mybir
    from concourse.bass_utils import run_bass_kernel_spmd as _run

    nc = _bacc.Bacc("TRN2", target_bir_lowering=False, num_devices=1)
    arrays, aps = {}, {}
    for name, x in _layouts({n: inputs[n] for n in _INS}).items():
        x = _np.ascontiguousarray(x)
        arrays[f"in_{name}_dram"] = x
        aps[name] = nc.dram_tensor(f"in_{name}_dram", x.shape, _mybir.dt.from_np(x.dtype), kind="ExternalInput").ap()
    shape, dtype = _OUTS[0]
    out = nc.dram_tensor("out_0_dram", shape, _mybir.dt.from_np(_np.dtype(dtype)), kind="ExternalOutput").ap()
    tower(nc, aps, out)
    r = _run(nc, [arrays], core_ids=[0])
    return r.results[0]["out_0_dram"]
```

```python
from contextlib import ExitStack

import concourse.bass as bass
from concourse import mybir

ALU = mybir.AluOpType
ACT = mybir.ActivationFunctionType
F32 = mybir.dt.float32
BF16 = mybir.dt.bfloat16
I32 = mybir.dt.int32
AX = mybir.AxisListType

IMAGES = 8
CHANNELS, SIDE, PATCH = 3, 96, 8
GRID = SIDE // PATCH
TOKENS = GRID * GRID
T = TOKENS // 2
TILES = 2 * IMAGES
D = 192
HALF = D // 2
NTOK = IMAGES * TOKENS
D_INNER = 2 * D
HEADS, HEAD = 6, 64
STATE = 64
NCH = (D_INNER + 2 * STATE) // 128
TAPS = 4
D_PROJ = 2 * D_INNER + 2 * STATE + HEADS
AHEADS, AHEAD = 12, 16
PAD = 32
GROUPS = AHEADS // 4
EXPERTS = 8
CAP = 360
CHUNK = CAP // 3
FF = 4 * D
FT = FF // 128
ROW = D + EXPERTS + 1
GATE0, TOKCOL = D, D + EXPERTS
SLOTS = EXPERTS * CAP
OUT_OF_RANGE = 8192.0
EPS = 1e-5
QMAX = 127.0
MAGIC = 12582912.0
RT = NTOK // 128
assert CAP == int(2 * 1.25 * NTOK // EXPERTS) and CAP % 2 == 0 and NTOK == TILES * T


def tower(nc, a, out):
    with ExitStack() as ctx:
        def sb(name, shape, dt=F32):
            return ctx.enter_context(nc.sbuf_tensor(name, shape, dt))

        def over(arena, at, shape, dt=F32):
            names = "abcdef"[:len(shape) - 1]
            size = 1
            for n in shape[1:]:
                size *= n
            end = at + (size if dt == F32 else size // 2)
            view = arena[0:shape[0], at:end]
            if dt != F32:
                view = view.bitcast(dt)
            return view.rearrange(f"p ({' '.join(names)}) -> p {' '.join(names)}", **dict(zip(names, shape[1:]))), end

        def sem(name):
            return ctx.enter_context(nc.semaphore(name))

        xslots = nc.dram_tensor("xslots", [SLOTS, ROW], F32, kind="Internal").ap()
        xrows = nc.dram_tensor("xrows", [NTOK, D], F32, kind="Internal").ap()
        ysum = nc.dram_tensor("ysum", [NTOK + CAP, D], F32, kind="Internal").ap()

        ps = ctx.enter_context(nc.psum_tensor("ps", [128, 8, 512], F32))

        arena_p = sb("arena_p", [128, 2 * GROUPS * 12 * T])
        xin, n = over(arena_p, 0, [HALF, 2, NTOK])
        rnd, _ = over(arena_p, n, [HALF, 2, NTOK])
        probs, n = over(arena_p, 0, [T, GROUPS, 4, 3, T])
        probsT, _ = over(arena_p, n, [T, GROUPS, 4, 3, T])
        hid, n = over(arena_p, 0, [128, FT, CAP])
        xsT, _ = over(arena_p, n, [HALF, 2, 2, CAP])
        arena_m = sb("arena_m", [128, 3 * 3 * HEADS * T])
        mix, n = over(arena_m, 0, [T, 2, 3, HEADS, T])
        decay, _ = over(arena_m, n, [T, 3, HEADS, T])
        fcw, _ = over(arena_m, 0, [HALF, 2, 2, FF])
        arena_x = sb("arena_x", [128, 2 * NCH * TOKENS + 2 * 2 * D_INNER])
        xc, n = over(arena_x, 0, [128, 2, NCH, TOKENS])
        dtx, _ = over(arena_x, n, [T, 2, 2, HEADS, HEAD])
        pjw, _ = over(arena_x, 0, [128, 2, FT, D])
        arena_q = sb("arena_q", [128, TILES * ROW])
        xqT, _ = over(arena_q, 0, [HALF, 2, NTOK], BF16)
        xd, _ = over(arena_q, 0, [128, RT, ROW])
        ident = sb("ident", [128, 128])
        identb = sb("identb", [128, 128], BF16)
        r_le_t = sb("r_le_t", [T, T], BF16)
        r_gt_s = sb("r_gt_s", [T, T], BF16)
        r_lt_t = sb("r_lt_t", [128, 128], BF16)
        onesb = sb("onesb", [128, 128], BF16)
        onecol = sb("onecol", [128, 1])
        sumrow = sb("sumrow", [128, 128])
        causal = sb("causal", [T, 3, T])
        maskneg = sb("maskneg", [T, 3, T], BF16)
        minus_half = sb("minus_half", [T, 4])
        revw = sb("revw", [128, RT, EXPERTS])
        restart = sb("restart", [128, EXPERTS * 2 * RT])
        win = sb("win", [HALF, 2, D_PROJ])
        cw = sb("cw", [128, NCH, TAPS])
        cb = sb("cb", [128, NCH])
        dtb = sb("dtb", [T, HEADS])
        alog = sb("alog", [T, HEADS])
        dskip = sb("dskip", [128, 3])
        normw = sb("normw", [128, 3])
        wout = sb("wout", [128, 3, D])
        ln1w = sb("ln1w", [HALF, 2])
        ln1b = sb("ln1b", [HALF, 2])
        ln2w = sb("ln2w", [T, D])
        ln2b = sb("ln2b", [T, D])
        wqkv = sb("wqkv", [HALF, 2, 3 * D])
        wqk = sb("wqk", [HALF, 2, 2, AHEADS, PAD])
        qkb = sb("qkb", [128, 2, GROUPS])
        vb = sb("vb", [T, D])
        projw = sb("projw", [128, GROUPS, D])
        projb = sb("projb", [T, D])
        wg = sb("wg", [HALF, 2, EXPERTS])
        tokb = sb("tokb", [T, D])
        fcb = sb("fcb", [128, EXPERTS * FT])
        pjb = sb("pjb", [CHUNK, EXPERTS * D])
        win_tok = sb("win_tok", [HALF, 2, D])
        rndw = sb("rndw", [HALF, 2 * D])
        wqT = sb("wqT", [HALF, 2, D], BF16)
        absmax = sb("absmax", [128, 2])
        absall = sb("absall", [128, 2])
        scales = sb("scales", [128, 2])
        inv = sb("inv", [128, 2])
        sxw = sb("sxw", [128, 1])
        h = sb("h", [T, TILES, D])
        hn = sb("hn", [T, TILES, D])
        u = hn
        stats_all = sb("stats_all", [T, TILES, 6])
        mv_all = sb("mv_all", [T, TILES, 2])
        veps_all = sb("veps_all", [T, TILES])
        rstd_all = sb("rstd_all", [T, TILES])
        hnT = sb("hnT", [HALF, 2, NTOK])
        stats = sb("stats", [T, 2, 6])
        spare = sb("spare", [1, 1])
        sparep = sb("sparep", [1, 1])
        mv = sb("mv", [T, 2, 2])
        veps = sb("veps", [T, 2])
        rstd = sb("rstd", [T, 2])
        dpre = sb("dpre", [T, TILES, HEADS])
        dabs = sb("dabs", [T, TILES, HEADS])
        dlost = sb("dlost", [T, TILES, HEADS])
        dpos = sb("dpos", [T, TILES, HEADS])
        donep = sb("donep", [T, TILES, HEADS])
        aexp = sb("aexp", [T, HEADS])
        dexp = sb("dexp", [T, TILES, HEADS])
        dlog = sb("dlog", [T, TILES, HEADS])
        dt = sb("dt", [T, TILES, HEADS])
        amat = sb("amat", [T, TILES, HEADS])
        arest = sb("arest", [T, TILES, HEADS])
        asplit = sb("asplit", [T, 3, TILES, HEADS], BF16)
        xpad = sb("xpad", [128, NCH, TAPS - 1 + TOKENS])
        conv = sb("conv", [128, NCH, TOKENS])
        cT = sb("cT", [STATE, TOKENS])
        sz = sb("sz", [128, 2, 3, TOKENS])
        amask = sb("amask", [T, 3, 2, HEADS, T], BF16)
        cbm = sb("cbm", [T, 3, T])
        yg = sb("yg", [128, 3, TOKENS])
        ysq = sb("ysq", [128, 3, TOKENS])
        msq = sb("msq", [T, 2])
        rms = sb("rms", [T, 2])
        xh = sb("xh", [T, 2, 2, D])
        xT = sb("xT", [HALF, 2, TOKENS])
        qs = sb("qs", [128, GROUPS, TOKENS])
        ks = sb("ks", [128, GROUPS, TOKENS])
        vpad = sb("vpad", [T, 2, AHEADS, PAD])
        smax = sb("smax", [T, 3, 4, 2])
        sneg = sb("sneg", [T, 3, 4, 2])
        rden = sb("rden", [128, GROUPS, TOKENS])
        pvs = yg
        att = ysq
        x1 = sb("x1", [T, 2, D])
        xh2 = sb("xh2", [T, 2, D])
        x2 = sb("x2", [T, 2, D])
        x2T = sb("x2T", [HALF, 2, TOKENS])
        base = sb("base", [T, 2, D])
        lg = sb("lg", [128, RT, EXPERTS])
        lgT = hnT[0:EXPERTS, 0, :]
        top = sb("top", [128, 2, RT])
        cand = sb("cand", [128, RT, EXPERTS])
        cand2 = sb("cand2", [128, RT, EXPERTS])
        lg2 = sb("lg2", [128, RT, EXPERTS])
        pick = sb("pick", [128, 2, RT])
        hotb = sb("hotb", [128, 2, RT, EXPERTS], BF16)
        tot = sb("tot", [128, EXPERTS, 2 * RT])
        incl = sb("incl", [128, EXPERTS, 2 * RT])
        before = sb("before", [128, EXPERTS, 2 * RT])
        rankm = sb("rankm", [128, 2 * RT, EXPERTS])
        rank = sb("rank", [128, 2 * RT])
        late = sb("late", [128, 2 * RT])
        slotf = sb("slotf", [128, 2 * RT])
        slot = sb("slot", [128, 2 * RT], I32)
        pdiff = sb("pdiff", [128, RT])
        pexp = sb("pexp", [128, RT])
        psum1 = sb("psum1", [128, RT])
        p1 = sb("p1", [128, RT])
        p2 = sb("p2", [128, RT])
        g1 = sb("g1", [128, RT, EXPERTS])
        g2 = sb("g2", [128, RT, EXPERTS])
        fill = sb("fill", [CHUNK, 3, ROW])
        xs = sb("xs", [CHUNK, 2, 3, D])
        meta = sb("meta", [CHUNK, 3 * EXPERTS, EXPERTS + 1])
        yrow = sb("yrow", [CHUNK, 2, 3], I32)
        ob = sb("ob", [CHUNK, 3, D])
        og = sb("og", [CHUNK, 2, 3, D])

        s_x = sem("s_x")
        s_w = sem("s_w")
        s_wt = sem("s_wt")
        s_par = sem("s_par")
        s_part = sem("s_part")
        s_moeb = sem("s_moeb")
        s_fillx = sem("s_fillx")
        s_const = sem("s_const")
        s_pad = sem("s_pad")
        s_padb = sem("s_padb")
        s_prep = sem("s_prep")
        s_fcbT = sem("s_fcbT")
        s_fcb = sem("s_fcb")
        s_absmax = sem("s_absmax")
        s_absall = sem("s_absall")
        s_scale = sem("s_scale")
        s_rnd = sem("s_rnd")
        s_q = sem("s_q")
        s_qT = sem("s_qT")
        s_qTe = sem("s_qTe")
        s_qTd = sem("s_qTd")
        s_tok = sem("s_tok")
        s_h = sem("s_h")
        s_var = sem("s_var")
        s_rstd = sem("s_rstd")
        s_hn = sem("s_hn")
        s_hnT = sem("s_hnT")
        s_hnTe = sem("s_hnTe")
        s_a0 = sem("s_a0")
        s_dtp = sem("s_dtp")
        s_dabs = sem("s_dabs")
        s_dexp = sem("s_dexp")
        s_donep = sem("s_donep")
        s_dlog = sem("s_dlog")
        s_aexp = sem("s_aexp")
        s_as = sem("s_as")
        s_px = sem("s_px")
        s_pbc = sem("s_pbc")
        s_pz = sem("s_pz")
        s_padx = sem("s_padx")
        s_padbc = sem("s_padbc")
        s_convx = sem("s_convx")
        s_convbc = sem("s_convbc")
        s_xc = sem("s_xc")
        s_bc = sem("s_bc")
        s_cT = sem("s_cT")
        s_z = sem("s_z")
        s_amask = sem("s_amask")
        s_seg = sem("s_seg")
        s_decay = sem("s_decay")
        s_xsT = sem("s_xsT")
        s_cb = sem("s_cb")
        s_cbm = sem("s_cbm")
        s_mix = sem("s_mix")
        s_y = sem("s_y")
        s_yg = sem("s_yg")
        s_ysq = sem("s_ysq")
        s_wo = sem("s_wo")
        s_msq = sem("s_msq")
        s_rms = sem("s_rms")
        s_h1 = sem("s_h1")
        s_conv_step = sem("s_conv_step")
        s_y_step = sem("s_y_step")
        s_var1 = sem("s_var1")
        s_rstd1 = sem("s_rstd1")
        s_xh = sem("s_xh")
        s_xhT = sem("s_xhT")
        s_xT = sem("s_xT")
        s_q1 = sem("s_q1")
        s_k1 = sem("s_k1")
        s_qk = sem("s_qk")
        s_v = sem("s_v")
        s_vpad = sem("s_vpad")
        s_s = sem("s_s")
        s_max = sem("s_max")
        s_exp = sem("s_exp")
        s_pT = sem("s_pT")
        s_pTe = sem("s_pTe")
        s_pT1 = sem("s_pT1")
        s_pv = sem("s_pv")
        s_ao = sem("s_ao")
        s_pvs = sem("s_pvs")
        s_sel = sem("s_sel")
        s_pr = sem("s_pr")
        s_x1 = sem("s_x1")
        s_base = sem("s_base")
        s_based = sem("s_based")
        s_var2 = sem("s_var2")
        s_rstd2 = sem("s_rstd2")
        s_x2 = sem("s_x2")
        s_xd = sem("s_xd")
        s_x2T = sem("s_x2T")
        s_x2Te = sem("s_x2Te")
        s_lgp = sem("s_lgp")
        s_lg = sem("s_lg")
        s_lgt = sem("s_lgt")
        s_ln_step = sem("s_ln_step")
        s_max_step = sem("s_max_step")
        s_x1_step = sem("s_x1_step")
        s_ao_step = sem("s_ao_step")
        s_hot = sem("s_hot")
        s_pre = sem("s_pre")
        s_slot = sem("s_slot")
        s_pd = sem("s_pd")
        s_pe = sem("s_pe")
        s_gate = sem("s_gate")
        s_r_step = sem("s_r_step")
        s_scat = sem("s_scat")
        s_meta = sem("s_meta")
        s_et = sem("s_et")
        s_ete = sem("s_ete")
        s_fc = sem("s_fc")
        s_gelu = sem("s_gelu")
        s_pj = sem("s_pj")
        s_ob = sem("s_ob")
        s_og = sem("s_og")
        s_add = sem("s_add")
        s_out = sem("s_out")
        s_rmsp = sem("s_rmsp")
        s_ln2p = sem("s_ln2p")
        s_lnp = sem("s_lnp")
        s_ap = sem("s_ap")
        s_tokcol = sem("s_tokcol")
        s_relay = sem("s_relay")
        s_ew = [sem("s_ew0"), sem("s_ew1")]
        s_ex = [sem("s_ex0"), sem("s_ex1")]

        def bc(ap, n):
            return ap.unsqueeze(len(ap.shape)).to_broadcast(list(ap.shape) + [n])

        def bc_at(ap, at, n):
            v = ap.unsqueeze(at)
            s = list(v.shape)
            s[at] = n
            return v.to_broadcast(s)

        def imgs(t, i):
            return t[:, bass.ds(i * 2, 2), :]

        def tile(t, i, j):
            return t[:, bass.ds(i * 2 + j, 1), :].rearrange("t o d -> t (o d)")

        def run_slots(eng, slot):
            slot(0, 0, True, False)
            with eng.Fori(1, IMAGES - 2, 2) as i:
                slot(i, 1, False, False)
                slot(i + 1, 0, False, False)
            slot(7, 1, False, True)

        class Chain:

            def __init__(self, eng, s, i, per):
                self.eng, self.s, self.i, self.per, self.n = eng, s, i, per, 0

            def __call__(self, ins):
                self.n += 1
                ins.then_inc(self.s, 1)
                self.eng.wait_ge(self.s, self.i * self.per + self.n)

            def close(self):
                assert self.n == self.per, (self.n, self.per)

        block = ctx.enter_context(nc.Block())
        NPAR, NPART = 6, 14

        @block.sync
        def _(sp):
            def load(dst, src, s):
                sp.dma_start(dst, src).then_inc(s, 16)

            for c in range(2):
                load(xin[:, c, 0:NTOK // 2], a["patches"][c * HALF:(c + 1) * HALF, 0:NTOK // 2], s_x)
            load(win[:], a["L0_attn_W_in"].rearrange("(c p) n -> p c n", p=HALF), s_par)
            load(cw[:], a["L0_attn_conv_w"].rearrange("(c p) k -> p c k", p=128), s_par)
            load(cb[:], a["conv_b"], s_par)
            load(dskip[:], a["d_skip"], s_par)
            load(normw[:], a["norm_w"], s_par)
            load(wout[:], a["L0_attn_W_out"].rearrange("(c p) n -> p c n", p=128), s_par)
            load(wqkv[:], a["L0_ffn_attn_qkv_w"].rearrange("(c p) n -> p c n", p=HALF), s_part)
            sp.wait_ge(s_const, 1)
            load(ysum[NTOK:NTOK + CAP, :].rearrange("(c p) d -> p c d", p=CHUNK), fill[:, :, 0:D], s_based)
            sp.wait_ge(s_padb, 1)
            for g in range(4):
                load(qkb[PAD * g:PAD * g + AHEAD, :, :], a["qk_b"][g], s_part)
                load(projw[PAD * g:PAD * g + AHEAD, :, :],
                     a["L0_ffn_attn_proj_w"].rearrange("(c g r) n -> g r c n", g=4, r=AHEAD)[g], s_part)
            load(ln1w[:], a["ln1_w"], s_part)
            load(ln1b[:], a["ln1_b"], s_part)
            load(fcb[:], a["fc_b"], s_part)
            load(wg[:], a["L0_ffn_w_g"].rearrange("(c p) n -> p c n", p=HALF), s_part)
            load(vb[:], a["L0_ffn_attn_qkv_b"][2 * D:3 * D].rearrange("(o d) -> o d", o=1).to_broadcast([T, D]), s_part)
            load(pjb[:], a["L0_ffn_exp_proj_b"].rearrange("e o d -> o (e d)").to_broadcast([CHUNK, EXPERTS * D]), s_moeb)

            def load_weights(e, p):
                load(fcw[:, p, :, :], a["L0_ffn_exp_fc_w"][e].rearrange("(c p) f -> p c f", p=HALF), s_ew[p])
                load(pjw[:, p, :, :], a["L0_ffn_exp_proj_w"][e].rearrange("(f p) d -> p f d", p=128), s_ew[p])

            with sp.Fori(0, IMAGES - 1, 2) as i:
                for p in range(2):
                    sp.wait_ge(s_bc, i + p + 1)
                    load(cT[:, :], xc[STATE:128, p, NCH - 1, :], s_cT)

            sp.wait_ge(s_wo, IMAGES)
            load_weights(0, 0)
            load_weights(1, 1)

            with sp.Fori(0, IMAGES - 1, 2) as i:
                for p in range(2):
                    sp.wait_ge(s_base, i + p + 1)
                    load(ysum[bass.ds((i + p) * TOKENS, TOKENS), :].rearrange("(j t) d -> t j d", t=T), base[:], s_based)
                    sp.wait_ge(s_x2, i + p + 1)
                    load(xrows[bass.ds((i + p) * TOKENS, TOKENS), :].rearrange("(j t) d -> t j d", t=T), x2[:], s_based)
            sp.wait_ge(s_based, 16 * (2 * IMAGES + 1))
            load(xd[:, :, 0:D], xrows.rearrange("(n p) d -> p n d", p=128), s_xd)

            def load_rows(e, p):
                load(xs[:, p, :, :], xslots[bass.ds(e * CAP, CAP), 0:D].rearrange("(c p) n -> p c n", p=CHUNK), s_ex[p])

            sp.wait_ge(s_scat, 16 * 2 * RT)
            load_rows(0, 0)
            load_rows(1, 1)
            load(meta[:], xslots[:, D:ROW].rearrange("(c p) n -> p c n", p=CHUNK), s_meta)
            with sp.Fori(0, EXPERTS - 3, 2) as e:
                for p in range(2):
                    fw = a["L0_ffn_exp_fc_w"][bass.ds(e + (p + 2), 1)].rearrange("o (c p) f -> p (o c) f", p=HALF)
                    pw = a["L0_ffn_exp_proj_w"][bass.ds(e + (p + 2), 1)].rearrange("o (f p) d -> p (o f) d", p=128)
                    sp.wait_ge(s_et, e + p + 1)
                    load_rows(e + (p + 2), p)
                    sp.wait_ge(s_fc, (e + p + 1) * FT)
                    load(fcw[:, p, :, :], fw, s_ew[p])
                    sp.wait_ge(s_pj, e + p + 1)
                    load(pjw[:, p, :, :], pw, s_ew[p])
            sp.wait_ge(s_add, EXPERTS * 48)
            load(out.rearrange("b t d -> (b t) d"), ysum[0:NTOK, :], s_out)
            sp.wait_ge(s_out, 16)

        @block.scalar
        def _(act):
            def load(dst, src, s):
                act.dma_start(dst, src).then_inc(s, 16)

            act_f = nc.scalar.activation
            load(win_tok[:], a["patch_w"].rearrange("(c p) d -> p c d", p=HALF), s_wt)
            for c in range(2):
                load(xin[:, c, NTOK // 2:], a["patches"][c * HALF:(c + 1) * HALF, NTOK // 2:], s_x)
            for dst, name in ((tokb, "L0_tok_b"), (dtb, "L0_attn_dt_bias"), (alog, "L0_attn_A_log"),
                              (ln2w, "L0_ffn_ln2_w"), (ln2b, "L0_ffn_ln2_b"), (projb, "L0_ffn_attn_proj_b")):
                load(dst[:], a[name].rearrange("(o d) -> o d", o=1).to_broadcast(list(dst.shape)), s_w)
            act.wait_ge(s_w, 16 * 6)
            act_f(aexp[:], alog[:], ACT.Exp).then_inc(s_aexp, 1)

            act.wait_ge(s_rnd, 1)
            act_f(wqT[:].rearrange("p c k -> p (c k)"), rndw[:], ACT.Copy, bias=-MAGIC)
            for n in range(2):
                act.wait_ge(s_rnd, n + 1)
                at = slice(n * NTOK // 2, (n + 1) * NTOK // 2)
                act_f(xqT[:, :, at], rnd[:, :, at], ACT.Copy, bias=-MAGIC).then_inc(s_q, 1)
            for b in range(IMAGES):
                act.wait_ge(s_hnT, b + 1)
                act_f(hnT[:, :, b * TOKENS:(b + 1) * TOKENS],
                      ps[0:HALF, b % 2, 0:2 * TOKENS].rearrange("k (c t) -> k c t", c=2), ACT.Copy).then_inc(s_hnTe, 1)
            act.wait_ge(s_dabs, 1)
            act_f(dexp[:], dabs[:], ACT.Exp, scale=-1.0).then_inc(s_dexp, 1)
            act.wait_ge(s_donep, 1)
            act_f(dlog[:], donep[:], ACT.Ln).then_inc(s_dlog, 1)

            x_tiles, bc_tile = slice(0, NCH - 1), NCH - 1

            def last_tap(tiles, src):
                for c in tiles:
                    ins = act_f(conv[:, c, :], src(c), ACT.Identity, bias=cb[:, c:c + 1], scale=cw[:, c, TAPS - 1:])
                return ins

            def pad(m, first):
                act.wait_ge(s_px, m + 1)
                act_f(xpad[:, x_tiles, TAPS - 1:], ps[:, 1, 0:3 * TOKENS].rearrange("k (c t) -> k c t", c=3), ACT.Copy)
                act.wait_ge(s_pbc, m + 1)
                act_f(xpad[:, bc_tile, TAPS - 1:], ps[:, 0, 0:TOKENS], ACT.Copy)
                if not first:
                    act.wait_ge(s_xc, m)
                last_tap([bc_tile], lambda c: ps[:, 0, 0:TOKENS]).then_inc(s_padbc, 1)
                last_tap(range(NCH - 1), lambda c: ps[:, 1, c * TOKENS:(c + 1) * TOKENS]).then_inc(s_padx, 1)

            def mean_square(m):
                act.wait_ge(s_yg, m + 1)
                act_f(ysq[:], yg[:], ACT.Square).then_inc(s_ysq, 1)
                act.wait_ge(s_wo, m + 1)
                act_f(msq[:], ps[0:T, 4, 400:402], ACT.Copy, bias=EPS, scale=1.0 / D_INNER).then_inc(s_msq, 1)

            def ssm_slot(i, p, first, last):
                act.wait_ge(s_convbc, i + 1)
                act_f(xc[:, p, bc_tile, :], conv[:, bc_tile, :], ACT.Silu).then_inc(s_bc, 1)
                act.wait_ge(s_pz, i + 1)
                act_f(sz[:, p, :, :].rearrange("k c t -> k (c t)"), ps[:, 2, 0:3 * TOKENS], ACT.Silu).then_inc(s_z, 1)
                if not first:
                    mean_square(i - 1)
                act.wait_ge(s_convx, i + 1)
                act_f(xc[:, p, x_tiles, :], conv[:, x_tiles, :], ACT.Silu).then_inc(s_xc, 1)
                act.wait_ge(s_seg, i + 1)
                act_f(decay[:].rearrange("s k h t -> s k (h t)"), ps[0:T, 5:8, 0:HEADS * T], ACT.Exp).then_inc(s_decay, 1)
                if not last:
                    pad(i + 1, False)

            pad(0, True)
            run_slots(act, ssm_slot)
            mean_square(IMAGES - 1)

            act.wait_ge(s_part, 16 * NPART)

            def enter_T(m):
                act.wait_ge(s_xhT, m + 1)
                for c in range(2):
                    ins = act_f(xT[:, c, :], ps[0:HALF, 4, c * TOKENS:(c + 1) * TOKENS], ACT.Identity,
                                bias=ln1b[:, c:c + 1], scale=ln1w[:, c:c + 1])
                ins.then_inc(s_xT, 1)

            def weighted(m):
                act.wait_ge(s_pv, m + 1)
                act_f(pvs[:].rearrange("p c t -> p (c t)"), ps[:, 7, 0:GROUPS * TOKENS], ACT.Copy).then_inc(s_pvs, 1)

            def att_x2(m):
                act.wait_ge(s_x2T, m + 1)
                act_f(x2T[:], ps[0:HALF, 4, 0:2 * TOKENS].rearrange("k (c t) -> k c t", c=2), ACT.Copy).then_inc(s_x2Te, 1)

            def logits(m):
                act.wait_ge(s_lgp, m + 1)
                act_f(lgT[:, bass.ds(m * TOKENS, TOKENS)], ps[0:EXPERTS, 4, 2 * TOKENS:3 * TOKENS], ACT.Copy).then_inc(s_lg, 1)

            def att_slot(i, p, first, last):
                for k, ready, out_ in ((0, s_q1, qs), (1, s_k1, ks)):
                    act.wait_ge(ready, i + 1)
                    for c in range(GROUPS):
                        ins = act_f(out_[:, c, :], ps[:, 5 + k, c * TOKENS:(c + 1) * TOKENS], ACT.Identity,
                                    bias=qkb[:, k, c:c + 1])
                ins.then_inc(s_qk, 1)

                def weights(r):
                    act.wait_ge(s_max, i * 3 + (r + 1))
                    for n in range(4):
                        bank, at = (2 * r + n // 2, n % 2 * 3 * T) if r < 2 else (n, 0)
                        act_f(probs[:, r, n, 0, :], ps[0:T, bank, at:at + T], ACT.Exp, bias=sneg[:, r, n, 0:1])
                        ins = act_f(probs[:, r, n, 1:3, :].rearrange("t k s -> t (k s)"),
                                    ps[0:T, bank, at + T:at + 3 * T], ACT.Exp, bias=sneg[:, r, n, 1:2])
                    ins.then_inc(s_exp, 1)

                def turned(r):
                    act.wait_ge(s_pT, i * 3 + (r + 1))
                    act_f(probsT[:, r].rearrange("s (b g) k t -> s b (g k t)", b=2),
                          ps[0:T, 5:7, 0:6 * T], ACT.Copy).then_inc(s_pTe, 1)

                weights(0)
                weights(1)
                turned(0)
                if not last:
                    enter_T(i + 1)
                weights(2)
                turned(2)
                if not first:
                    att_x2(i - 1)
                    logits(i - 1)
                weighted(i)

            enter_T(0)
            run_slots(act, att_slot)
            att_x2(IMAGES - 1)
            logits(IMAGES - 1)

            act.wait_ge(s_pd, 1)
            act_f(pexp[:], pdiff[:], ACT.Exp).then_inc(s_pe, 1)

            def exp_slot(e, p, first, last):
                for f in range(FT):
                    if f == 0:
                        act.wait_ge(s_pj, e)
                    act.wait_ge(s_fc, e * FT + (f + 1))
                    act_f(hid[:, f, :], ps[:, 2 + (2 * p + f) % 4, 0:CAP], ACT.Gelu,
                          bias=fcb[:, bass.ds(e * FT + f, 1)]).then_inc(s_gelu, 1)

            run_slots(act, exp_slot)

        @block.gpsimd
        def _(pool):
            g = nc.gpsimd
            g.memset(ident[:], 0.0)
            g.memset(identb[:], 0.0)
            g.memset(r_le_t[:], 1.0)
            g.memset(r_gt_s[:], 1.0)
            g.memset(r_lt_t[:], 1.0)
            g.memset(causal[:], 1.0)
            g.memset(maskneg[:], 0.0)
            g.memset(restart[:], 1.0)
            g.memset(fill[:], 0.0)
            g.memset(onesb[:], 1.0)
            g.memset(onecol[:], 1.0)
            g.memset(minus_half[:], -0.5)
            g.memset(xpad[:, :, 0:TAPS - 1], 0.0)
            g.memset(vpad[:], 1.0)
            g.memset(wqk[:], 0.0)
            g.memset(projw[:], 0.0)
            g.memset(sumrow[:], 0.0)
            g.memset(qkb[:], 0.0).then_inc(s_padb, 1)
            pool.wait_ge(s_padb, 1)
            for m in (ident, identb):
                g.affine_select(out=m[:], in_=m[:], compare_op=ALU.not_equal, fill=1.0, base=0,
                                pattern=[[-1, 128]], channel_multiplier=1)
            g.affine_select(out=sumrow[:], in_=sumrow[:], compare_op=ALU.not_equal, fill=1.0, base=-AHEAD,
                            pattern=[[-PAD, 4], [0, PAD]], channel_multiplier=1)
            g.affine_select(out=r_le_t[:], in_=r_le_t[:], compare_op=ALU.is_ge, fill=0.0, base=0,
                            pattern=[[1, T]], channel_multiplier=-1)
            g.affine_select(out=r_gt_s[:], in_=r_gt_s[:], compare_op=ALU.is_gt, fill=0.0, base=0,
                            pattern=[[-1, T]], channel_multiplier=1)
            g.affine_select(out=r_lt_t[:], in_=r_lt_t[:], compare_op=ALU.is_gt, fill=0.0, base=0,
                            pattern=[[1, 128]], channel_multiplier=-1)
            g.affine_select(out=causal[:, 0:3:2, :], in_=causal[:, 0:3:2, :], compare_op=ALU.is_ge, fill=0.0,
                            base=0, pattern=[[0, 2], [1, T]], channel_multiplier=-1)
            g.affine_select(out=maskneg[:, 0:3:2, :], in_=maskneg[:, 0:3:2, :], compare_op=ALU.is_ge, fill=-1e30,
                            base=0, pattern=[[0, 2], [-1, T]], channel_multiplier=1)
            g.affine_select(out=restart[:], in_=restart[:], compare_op=ALU.not_equal, fill=0.0,
                            base=0, pattern=[[0, EXPERTS], [1, 2 * RT]], channel_multiplier=0)
            for e in range(EXPERTS):
                g.memset(revw[:, :, e], float(EXPERTS - e))
            g.iota(fill[:, :, TOKCOL].bitcast(I32), pattern=[[CHUNK, 3]], base=NTOK, channel_multiplier=1
                   ).then_inc(s_const, 1)
            pool.wait_ge(s_const, 1)
            pool.wait_ge(s_absmax, 2)
            g.partition_all_reduce(absall[0:HALF, :], absmax[0:HALF, :], HALF, bass.bass_isa.ReduceOp.absmax
                                   ).then_inc(s_absall, 1)
            for e in range(EXPERTS):
                pool.dma_start(xslots[e * CAP:(e + 1) * CAP, :].rearrange("(c p) n -> p c n", p=CHUNK), fill[:]
                               ).then_inc(s_fillx, 16)
            for n in range(TILES // 4):
                pool.wait_ge(s_var, n + 1)
                four = slice(4 * n, 4 * n + 4)
                g.tensor_tensor(rstd_all[:, four], veps_all[:, four], minus_half[:], ALU.pow).then_inc(s_rstd, 1)
            pool.wait_ge(s_par, 16 * NPAR)
            g.tensor_tensor(wout[:], wout[:], bc(normw[:], D), ALU.mult)
            pool.wait_ge(s_part, 16 * NPART)
            scale = float(AHEAD) ** -0.5
            for k in range(2):
                for c in range(2):
                    src = wqkv[:, c, k * D:(k + 1) * D].rearrange("p (h d) -> p h d", d=AHEAD)
                    g.tensor_scalar(wqk[:, c, k, :, 0:AHEAD], src, 1.0 if k else scale, None, ALU.mult)
            g.tensor_scalar(qkb[:, 0, :], qkb[:, 0, :], scale, None, ALU.mult).then_inc(s_prep, 1)

            def pow_rms(m):
                pool.wait_ge(s_msq, m + 1)
                g.tensor_tensor(rms[:], msq[:], minus_half[:, 0:2], ALU.pow).then_inc(s_rms, 1)

            pool.wait_ge(s_as, 1)

            def ssm_slot(i, p, first, last):
                pool.wait_ge(s_seg, i)
                for k in range(3):
                    ins = g.tensor_tensor(amask[:, k], bc_at(bc_at(r_le_t[:], 1, HEADS), 1, 2),
                                          bc(asplit[:, k, bass.ds(i * 2, 2), :], T), ALU.mult)
                ins.then_inc(s_amask, 1)
                if not first:
                    pow_rms(i - 1)

            run_slots(pool, ssm_slot)
            pow_rms(IMAGES - 1)

            def rstd_ln(i):
                for n in range(2):
                    pool.wait_ge(s_var1, i * 2 + (n + 1))
                    g.tensor_tensor(rstd[:], veps[:], minus_half[:, 0:2], ALU.pow).then_inc(s_rstd1, 1)

            def after_attention(m):
                pool.wait_ge(s_x1, m + 1)
                pool.wait_ge(s_based, m * 32 + 16)
                g.tensor_tensor(base[:], x1[:], imgs(h, m), ALU.add).then_inc(s_base, 1)
                pool.wait_ge(s_var2, m + 1)
                g.tensor_tensor(rstd[:], veps[:], minus_half[:, 0:2], ALU.pow).then_inc(s_rstd2, 1)

            rstd_ln(0)
            g.iota(xd[:, :, TOKCOL].bitcast(I32), pattern=[[128, RT]], base=0, channel_multiplier=1).then_inc(s_tokcol, 1)

            def att_slot(i, p, first, last):
                if not last:
                    rstd_ln(i + 1)
                if not first:
                    after_attention(i - 1)

            run_slots(pool, att_slot)
            after_attention(IMAGES - 1)

            pool.wait_ge(s_gate, 1)
            pool.wait_ge(s_slot, 1)
            pool.wait_ge(s_xd, 16)
            pool.wait_ge(s_tokcol, 1)
            pool.wait_ge(s_fillx, 16 * EXPERTS)
            for n in range(2 * RT):
                g.indirect_dma_start(out=xslots[:, :],
                                     out_offset=bass.IndirectOffsetOnAxis(ap=slot[:, n:n + 1], axis=0),
                                     in_=xd[:, n % RT, :], in_offset=None,
                                     bounds_check=SLOTS - 1, oob_is_err=False).then_inc(s_scat, 16)

            pool.wait_ge(s_based, 16 * (2 * IMAGES + 1))

            def exp_slot(e, p, first, last):
                pool.wait_ge(s_relay, e)
                pool.wait_ge(s_og, e + 1)
                pool.wait_ge(s_add, e * 48)
                g.tensor_tensor(sparep[:], onecol[0:1, :], onecol[0:1, :], ALU.mult).then_inc(s_relay, 1)
                for c in range(3):
                    g.indirect_dma_start(out=ysum[:, :],
                                         out_offset=bass.IndirectOffsetOnAxis(
                                             ap=yrow[:, p, c:c + 1], axis=0),
                                         in_=og[:, p, c, :], in_offset=None, compute_op=ALU.add).then_inc(s_add, 16)

            run_slots(pool, exp_slot)

        @block.vector
        def _(dve):
            v = nc.vector

            dve.wait_ge(s_wt, 16)
            v.tensor_reduce(absmax[0:HALF, 1:2], win_tok[:].rearrange("p j k -> p (j k)"), AX.X, ALU.max,
                            apply_absolute_value=True).then_inc(s_absmax, 1)
            dve.wait_ge(s_x, 16 * 4)
            v.tensor_reduce(absmax[0:HALF, 0:1], xin.rearrange("x c t -> x (c t)"), AX.X, ALU.max,
                            apply_absolute_value=True).then_inc(s_absmax, 1)
            dve.wait_ge(s_absall, 1)
            link = Chain(dve, s_a0, 0, 99)
            link(v.tensor_scalar(scales[0:HALF, :], absall[0:HALF, :], 1e-8, 1.0 / QMAX, ALU.max, ALU.mult))
            v.tensor_tensor(sxw[0:HALF, :], scales[0:HALF, 0:1], scales[0:HALF, 1:2], ALU.mult)
            link(v.reciprocal(inv[0:HALF, :], scales[0:HALF, :]))
            v.tensor_scalar(rndw[:], win_tok[:].rearrange("p j k -> p (j k)"), inv[0:HALF, 1:2], MAGIC, ALU.mult, ALU.add)
            for n in range(2):
                at = slice(n * NTOK // 2, (n + 1) * NTOK // 2)
                link(v.tensor_scalar(rnd[:, :, at], xin[:, :, at], inv[0:HALF, 0:1], MAGIC, ALU.mult, ALU.add))
                if n == 0:
                    v.tensor_scalar(rndw[:], rndw[:], MAGIC - QMAX, MAGIC + QMAX, ALU.max, ALU.min)
                v.tensor_scalar(rnd[:, :, at], rnd[:, :, at], MAGIC - QMAX, MAGIC + QMAX, ALU.max, ALU.min
                                ).then_inc(s_rnd, 1)

            def embed(b):
                dve.wait_ge(s_tok, b + 1)
                v.scalar_tensor_tensor(out=h[:, 2 * b:2 * b + 2, :],
                                       in0=ps[0:T, 5 + b % 2, 0:2 * D].rearrange("t (j d) -> t j d", j=2),
                                       scalar=sxw[0:T, :], in1=bc_at(tokb[:], 1, 2), op0=ALU.mult, op1=ALU.add
                                       ).then_inc(s_h, 1)

            def embedded_stats(b):
                dve.wait_ge(s_h, b + 1)
                for j in range(2 * b, 2 * b + 2):
                    ins = v.bn_stats(stats_all[:, j, :], h[:, j, :])
                return ins

            def spread_pair(n):
                for j in range(4 * n, 4 * n + 4):
                    ins = v.bn_aggr(mv_all[:, j, :], stats_all[:, j, :])
                link(ins)
                four = slice(4 * n, 4 * n + 4)
                v.tensor_scalar_add(veps_all[:, four], mv_all[:, four, 1], EPS).then_inc(s_var, 1)

            def normalise_pair(n):
                dve.wait_ge(s_rstd, n + 1)
                for j in range(4 * n, 4 * n + 4):
                    v.tensor_scalar(hn[:, j, :], h[:, j, :], mv_all[:, j, 0:1], rstd_all[:, j:j + 1],
                                    ALU.subtract, ALU.mult).then_inc(s_hn, 1)

            for b in range(IMAGES + 1):
                if b < IMAGES:
                    embed(b)
                if b:
                    ins = embedded_stats(b - 1)
                    if b % 2 == 0:
                        link(ins)
                        spread_pair(b // 2 - 1)
                        if b >= 4:
                            normalise_pair(b // 2 - 2)
            normalise_pair(IMAGES // 2 - 1)
            dve.wait_ge(s_dtp, 1)
            link(v.tensor_tensor(dpre[:], ps[0:T, 3, 0:TILES * HEADS].rearrange("t (j h) -> t j h", h=HEADS),
                                 bc_at(dtb[:], 1, TILES), ALU.add))
            link(v.tensor_scalar(dpos[:], dpre[:], 0.0, None, ALU.max))
            v.scalar_tensor_tensor(out=dabs[:], in0=dpos[:], scalar=2.0, in1=dpre[:], op0=ALU.mult, op1=ALU.subtract
                                   ).then_inc(s_dabs, 1)
            dve.wait_ge(s_dexp, 1)
            v.tensor_scalar_add(donep[:], dexp[:], 1.0).then_inc(s_donep, 1)
            dve.wait_ge(s_donep, 1)
            link(v.scalar_tensor_tensor(out=dlost[:], in0=donep[:], scalar=-1.0, in1=dexp[:],
                                        op0=ALU.add, op1=ALU.subtract))
            link(v.tensor_tensor(dpos[:], dpos[:], dlost[:], ALU.subtract))
            dve.wait_ge(s_dlog, 1)
            link(v.tensor_tensor(dt[:], dpos[:], dlog[:], ALU.add))
            dve.wait_ge(s_aexp, 1)
            link(v.scalar_tensor_tensor(out=amat[:], in0=dt[:], scalar=-1.0, in1=bc_at(aexp[:], 1, TILES),
                                        op0=ALU.mult, op1=ALU.mult))
            link(v.tensor_copy(asplit[:, 0], amat[:]))
            link(v.tensor_tensor(arest[:], amat[:], asplit[:, 0], ALU.subtract))
            link(v.tensor_copy(asplit[:, 1], arest[:]))
            link(v.tensor_tensor(arest[:], arest[:], asplit[:, 1], ALU.subtract))
            v.tensor_copy(asplit[:, 2], arest[:]).then_inc(s_as, 1)
            dve.wait_ge(s_par, 16 * NPAR)
            dve.wait_ge(s_const, 1)

            def gate_y(m, q):
                step = Chain(dve, s_y_step, m, 1)
                dve.wait_ge(s_y, m + 1)
                for c in range(3):
                    ins = v.scalar_tensor_tensor(out=yg[:, c, :], in0=xc[:, q, c, :], scalar=dskip[:, c:c + 1],
                                                 in1=ps[:, 3, c * TOKENS:(c + 1) * TOKENS], op0=ALU.mult, op1=ALU.add)
                step(ins)
                v.tensor_tensor(yg[:], yg[:], sz[:, q], ALU.mult).then_inc(s_yg, 1)

            def residual(m):
                dve.wait_ge(s_rms, m + 1)
                for j in range(2):
                    ins = v.scalar_tensor_tensor(out=tile(h, m, j), in0=ps[0:T, 4, j * D:(j + 1) * D],
                                                 scalar=rms[:, j:j + 1], in1=tile(h, m, j), op0=ALU.mult, op1=ALU.add)
                ins.then_inc(s_h1, 1)

            def convolve(step, tiles):
                for k in range(TAPS - 1):
                    for c in tiles:
                        ins = v.scalar_tensor_tensor(out=conv[:, c, :], in0=xpad[:, c, k:k + TOKENS],
                                                     scalar=cw[:, c, k:k + 1], in1=conv[:, c, :],
                                                     op0=ALU.mult, op1=ALU.add)
                    if k < TAPS - 2:
                        step(ins)
                return ins

            def ssm_slot(i, p, first, last):
                step = Chain(dve, s_conv_step, i, 2 * (TAPS - 2))
                dve.wait_ge(s_padbc, i + 1)
                convolve(step, [NCH - 1]).then_inc(s_convbc, 1)
                if not first:
                    gate_y(i - 1, 1 - p)
                dve.wait_ge(s_padx, i + 1)
                convolve(step, range(NCH - 1)).then_inc(s_convx, 1)
                step.close()
                if not first:
                    residual(i - 1)
                dve.wait_ge(s_xsT, i + 1)
                for j in range(2):
                    ins = v.tensor_tensor(dtx[:, p, j], ps[0:T, 3 + j, 0:D_INNER].rearrange("t (h d) -> t h d", h=HEADS),
                                          bc(tile(dt, i, j), HEAD), ALU.mult)
                dve.wait_ge(s_cb, i + 1)
                v.tensor_tensor(cbm[:], ps[0:T, 0, TOKENS:TOKENS + 3 * T].rearrange("s (k t) -> s k t", k=3),
                                causal[:], ALU.mult).then_inc(s_cbm, 1)
                dve.wait_ge(s_cbm, i + 1)
                dve.wait_ge(s_decay, i + 1)
                v.tensor_tensor(mix[:, p], decay[:], bc_at(cbm[:], 2, HEADS), ALU.mult).then_inc(s_mix, 1)

            run_slots(dve, ssm_slot)
            gate_y(IMAGES - 1, 1)
            residual(IMAGES - 1)

            def spread(step, src, s_var_):
                v.memset(spare[:], 0.0)
                v.bn_stats(stats[:, 0, :], src(0))
                step(v.bn_stats(stats[:, 1, :], src(1)))
                v.memset(spare[:], 0.0)
                v.bn_aggr(mv[:, 0, :], stats[:, 0, :])
                step(v.bn_aggr(mv[:, 1, :], stats[:, 1, :]))
                v.tensor_scalar_add(veps[:], mv[:, :, 1], EPS).then_inc(s_var_, 1)

            def normalise(src, dst, s_rstd_, count):
                dve.wait_ge(s_rstd_, count)
                for j in range(2):
                    ins = v.tensor_scalar(dst(j), src(j), mv[:, j, 0:1], rstd[:, j:j + 1], ALU.subtract, ALU.mult)
                return ins

            def enter(i, p):
                step = Chain(dve, s_ln_step, i, 5)
                spread(step, lambda j: tile(h, i, j), s_var1)
                step(normalise(lambda j: tile(h, i, j), lambda j: tile(u, i, j), s_rstd1, i * 2 + 1))
                spread(step, lambda j: tile(u, i, j), s_var1)
                normalise(lambda j: tile(u, i, j), lambda j: xh[:, p, j, :], s_rstd1, i * 2 + 2).then_inc(s_xh, 1)
                step.close()

            def maxima(i, r):
                step = Chain(dve, s_max_step, i * 3 + r, 1)
                dve.wait_ge(s_s, i * 3 + (r + 1))
                if r < 2:
                    sc = ps[0:T, 2 * r:2 * r + 2, 0:6 * T].rearrange("t b (c s) -> t b c s", c=2)
                    own, both = sc[:, :, :, 0:T], sc[:, :, :, T:3 * T]
                    top4 = smax[:, r].rearrange("t (b c) j -> t b c j", b=2)
                else:
                    own, both, top4 = ps[0:T, 0:4, 0:T], ps[0:T, 0:4, T:3 * T], smax[:, r]
                v.tensor_reduce(top4[..., 0], own, AX.X, ALU.max)
                step(v.tensor_reduce(top4[..., 1], both, AX.X, ALU.max))
                v.tensor_scalar(sneg[:, r], smax[:, r], -1.0, None, ALU.mult).then_inc(s_max, 1)

            def attended(m):
                step = Chain(dve, s_ao_step, m, 1)
                dve.wait_ge(s_sel, m + 1)
                step(v.reciprocal(rden[:].rearrange("p c t -> p (c t)"), ps[:, 4, 0:GROUPS * TOKENS]))
                v.tensor_tensor(att[:], pvs[:], rden[:], ALU.mult).then_inc(s_ao, 1)

            def after_attention(m, between=None):
                step = Chain(dve, s_x1_step, m, 5)
                dve.wait_ge(s_pr, m + 1)
                step(v.tensor_tensor(x1[:], ps[0:T, 4, 0:2 * D].rearrange("t (j d) -> t j d", j=2),
                                     bc_at(projb[:], 1, 2), ALU.add))
                v.tensor_tensor(x1[:], x1[:], imgs(u, m), ALU.add).then_inc(s_x1, 1)
                dve.wait_ge(s_x1, m + 1)
                spread(step, lambda j: x1[:, j, :], s_var2)
                if between:
                    between()
                step(normalise(lambda j: x1[:, j, :], lambda j: xh2[:, j, :], s_rstd2, m + 1))
                step(v.tensor_tensor(xh2[:], xh2[:], bc_at(ln2w[:], 1, 2), ALU.mult))
                dve.wait_ge(s_based, m * 32 + 16)
                v.tensor_tensor(x2[:], xh2[:], bc_at(ln2b[:], 1, 2), ALU.add).then_inc(s_x2, 1)
                step.close()

            def att_slot(i, p, first, last):
                if not last:
                    enter(i + 1, 1 - p)
                if not first:
                    attended(i - 1)
                maxima(i, 0)
                maxima(i, 1)
                dve.wait_ge(s_v, i + 1)
                v.tensor_tensor(vpad[:, :, :, 0:AHEAD],
                                ps[0:T, 7, 0:2 * D].rearrange("t (j h d) -> t j h d", j=2, d=AHEAD),
                                bc_at(vb[:], 1, 2).rearrange("t j (h d) -> t j h d", d=AHEAD), ALU.add).then_inc(s_vpad, 1)

                def last_maxima():
                    maxima(i, 2)
                    dve.wait_ge(s_pT, i * 3 + 2)
                    v.tensor_copy(probsT[:, 1].rearrange("s (b g) k t -> s b (g k t)", b=2), ps[0:T, 5:7, 0:6 * T]
                                  ).then_inc(s_pT1, 1)

                if first:
                    last_maxima()
                else:
                    after_attention(i - 1, last_maxima)

            dve.wait_ge(s_prep, 1)
            dve.wait_ge(s_part, 16 * NPART)
            dve.wait_ge(s_h1, IMAGES)
            enter(0, 0)
            run_slots(dve, att_slot)
            attended(IMAGES - 1)
            after_attention(IMAGES - 1)

            link = Chain(dve, s_r_step, 0, 99)
            dve.wait_ge(s_lgt, 1)
            link(v.tensor_copy(lg[:], ps[:, 2, 0:RT * EXPERTS].rearrange("t (j e) -> t j e", e=EXPERTS)))
            src = lg
            for k in range(2):
                link(v.tensor_reduce(top[:, k, :], src[:], AX.X, ALU.max))
                link(v.tensor_tensor(cand[:], src[:], bc(top[:, k, :], EXPERTS), ALU.is_equal))
                link(v.tensor_tensor(cand2[:], cand[:], revw[:], ALU.mult))
                link(v.tensor_reduce(pick[:, k, :], cand2[:], AX.X, ALU.max))
                link(v.tensor_tensor(hotb[:, k], revw[:], bc(pick[:, k, :], EXPERTS), ALU.is_equal))
                if k == 0:
                    link(v.scalar_tensor_tensor(out=lg2[:], in0=hotb[:, 0], scalar=-3e38, in1=lg[:],
                                                op0=ALU.mult, op1=ALU.add))
                    src = lg2
            v.tensor_tensor(pdiff[:], top[:, 1, :], top[:, 0, :], ALU.subtract).then_inc(s_pd, 1)
            dve.wait_ge(s_pre, 1)
            prev = ps[:, 0, 0:2 * RT * EXPERTS].rearrange("t (n e) -> t e n", e=EXPERTS)
            totv = ps[:, 1, 0:2 * RT * EXPERTS].rearrange("t (n e) -> t e n", e=EXPERTS)
            link(v.tensor_copy(tot[:], totv))
            link(v.tensor_tensor_scan(incl[:].rearrange("t e n -> t (e n)"), restart[:],
                                      tot[:].rearrange("t e n -> t (e n)"), 0.0, ALU.mult, ALU.add))
            link(v.tensor_tensor(before[:], incl[:], tot[:], ALU.subtract))
            link(v.tensor_tensor(before[:], before[:], prev, ALU.add))
            link(v.tensor_tensor(rankm[:], before[:].rearrange("t e n -> t n e"),
                                 hotb[:].rearrange("t k j e -> t (k j) e"), ALU.mult))
            link(v.tensor_reduce(rank[:], rankm[:], AX.X, ALU.add))
            v.tensor_scalar(late[:], rank[:], float(CAP), OUT_OF_RANGE, ALU.is_ge, ALU.mult)
            link(v.scalar_tensor_tensor(out=slotf[:], in0=pick[:].rearrange("t k j -> t (k j)"), scalar=-float(CAP),
                                        in1=rank[:], op0=ALU.mult, op1=ALU.add))
            link(v.scalar_tensor_tensor(out=slotf[:], in0=slotf[:], scalar=float(EXPERTS * CAP), in1=late[:],
                                        op0=ALU.add, op1=ALU.add))
            v.tensor_copy(slot[:], slotf[:]).then_inc(s_slot, 1)
            dve.wait_ge(s_pe, 1)
            link(v.tensor_scalar_add(psum1[:], pexp[:], 1.0))
            link(v.reciprocal(p1[:], psum1[:]))
            link(v.tensor_tensor(p2[:], p1[:], pexp[:], ALU.mult))
            v.tensor_tensor(g1[:], hotb[:, 0], bc(p1[:], EXPERTS), ALU.mult)
            link(v.tensor_tensor(g2[:], hotb[:, 1], bc(p2[:], EXPERTS), ALU.mult))
            v.tensor_tensor(xd[:, :, GATE0:GATE0 + EXPERTS], g1[:], g2[:], ALU.add).then_inc(s_gate, 1)

            def rows_out(e, p):
                dve.wait_ge(s_et, e + 1)
                for c in range(2):
                    ins = v.tensor_copy(xsT[:, p, c, :], ps[0:HALF, c, 0:CAP])
                ins.then_inc(s_ete, 1)

            rows_out(0, 0)
            metaf = meta[:].rearrange("s c n -> s (c n)")
            rows = meta[:, :, EXPERTS].bitcast(I32)
            dve.wait_ge(s_meta, 16)
            dve.wait_ge(s_moeb, 16)

            def exp_slot(e, p, first, last):
                if not last:
                    rows_out(e + 1, 1 - p)
                dve.wait_ge(s_og, e)
                dve.wait_ge(s_pj, e + 1)
                bias = pjb[:, bass.ds(e * D, D)]
                v.tensor_tensor(ob[:, 0:2, :], ps[0:CHUNK, 6, 0:2 * D].rearrange("s (c d) -> s c d", c=2),
                                bc_at(bias, 1, 2), ALU.add)
                v.tensor_tensor(ob[:, 2, :], ps[0:CHUNK, 7, 0:D], bias, ALU.add).then_inc(s_ob, 1)
                dve.wait_ge(s_ob, e + 1)
                dve.wait_ge(s_relay, e)
                v.tensor_copy(yrow[:, p, :], rows[:, bass.ds(e * 3, 3)])
                for c in range(3):
                    gate = metaf[:, bass.ds((e * 3 + c) * (EXPERTS + 1) + e, 1)]
                    ins = v.tensor_scalar(og[:, p, c, :], ob[:, c, :], gate, None, ALU.mult)
                ins.then_inc(s_og, 1)

            run_slots(dve, exp_slot)

        @block.tensor
        def _(pe):
            mm, tr = nc.tensor.matmul, nc.tensor.transpose
            pe.wait_ge(s_const, 1)

            for b in range(IMAGES):
                pe.wait_ge(s_q, 1 + b // 4)
                if b >= 2:
                    pe.wait_ge(s_h, b - 1)
                for j in range(2):
                    at = b * TOKENS + j * T
                    for c in range(2):
                        ins = mm(ps[0:T, 5 + b % 2, j * D:(j + 1) * D], xqT[:, c, at:at + T], wqT[:, c, :],
                                 start=c == 0, stop=c == 1)
                ins.then_inc(s_tok, 1)
            pe.wait_ge(s_par, 16 * NPAR)

            def time_steps(b):
                pe.wait_ge(s_hnTe, b + 1)
                for j in range(2 * b, 2 * b + 2):
                    for c in range(2):
                        ins = mm(ps[0:T, 3, j * HEADS:(j + 1) * HEADS], hnT[:, c, j * T:(j + 1) * T],
                                 win[:, c, D_PROJ - HEADS:D_PROJ], start=c == 0, stop=c == 1)
                return ins

            for b in range(IMAGES):
                pe.wait_ge(s_hn, 2 * b + 2)
                if b >= 2:
                    pe.wait_ge(s_hnTe, b - 1)
                for c in range(2):
                    for j in range(2):
                        at = c * TOKENS + j * T
                        ins = tr(ps[0:HALF, b % 2, at:at + T], hn[:, 2 * b + j, c * HALF:(c + 1) * HALF], ident[0:T, 0:T])
                ins.then_inc(s_hnT, 1)
                if b:
                    time_steps(b - 1)
            time_steps(IMAGES - 1).then_inc(s_dtp, 1)

            def project(done, bank, n, c0, m):
                for c in range(n):
                    w = (c0 + c) * 128
                    for k in range(2):
                        ins = mm(ps[:, bank, c * TOKENS:(c + 1) * TOKENS], win[:, k, w:w + 128],
                                 hnT[:, k, bass.ds(m * TOKENS, TOKENS)], start=k == 0, stop=k == 1)
                ins.then_inc(done, 1)

            def project_x(m):
                project(s_px, 1, 3, 3, m)

            def project_bc(m):
                project(s_pbc, 0, 1, 6, m)

            def scan(m, q):
                pe.wait_ge(s_mix, m + 1)
                for hd in range(HEADS):
                    r = slice(64 * (hd % 2), 64 * (hd % 2) + 64)
                    at = (hd // 2) * TOKENS
                    mm(ps[r, 3, at:at + TOKENS], dtx[:, q, 0, hd, :], mix[:, q, 0:2, hd, :], start=True, stop=False)
                    ins = mm(ps[r, 3, at + T:at + TOKENS], dtx[:, q, 1, hd, :], mix[:, q, 2, hd, :], start=False, stop=True)
                ins.then_inc(s_y, 1)

            def project_y(m):
                pe.wait_ge(s_yg, m + 1)
                for j in range(2):
                    for c in range(3):
                        mm(ps[0:T, 4, j * D:(j + 1) * D], yg[:, c, j * T:(j + 1) * T], wout[:, c, :],
                           start=c == 0, stop=c == 2)
                pe.wait_ge(s_ysq, m + 1)
                for j in range(2):
                    for c in range(3):
                        ins = mm(ps[0:T, 4, 400 + j:401 + j], ysq[:, c, j * T:(j + 1) * T], onecol[:, :],
                                 start=c == 0, stop=c == 2)
                ins.then_inc(s_wo, 1)

            def ssm_slot(i, p, first, last):
                if not first:
                    scan(i - 1, 1 - p)
                    pe.wait_ge(s_z, i)
                project(s_pz, 2, 3, 0, i)
                if not first:
                    project_y(i - 1)
                pe.wait_ge(s_amask, i + 1)
                if not first:
                    pe.wait_ge(s_decay, i)
                for k in range(3):
                    mm(ps[0:T, 5, 0:HEADS * T], r_gt_s[:], amask[:, k, 0], start=k == 0, stop=k == 2)
                for k in range(3):
                    mm(ps[0:T, 7, 0:HEADS * T], r_gt_s[:], amask[:, k, 1], start=k == 0, stop=k == 2)
                for k in range(3):
                    mm(ps[0:T, 6, 0:HEADS * T], r_gt_s[:],
                       amask[:, k, 0, :, T - 1:T].to_broadcast([T, HEADS, T]), start=k == 0, stop=False)
                for k in range(3):
                    ins = mm(ps[0:T, 6, 0:HEADS * T], onesb[0:T, 0:T], amask[:, k, 1], start=False, stop=k == 2)
                ins.then_inc(s_seg, 1)
                pe.wait_ge(s_xc, i + 1)
                if not first:
                    pe.wait_ge(s_h1, i)
                for j in range(2):
                    for c in range(3):
                        ins = tr(ps[0:T, 3 + j, c * 128:(c + 1) * 128], xc[:, p, c, j * T:(j + 1) * T], ident[:])
                ins.then_inc(s_xsT, 1)
                pe.wait_ge(s_cT, (i + 1) * 16)
                mm(ps[0:T, 0, TOKENS:2 * TOKENS], xc[0:STATE, p, 3, 0:T], cT[:, :], start=True, stop=True)
                mm(ps[0:T, 0, 2 * TOKENS:2 * TOKENS + T], xc[0:STATE, p, 3, T:TOKENS], cT[:, T:TOKENS],
                   start=True, stop=True).then_inc(s_cb, 1)
                if not last:
                    project_x(i + 1)
                    pe.wait_ge(s_cbm, i + 1)
                    project_bc(i + 1)

            project_x(0)
            project_bc(0)
            run_slots(pe, ssm_slot)
            scan(IMAGES - 1, 1)
            project_y(IMAGES - 1)

            pe.wait_ge(s_prep, 1)
            pe.wait_ge(s_part, 16 * NPART)
            pe.wait_ge(s_h1, IMAGES)

            def weight_sums(m):
                pe.wait_ge(s_pvs, m + 1)
                mm(ps[:, 4, 0:GROUPS * TOKENS], sumrow[:], pvs[:].rearrange("p c t -> p (c t)"), start=True, stop=True
                   ).then_inc(s_sel, 1)

            def att_project(m):
                pe.wait_ge(s_ao, m + 1)
                for j in range(2):
                    for c in range(GROUPS):
                        ins = mm(ps[0:T, 4, j * D:(j + 1) * D], att[:, c, j * T:(j + 1) * T], projw[:, c, :],
                                 start=c == 0, stop=c == GROUPS - 1)
                ins.then_inc(s_pr, 1)

            def enter_T(m, p):
                pe.wait_ge(s_xh, m + 1)
                for c in range(2):
                    for j in range(2):
                        at = c * TOKENS + j * T
                        ins = tr(ps[0:HALF, 4, at:at + T], xh[:, p, j, c * HALF:(c + 1) * HALF], ident[0:T, 0:T])
                ins.then_inc(s_xhT, 1)

            def router_T(m):
                pe.wait_ge(s_x2, m + 1)
                for c in range(2):
                    for j in range(2):
                        at = c * TOKENS + j * T
                        ins = tr(ps[0:HALF, 4, at:at + T], x2[:, j, c * HALF:(c + 1) * HALF], ident[0:T, 0:T])
                ins.then_inc(s_x2T, 1)

            def router(m):
                pe.wait_ge(s_x2Te, m + 1)
                for c in range(2):
                    ins = mm(ps[0:EXPERTS, 4, 2 * TOKENS:3 * TOKENS], wg[:, c, :], x2T[:, c, :], start=c == 0, stop=c == 1)
                ins.then_inc(s_lgp, 1)

            rounds = [[(2 * r + n // 2, n % 2) for n in range(4)] for r in range(2)] + [[(n, 2) for n in range(4)]]

            def att_slot(i, p, first, last):
                pe.wait_ge(s_xT, i + 1)
                if not first:
                    pe.wait_ge(s_pTe, i * 2)
                for k in range(2):
                    for c in range(GROUPS):
                        for f in range(2):
                            w = wqk[:, f, k, 4 * c:4 * c + 4, :].rearrange("p h d -> p (h d)")
                            ins = mm(ps[:, 5 + k, c * TOKENS:(c + 1) * TOKENS], w, xT[:, f, :], start=f == 0, stop=f == 1)
                    ins.then_inc(s_k1 if k else s_q1, 1)
                if not first:
                    weight_sums(i - 1)
                for j in range(2):
                    for f in range(2):
                        ins = mm(ps[0:T, 7, j * D:(j + 1) * D], xT[:, f, j * T:(j + 1) * T], wqkv[:, f, 2 * D:3 * D],
                                 start=f == 0, stop=f == 1)
                ins.then_inc(s_v, 1)
                def scores(r):
                    heads = 2 if r < 2 else 1
                    for bank in sorted({g for g, c in rounds[r]}):
                        mm(ps[0:T, bank, 0:heads * 3 * T].rearrange("t (c s) -> t c s", c=heads), identb[0:T, 0:T],
                           bc_at(maskneg[:].rearrange("t k s -> t (k s)"), 1, heads), start=True, stop=False)
                    for g, c in sorted(rounds[r], key=lambda head: head[1]):
                        quad = slice(PAD * g, PAD * g + PAD)
                        at = c * 3 * T if r < 2 else 0
                        mm(ps[0:T, g, at:at + T], qs[quad, c, 0:T], ks[quad, c, 0:T], start=False, stop=False)
                        ins = mm(ps[0:T, g, at + T:at + 3 * T], qs[quad, c, T:TOKENS], ks[quad, c, :],
                                 start=False, stop=heads == 1 or c == 1)
                    ins.then_inc(s_s, 1)

                def turn(r):
                    pe.wait_ge(s_exp, i * 3 + (r + 1))
                    if r == 1:
                        pe.wait_ge(s_pTe, i * 2 + 1)
                    if r == 2:
                        pe.wait_ge(s_pT1, i + 1)
                    for n in range(4):
                        for k in range(3):
                            at = ((n % 2) * 3 + k) * T
                            ins = tr(ps[0:T, 5 + n // 2, at:at + T], probs[:, r, n, k, :], ident[0:T, 0:T])
                    ins.then_inc(s_pT, 1)

                def weigh(r):
                    if r == 1:
                        pe.wait_ge(s_pT1, i + 1)
                    else:
                        pe.wait_ge(s_pTe, i * 2 + (2 if r else 1))
                    for g, c in sorted(rounds[r], key=lambda head: head[1]):
                        n = rounds[r].index((g, c))
                        quad = slice(PAD * g, PAD * g + PAD)
                        at = c * TOKENS
                        mm(ps[quad, 7, at:at + TOKENS], vpad[:, 0, 4 * c + g, :],
                           probsT[:, r, n, 0:2, :].rearrange("s k t -> s (k t)"), start=True, stop=False)
                        ins = mm(ps[quad, 7, at + T:at + TOKENS], vpad[:, 1, 4 * c + g, :], probsT[:, r, n, 2, :],
                                 start=False, stop=True)
                    if r == 2:
                        ins.then_inc(s_pv, 1)

                pe.wait_ge(s_qk, i + 1)
                if not first:
                    pe.wait_ge(s_exp, i * 3)
                scores(0)
                scores(1)
                if not first:
                    att_project(i - 1)
                turn(0)
                if not first:
                    pe.wait_ge(s_x1_step, i * 5 - 4)
                if not last:
                    enter_T(i + 1, 1 - p)
                pe.wait_ge(s_exp, i * 3 + 2)
                scores(2)
                pe.wait_ge(s_vpad, i + 1)
                weigh(0)
                turn(1)
                weigh(1)
                turn(2)
                if not last:
                    pe.wait_ge(s_xT, i + 2)
                if not first:
                    router_T(i - 1)
                weigh(2)
                if not first:
                    router(i - 1)

            enter_T(0, 0)
            run_slots(pe, att_slot)
            weight_sums(IMAGES - 1)
            att_project(IMAGES - 1)
            pe.wait_ge(s_x1, IMAGES)
            router_T(IMAGES - 1)
            router(IMAGES - 1)

            pe.wait_ge(s_lg, IMAGES)
            for j in range(RT):
                ins = tr(ps[:, 2, j * EXPERTS:(j + 1) * EXPERTS], lgT[:, j * 128:(j + 1) * 128], ident[0:EXPERTS, 0:EXPERTS])
            ins.then_inc(s_lgt, 1)
            pe.wait_ge(s_pd, 1)
            hot = hotb[:].rearrange("t k j e -> t (k j e)")
            mm(ps[:, 0, 0:2 * RT * EXPERTS], r_lt_t[:], hot, start=True, stop=True)
            mm(ps[:, 1, 0:2 * RT * EXPERTS], onesb[:], hot, start=True, stop=True).then_inc(s_pre, 1)

            def rows_in(e, p, n):
                pe.wait_ge(s_ex[p], n * 16)
                for c in range(2):
                    for k in range(3):
                        ins = tr(ps[0:HALF, c, k * CHUNK:(k + 1) * CHUNK], xs[:, p, k, c * HALF:(c + 1) * HALF],
                                 ident[0:CHUNK, 0:CHUNK])
                ins.then_inc(s_et, 1)

            pe.wait_ge(s_slot, 1)
            rows_in(0, 0, 1)

            def exp_slot(e, p, first, last):
                half = 1 if first else 4 if last else None
                n = half if half else (e + (1 if p else 2)) // 2
                pe.wait_ge(s_ew[p], n * 32)
                pe.wait_ge(s_ete, e + 1)
                for f in range(FT):
                    if not first or f > 3:
                        pe.wait_ge(s_gelu, e * FT + (f - 3))
                    for c in range(2):
                        ins = mm(ps[:, 2 + (2 * p + f) % 4, 0:CAP], fcw[:, p, c, f * 128:(f + 1) * 128], xsT[:, p, c, :],
                                 start=c == 0, stop=c == 1)
                    ins.then_inc(s_fc, 1)
                if not last:
                    rows_in(e + 1, 1 - p, 1 if first else (e + (3 if p else 2)) // 2)
                pe.wait_ge(s_gelu, e * FT + FT)
                pe.wait_ge(s_ob, e)
                for k in range(3):
                    for f in range(FT):
                        ins = mm(ps[0:CHUNK, 6 + k // 2, (k % 2) * D:(k % 2) * D + D],
                                 hid[:, f, k * CHUNK:(k + 1) * CHUNK], pjw[:, p, f, :], start=f == 0, stop=f == FT - 1)
                ins.then_inc(s_pj, 1)

            run_slots(pe, exp_slot)


def _layouts(v):
    import numpy as np

    g = {n: np.asarray(x) for n, x in v.items()}
    x, w = g.pop("x"), g.pop("L0_tok_w")
    g["patches"] = x.reshape(IMAGES, CHANNELS, GRID, PATCH, GRID, PATCH).transpose(1, 3, 5, 0, 2, 4).reshape(D, NTOK)
    g["patch_w"] = w.reshape(D, D).T
    g["conv_b"] = g.pop("L0_attn_conv_b").reshape(NCH, 128).T
    g["norm_w"] = g.pop("L0_attn_norm_w").reshape(3, 128).T
    g["d_skip"] = np.repeat(g.pop("L0_attn_D").reshape(3, 2).T, HEAD, axis=0)
    g["ln1_w"] = g.pop("L0_ffn_ln1_w").reshape(2, HALF).T
    g["ln1_b"] = g.pop("L0_ffn_ln1_b").reshape(2, HALF).T
    g["qk_b"] = g["L0_ffn_attn_qkv_b"][:2 * D].reshape(2, GROUPS, 4, AHEAD).transpose(2, 3, 0, 1)
    g["fc_b"] = g.pop("L0_ffn_exp_fc_b").reshape(EXPERTS * FT, 128).T
    return g


_INS = ["x", "L0_tok_w", "L0_tok_b", "L0_attn_W_in", "L0_attn_conv_w", "L0_attn_conv_b", "L0_attn_dt_bias",
        "L0_attn_A_log", "L0_attn_D", "L0_attn_norm_w", "L0_attn_W_out", "L0_ffn_ln1_w", "L0_ffn_ln1_b",
        "L0_ffn_ln2_w", "L0_ffn_ln2_b", "L0_ffn_attn_qkv_w", "L0_ffn_attn_qkv_b", "L0_ffn_attn_proj_w",
        "L0_ffn_attn_proj_b", "L0_ffn_w_g", "L0_ffn_exp_fc_w", "L0_ffn_exp_fc_b", "L0_ffn_exp_proj_w",
        "L0_ffn_exp_proj_b"]
_OUTS = [((IMAGES, TOKENS, D), "float32")]


def kernel(**inputs):
    import numpy as _np
    import concourse.bacc as _bacc
    from concourse import mybir as _mybir
    from concourse.bass_utils import run_bass_kernel_spmd as _run

    nc = _bacc.Bacc("TRN2", target_bir_lowering=False, num_devices=1)
    arrays, aps = {}, {}
    for name, x in _layouts({n: inputs[n] for n in _INS}).items():
        x = _np.ascontiguousarray(x)
        arrays[f"in_{name}_dram"] = x
        aps[name] = nc.dram_tensor(f"in_{name}_dram", x.shape, _mybir.dt.from_np(x.dtype), kind="ExternalInput").ap()
    shape, dtype = _OUTS[0]
    out = nc.dram_tensor("out_0_dram", shape, _mybir.dt.from_np(_np.dtype(dtype)), kind="ExternalOutput").ap()
    tower(nc, aps, out)
    r = _run(nc, [arrays], core_ids=[0])
    return r.results[0]["out_0_dram"]
```

```python
from contextlib import ExitStack

import concourse.bass as bass
from concourse import mybir

ALU = mybir.AluOpType
ACT = mybir.ActivationFunctionType
F32 = mybir.dt.float32
BF16 = mybir.dt.bfloat16
I32 = mybir.dt.int32
AX = mybir.AxisListType

IMAGES = 8
CHANNELS, SIDE, PATCH = 3, 96, 8
GRID = SIDE // PATCH
TOKENS = GRID * GRID
T = TOKENS // 2
TILES = 2 * IMAGES
D = 192
HALF = D // 2
NTOK = IMAGES * TOKENS
D_INNER = 2 * D
HEADS, HEAD = 6, 64
STATE = 64
NCH = (D_INNER + 2 * STATE) // 128
TAPS = 4
D_PROJ = 2 * D_INNER + 2 * STATE + HEADS
AHEADS, AHEAD = 12, 16
PAD = 32
GROUPS = AHEADS // 4
EXPERTS = 8
CAP = 360
CHUNK = CAP // 3
FF = 4 * D
FT = FF // 128
ROW = D + EXPERTS + 1
GATE0, TOKCOL = D, D + EXPERTS
SLOTS = EXPERTS * CAP
OUT_OF_RANGE = 8192.0
EPS = 1e-5
QMAX = 127.0
MAGIC = 12582912.0
RT = NTOK // 128
assert CAP == int(2 * 1.25 * NTOK // EXPERTS) and CAP % 2 == 0 and NTOK == TILES * T


def tower(nc, a, out):
    with ExitStack() as ctx:
        def sb(name, shape, dt=F32):
            return ctx.enter_context(nc.sbuf_tensor(name, shape, dt))

        def over(arena, at, shape, dt=F32):
            names = "abcdef"[:len(shape) - 1]
            size = 1
            for n in shape[1:]:
                size *= n
            end = at + (size if dt == F32 else size // 2)
            view = arena[0:shape[0], at:end]
            if dt != F32:
                view = view.bitcast(dt)
            return view.rearrange(f"p ({' '.join(names)}) -> p {' '.join(names)}", **dict(zip(names, shape[1:]))), end

        def sem(name):
            return ctx.enter_context(nc.semaphore(name))

        xslots = nc.dram_tensor("xslots", [SLOTS, ROW], F32, kind="Internal").ap()
        xrows = nc.dram_tensor("xrows", [NTOK, D], F32, kind="Internal").ap()
        ysum = nc.dram_tensor("ysum", [NTOK + CAP, D], F32, kind="Internal").ap()

        ps = ctx.enter_context(nc.psum_tensor("ps", [128, 8, 512], F32))

        arena_p = sb("arena_p", [128, 2 * GROUPS * 12 * T])
        xin, n = over(arena_p, 0, [HALF, 2, NTOK])
        rnd, _ = over(arena_p, n, [HALF, 2, NTOK])
        probs, n = over(arena_p, 0, [T, GROUPS, 4, 3, T])
        probsT, _ = over(arena_p, n, [T, GROUPS, 4, 3, T])
        hid, n = over(arena_p, 0, [128, FT, CAP])
        xsT, _ = over(arena_p, n, [HALF, 2, 2, CAP])
        arena_m = sb("arena_m", [128, 3 * 3 * HEADS * T])
        mix, n = over(arena_m, 0, [T, 2, 3, HEADS, T])
        decay, _ = over(arena_m, n, [T, 3, HEADS, T])
        fcw, _ = over(arena_m, 0, [HALF, 2, 2, FF])
        arena_x = sb("arena_x", [128, 2 * NCH * TOKENS + 2 * 2 * D_INNER])
        xc, n = over(arena_x, 0, [128, 2, NCH, TOKENS])
        dtx, _ = over(arena_x, n, [T, 2, 2, HEADS, HEAD])
        pjw, _ = over(arena_x, 0, [128, 2, FT, D])
        arena_q = sb("arena_q", [128, TILES * ROW])
        xqT, _ = over(arena_q, 0, [HALF, 2, NTOK], BF16)
        xd, _ = over(arena_q, 0, [128, RT, ROW])
        ident = sb("ident", [128, 128])
        identb = sb("identb", [128, 128], BF16)
        r_le_t = sb("r_le_t", [T, T], BF16)
        r_gt_s = sb("r_gt_s", [T, T], BF16)
        r_lt_t = sb("r_lt_t", [128, 128], BF16)
        onesb = sb("onesb", [128, 128], BF16)
        onecol = sb("onecol", [128, 1])
        sumrow = sb("sumrow", [128, 4])
        causal = sb("causal", [T, 3, T])
        maskneg = sb("maskneg", [T, 3, T], BF16)
        minus_half = sb("minus_half", [T, 4])
        revw = sb("revw", [128, RT, EXPERTS])
        restart = sb("restart", [128, EXPERTS * 2 * RT])
        win = sb("win", [HALF, 2, D_PROJ])
        cw = sb("cw", [128, NCH, TAPS])
        cb = sb("cb", [128, NCH])
        dtb = sb("dtb", [T, HEADS])
        alog = sb("alog", [T, HEADS])
        dskip = sb("dskip", [128, 3])
        normw = sb("normw", [128, 3])
        wout = sb("wout", [128, 3, D])
        ln1w = sb("ln1w", [HALF, 2])
        ln1b = sb("ln1b", [HALF, 2])
        ln2w = sb("ln2w", [T, D])
        ln2b = sb("ln2b", [T, D])
        wqkv = sb("wqkv", [HALF, 2, 3 * D])
        wqk = sb("wqk", [HALF, 2, 2, AHEADS, PAD])
        qkb = sb("qkb", [128, 2, GROUPS])
        vb = sb("vb", [T, D])
        projw = sb("projw", [128, GROUPS, D])
        projb = sb("projb", [T, D])
        wg = sb("wg", [HALF, 2, EXPERTS])
        tokb = sb("tokb", [T, D])
        fcb = sb("fcb", [128, EXPERTS * FT])
        pjb = sb("pjb", [CHUNK, EXPERTS * D])
        win_tok = sb("win_tok", [HALF, 2, D])
        rndw = sb("rndw", [HALF, 2 * D])
        wqT = sb("wqT", [HALF, 2, D], BF16)
        absmax = sb("absmax", [128, 2])
        absall = sb("absall", [128, 2])
        scales = sb("scales", [128, 2])
        inv = sb("inv", [128, 2])
        sxw = sb("sxw", [128, 1])
        h = sb("h", [T, TILES, D])
        hn = sb("hn", [T, TILES, D])
        u = hn
        stats_all = sb("stats_all", [T, TILES, 6])
        mv_all = sb("mv_all", [T, TILES, 2])
        veps_all = sb("veps_all", [T, TILES])
        rstd_all = sb("rstd_all", [T, TILES])
        hnT = sb("hnT", [HALF, 2, NTOK])
        stats = sb("stats", [T, 2, 6])
        spare = sb("spare", [1, 1])
        sparep = sb("sparep", [1, 1])
        mv = sb("mv", [T, 2, 2])
        veps = sb("veps", [T, 2])
        rstd = sb("rstd", [T, 2])
        dpre = sb("dpre", [T, TILES, HEADS])
        dabs = sb("dabs", [T, TILES, HEADS])
        dlost = sb("dlost", [T, TILES, HEADS])
        dpos = sb("dpos", [T, TILES, HEADS])
        donep = sb("donep", [T, TILES, HEADS])
        aexp = sb("aexp", [T, HEADS])
        dexp = sb("dexp", [T, TILES, HEADS])
        dlog = sb("dlog", [T, TILES, HEADS])
        dt = sb("dt", [T, TILES, HEADS])
        amat = sb("amat", [T, TILES, HEADS])
        arest = sb("arest", [T, TILES, HEADS])
        asplit = sb("asplit", [T, 3, TILES, HEADS], BF16)
        xpad = sb("xpad", [128, NCH, TAPS - 1 + TOKENS])
        conv = sb("conv", [128, NCH, TOKENS])
        cT = sb("cT", [STATE, TOKENS])
        sz = sb("sz", [128, 2, 3, TOKENS])
        amask = sb("amask", [T, 3, 2, HEADS, T], BF16)
        cbm = sb("cbm", [T, 3, T])
        yg = sb("yg", [128, 3, TOKENS])
        ysq = sb("ysq", [128, 3, TOKENS])
        msq = sb("msq", [T, 2])
        rms = sb("rms", [T, 2])
        xh = sb("xh", [T, 2, 2, D])
        xT = sb("xT", [HALF, 2, TOKENS])
        qs = sb("qs", [128, GROUPS, TOKENS])
        ks = sb("ks", [128, GROUPS, TOKENS])
        vpad = sb("vpad", [T, 2, AHEADS, PAD])
        smax = sb("smax", [T, 3, 4, 2])
        sneg = sb("sneg", [T, 3, 4, 2])
        rsum = sb("rsum", [T, 2, GROUPS, 4])
        rwide = sb("rwide", [T, 2, GROUPS, 4, PAD])
        pvs = yg
        att = ysq
        x1 = sb("x1", [T, 2, D])
        xh2 = sb("xh2", [T, 2, D])
        x2 = sb("x2", [T, 2, D])
        x2T = sb("x2T", [HALF, 2, TOKENS])
        base = sb("base", [T, 2, D])
        lg = sb("lg", [128, RT, EXPERTS])
        lgT = hnT[0:EXPERTS, 0, :]
        top = sb("top", [128, 2, RT])
        cand = sb("cand", [128, RT, EXPERTS])
        cand2 = sb("cand2", [128, RT, EXPERTS])
        lg2 = sb("lg2", [128, RT, EXPERTS])
        pick = sb("pick", [128, 2, RT])
        hotb = sb("hotb", [128, 2, RT, EXPERTS], BF16)
        tot = sb("tot", [128, EXPERTS, 2 * RT])
        incl = sb("incl", [128, EXPERTS, 2 * RT])
        before = sb("before", [128, EXPERTS, 2 * RT])
        rankm = sb("rankm", [128, 2 * RT, EXPERTS])
        rank = sb("rank", [128, 2 * RT])
        late = sb("late", [128, 2 * RT])
        slotf = sb("slotf", [128, 2 * RT])
        slot = sb("slot", [128, 2 * RT], I32)
        pdiff = sb("pdiff", [128, RT])
        pexp = sb("pexp", [128, RT])
        psum1 = sb("psum1", [128, RT])
        p1 = sb("p1", [128, RT])
        p2 = sb("p2", [128, RT])
        g1 = sb("g1", [128, RT, EXPERTS])
        g2 = sb("g2", [128, RT, EXPERTS])
        fill = sb("fill", [CHUNK, 3, ROW])
        xs = sb("xs", [CHUNK, 2, 3, D])
        meta = sb("meta", [CHUNK, 3 * EXPERTS, EXPERTS + 1])
        yrow = sb("yrow", [CHUNK, 2, 3], I32)
        ob = sb("ob", [CHUNK, 3, D])
        og = sb("og", [CHUNK, 2, 3, D])

        s_x = sem("s_x")
        s_w = sem("s_w")
        s_wt = sem("s_wt")
        s_par = sem("s_par")
        s_part = sem("s_part")
        s_moeb = sem("s_moeb")
        s_fillx = sem("s_fillx")
        s_const = sem("s_const")
        s_padb = sem("s_padb")
        s_prep = sem("s_prep")
        s_absmax = sem("s_absmax")
        s_absall = sem("s_absall")
        s_rnd = sem("s_rnd")
        s_q = sem("s_q")
        s_tok = sem("s_tok")
        s_h = sem("s_h")
        s_var = sem("s_var")
        s_rstd = sem("s_rstd")
        s_hn = sem("s_hn")
        s_hnT = sem("s_hnT")
        s_hnTe = sem("s_hnTe")
        s_a0 = sem("s_a0")
        s_dtp = sem("s_dtp")
        s_dabs = sem("s_dabs")
        s_dexp = sem("s_dexp")
        s_donep = sem("s_donep")
        s_dlog = sem("s_dlog")
        s_aexp = sem("s_aexp")
        s_as = sem("s_as")
        s_px = sem("s_px")
        s_pbc = sem("s_pbc")
        s_pz = sem("s_pz")
        s_padx = sem("s_padx")
        s_padbc = sem("s_padbc")
        s_convx = sem("s_convx")
        s_convbc = sem("s_convbc")
        s_xc = sem("s_xc")
        s_bc = sem("s_bc")
        s_cT = sem("s_cT")
        s_z = sem("s_z")
        s_amask = sem("s_amask")
        s_seg = sem("s_seg")
        s_seg_own = sem("s_seg_own")
        s_decay = sem("s_decay")
        s_xsT = sem("s_xsT")
        s_cb = sem("s_cb")
        s_cbm = sem("s_cbm")
        s_mix = sem("s_mix")
        s_y = sem("s_y")
        s_yg = sem("s_yg")
        s_ysq = sem("s_ysq")
        s_wo = sem("s_wo")
        s_ssq = sem("s_ssq")
        s_msq = sem("s_msq")
        s_rms = sem("s_rms")
        s_h1 = sem("s_h1")
        s_conv_step = sem("s_conv_step")
        s_y_step = sem("s_y_step")
        s_var1 = sem("s_var1")
        s_rstd1 = sem("s_rstd1")
        s_xh = sem("s_xh")
        s_xhT = sem("s_xhT")
        s_xT = sem("s_xT")
        s_q1 = sem("s_q1")
        s_k1 = sem("s_k1")
        s_qk = sem("s_qk")
        s_v = sem("s_v")
        s_vpad = sem("s_vpad")
        s_s = sem("s_s")
        s_max = sem("s_max")
        s_exp = sem("s_exp")
        s_pT = sem("s_pT")
        s_pTe = sem("s_pTe")
        s_pv = sem("s_pv")
        s_ao = sem("s_ao")
        s_pvs = sem("s_pvs")
        s_sum = sem("s_sum")
        s_rsum = sem("s_rsum")
        s_rwide = sem("s_rwide")
        s_rT = sem("s_rT")
        s_pr = sem("s_pr")
        s_x1 = sem("s_x1")
        s_base = sem("s_base")
        s_based = sem("s_based")
        s_var2 = sem("s_var2")
        s_rstd2 = sem("s_rstd2")
        s_x2 = sem("s_x2")
        s_xd = sem("s_xd")
        s_x2T = sem("s_x2T")
        s_x2Te = sem("s_x2Te")
        s_lgp = sem("s_lgp")
        s_lg = sem("s_lg")
        s_lgt = sem("s_lgt")
        s_ln_step = sem("s_ln_step")
        s_max_step = sem("s_max_step")
        s_x1_step = sem("s_x1_step")
        s_pre = sem("s_pre")
        s_slot = sem("s_slot")
        s_pd = sem("s_pd")
        s_pe = sem("s_pe")
        s_gate = sem("s_gate")
        s_r_step = sem("s_r_step")
        s_scat = sem("s_scat")
        s_meta = sem("s_meta")
        s_et = sem("s_et")
        s_ete = sem("s_ete")
        s_fc = sem("s_fc")
        s_gelu = sem("s_gelu")
        s_pj = sem("s_pj")
        s_ob = sem("s_ob")
        s_og = sem("s_og")
        s_add = sem("s_add")
        s_out = sem("s_out")
        s_tokcol = sem("s_tokcol")
        s_relay = sem("s_relay")
        s_ew = [sem("s_ew0"), sem("s_ew1")]
        s_ex = [sem("s_ex0"), sem("s_ex1")]

        def bc(ap, n):
            return ap.unsqueeze(len(ap.shape)).to_broadcast(list(ap.shape) + [n])

        def bc_at(ap, at, n):
            v = ap.unsqueeze(at)
            s = list(v.shape)
            s[at] = n
            return v.to_broadcast(s)

        def imgs(t, i):
            return t[:, bass.ds(i * 2, 2), :]

        def tile(t, i, j):
            return t[:, bass.ds(i * 2 + j, 1), :].rearrange("t o d -> t (o d)")

        def run_slots(eng, slot):
            slot(0, 0, True, False)
            with eng.Fori(1, IMAGES - 2, 2) as i:
                slot(i, 1, False, False)
                slot(i + 1, 0, False, False)
            slot(7, 1, False, True)

        def run_att_slots(eng, slot):
            slot(0, 0, 0, False)
            slot(1, 1, 1, False)
            with eng.Fori(2, IMAGES - 3, 2) as i:
                slot(i, 0, 2, False)
                slot(i + 1, 1, 2, False)
            slot(6, 0, 2, False)
            slot(7, 1, 2, True)

        class Chain:

            def __init__(self, eng, s, i, per):
                self.eng, self.s, self.i, self.per, self.n = eng, s, i, per, 0

            def __call__(self, ins):
                self.n += 1
                ins.then_inc(self.s, 1)
                self.eng.wait_ge(self.s, self.i * self.per + self.n)

            def close(self):
                assert self.n == self.per, (self.n, self.per)

        block = ctx.enter_context(nc.Block())
        NPAR, NPART = 6, 14

        @block.sync
        def _(sp):
            def load(dst, src, s):
                sp.dma_start(dst, src).then_inc(s, 16)

            for c in range(2):
                load(xin[:, c, 0:NTOK // 2], a["patches"][c * HALF:(c + 1) * HALF, 0:NTOK // 2], s_x)
            load(win[:], a["L0_attn_W_in"].rearrange("(c p) n -> p c n", p=HALF), s_par)
            load(cw[:], a["L0_attn_conv_w"].rearrange("(c p) k -> p c k", p=128), s_par)
            load(cb[:], a["conv_b"], s_par)
            load(dskip[:], a["d_skip"], s_par)
            load(normw[:], a["norm_w"], s_par)
            load(wout[:], a["L0_attn_W_out"].rearrange("(c p) n -> p c n", p=128), s_par)
            load(wqkv[:], a["L0_ffn_attn_qkv_w"].rearrange("(c p) n -> p c n", p=HALF), s_part)
            sp.wait_ge(s_const, 1)
            load(ysum[NTOK:NTOK + CAP, :].rearrange("(c p) d -> p c d", p=CHUNK), fill[:, :, 0:D], s_based)
            sp.wait_ge(s_padb, 1)
            for g in range(4):
                load(qkb[PAD * g:PAD * g + AHEAD, :, :], a["qk_b"][g], s_part)
                load(projw[PAD * g:PAD * g + AHEAD, :, :],
                     a["L0_ffn_attn_proj_w"].rearrange("(c g r) n -> g r c n", g=4, r=AHEAD)[g], s_part)
            load(ln1w[:], a["ln1_w"], s_part)
            load(ln1b[:], a["ln1_b"], s_part)
            load(fcb[:], a["fc_b"], s_part)
            load(wg[:], a["L0_ffn_w_g"].rearrange("(c p) n -> p c n", p=HALF), s_part)
            load(vb[:], a["L0_ffn_attn_qkv_b"][2 * D:3 * D].rearrange("(o d) -> o d", o=1).to_broadcast([T, D]), s_part)
            load(pjb[:], a["L0_ffn_exp_proj_b"].rearrange("e o d -> o (e d)").to_broadcast([CHUNK, EXPERTS * D]), s_moeb)

            def load_weights(e, p):
                load(fcw[:, p, :, :], a["L0_ffn_exp_fc_w"][e].rearrange("(c p) f -> p c f", p=HALF), s_ew[p])
                load(pjw[:, p, :, :], a["L0_ffn_exp_proj_w"][e].rearrange("(f p) d -> p f d", p=128), s_ew[p])

            with sp.Fori(0, IMAGES - 1, 2) as i:
                for p in range(2):
                    sp.wait_ge(s_bc, i + p + 1)
                    load(cT[:, :], xc[STATE:128, p, NCH - 1, :], s_cT)

            sp.wait_ge(s_wo, IMAGES)
            load_weights(0, 0)
            load_weights(1, 1)

            with sp.Fori(0, IMAGES - 1, 2) as i:
                for p in range(2):
                    sp.wait_ge(s_base, i + p + 1)
                    load(ysum[bass.ds((i + p) * TOKENS, TOKENS), :].rearrange("(j t) d -> t j d", t=T), base[:], s_based)
                    sp.wait_ge(s_x2, i + p + 1)
                    load(xrows[bass.ds((i + p) * TOKENS, TOKENS), :].rearrange("(j t) d -> t j d", t=T), x2[:], s_based)
            sp.wait_ge(s_based, 16 * (2 * IMAGES + 1))
            load(xd[:, :, 0:D], xrows.rearrange("(n p) d -> p n d", p=128), s_xd)

            def load_rows(e, p):
                load(xs[:, p, :, :], xslots[bass.ds(e * CAP, CAP), 0:D].rearrange("(c p) n -> p c n", p=CHUNK), s_ex[p])

            sp.wait_ge(s_scat, 16 * 2 * RT)
            load_rows(0, 0)
            load_rows(1, 1)
            load(meta[:], xslots[:, D:ROW].rearrange("(c p) n -> p c n", p=CHUNK), s_meta)
            with sp.Fori(0, EXPERTS - 3, 2) as e:
                for p in range(2):
                    fw = a["L0_ffn_exp_fc_w"][bass.ds(e + (p + 2), 1)].rearrange("o (c p) f -> p (o c) f", p=HALF)
                    pw = a["L0_ffn_exp_proj_w"][bass.ds(e + (p + 2), 1)].rearrange("o (f p) d -> p (o f) d", p=128)
                    sp.wait_ge(s_et, e + p + 1)
                    load_rows(e + (p + 2), p)
                    sp.wait_ge(s_fc, (e + p + 1) * FT)
                    load(fcw[:, p, :, :], fw, s_ew[p])
                    sp.wait_ge(s_pj, e + p + 1)
                    load(pjw[:, p, :, :], pw, s_ew[p])
            sp.wait_ge(s_add, EXPERTS * 48)
            load(out.rearrange("b t d -> (b t) d"), ysum[0:NTOK, :], s_out)
            sp.wait_ge(s_out, 16)

        @block.scalar
        def _(act):
            def load(dst, src, s):
                act.dma_start(dst, src).then_inc(s, 16)

            act_f = nc.scalar.activation
            load(win_tok[:], a["patch_w"].rearrange("(c p) d -> p c d", p=HALF), s_wt)
            for c in range(2):
                load(xin[:, c, NTOK // 2:], a["patches"][c * HALF:(c + 1) * HALF, NTOK // 2:], s_x)
            for dst, name in ((tokb, "L0_tok_b"), (dtb, "L0_attn_dt_bias"), (alog, "L0_attn_A_log"),
                              (ln2w, "L0_ffn_ln2_w"), (ln2b, "L0_ffn_ln2_b"), (projb, "L0_ffn_attn_proj_b")):
                load(dst[:], a[name].rearrange("(o d) -> o d", o=1).to_broadcast(list(dst.shape)), s_w)
            act.wait_ge(s_w, 16 * 6)
            act_f(aexp[:], alog[:], ACT.Exp).then_inc(s_aexp, 1)

            act.wait_ge(s_rnd, 1)
            act_f(wqT[:].rearrange("p c k -> p (c k)"), rndw[:], ACT.Copy, bias=-MAGIC)
            for n in range(2):
                act.wait_ge(s_rnd, n + 1)
                at = slice(n * NTOK // 2, (n + 1) * NTOK // 2)
                act_f(xqT[:, :, at], rnd[:, :, at], ACT.Copy, bias=-MAGIC).then_inc(s_q, 1)
            for b in range(IMAGES):
                act.wait_ge(s_hnT, b + 1)
                act_f(hnT[:, :, b * TOKENS:(b + 1) * TOKENS],
                      ps[0:HALF, b % 2, 0:2 * TOKENS].rearrange("k (c t) -> k c t", c=2), ACT.Copy).then_inc(s_hnTe, 1)
            act.wait_ge(s_dabs, 1)
            act_f(dexp[:], dabs[:], ACT.Exp, scale=-1.0).then_inc(s_dexp, 1)
            act.wait_ge(s_donep, 1)
            act_f(dlog[:], donep[:], ACT.Ln).then_inc(s_dlog, 1)

            x_tiles, bc_tile = slice(0, NCH - 1), NCH - 1

            def last_tap(tiles, src):
                for c in tiles:
                    ins = act_f(conv[:, c, :], src(c), ACT.Identity, bias=cb[:, c:c + 1], scale=cw[:, c, TAPS - 1:])
                return ins

            def pad(m, first):
                act.wait_ge(s_px, m + 1)
                act_f(xpad[:, x_tiles, TAPS - 1:], ps[:, 1, 0:3 * TOKENS].rearrange("k (c t) -> k c t", c=3), ACT.Copy)
                act.wait_ge(s_pbc, m + 1)
                act_f(xpad[:, bc_tile, TAPS - 1:], ps[:, 0, 0:TOKENS], ACT.Copy)
                if not first:
                    act.wait_ge(s_xc, m)
                last_tap([bc_tile], lambda c: ps[:, 0, 0:TOKENS]).then_inc(s_padbc, 1)
                last_tap(range(NCH - 1), lambda c: ps[:, 1, c * TOKENS:(c + 1) * TOKENS]).then_inc(s_padx, 1)

            def mean_square(m):
                act.wait_ge(s_yg, m + 1)
                act_f(ysq[:], yg[:], ACT.Square).then_inc(s_ysq, 1)
                act.wait_ge(s_ssq, m + 1)
                act_f(msq[:], ps[0:T, 3, 432:434], ACT.Copy, bias=EPS, scale=1.0 / D_INNER).then_inc(s_msq, 1)

            def ssm_slot(i, p, first, last):
                act.wait_ge(s_convbc, i + 1)
                act_f(xc[:, p, bc_tile, :], conv[:, bc_tile, :], ACT.Silu).then_inc(s_bc, 1)
                act.wait_ge(s_pz, i + 1)
                act_f(sz[:, p, :, :].rearrange("k c t -> k (c t)"), ps[:, 2, 0:3 * TOKENS], ACT.Silu).then_inc(s_z, 1)
                if not first:
                    mean_square(i - 1)
                act.wait_ge(s_convx, i + 1)
                act_f(xc[:, p, x_tiles, :], conv[:, x_tiles, :], ACT.Silu).then_inc(s_xc, 1)
                act.wait_ge(s_seg_own, i + 1)
                act_f(decay[:, 0:3:2].rearrange("s k h t -> s k (h t)"), ps[0:T, 5:7, 0:HEADS * T], ACT.Exp)
                act.wait_ge(s_seg, i + 1)
                act_f(decay[:, 1].rearrange("s h t -> s (h t)"), ps[0:T, 7, 0:HEADS * T], ACT.Exp).then_inc(s_decay, 1)
                if not last:
                    pad(i + 1, False)

            pad(0, True)
            run_slots(act, ssm_slot)
            mean_square(IMAGES - 1)

            act.wait_ge(s_part, 16 * NPART)

            def enter_T(m, bank=4):
                act.wait_ge(s_xhT, m + 1)
                for c in range(2):
                    ins = act_f(xT[:, c, :], ps[0:HALF, bank, c * TOKENS:(c + 1) * TOKENS], ACT.Identity,
                                bias=ln1b[:, c:c + 1], scale=ln1w[:, c:c + 1])
                ins.then_inc(s_xT, 1)

            def queries(m):
                act.wait_ge(s_q1, m + 1)
                for c in range(GROUPS):
                    act_f(qs[:, c, :], ps[:, 4, c * TOKENS:(c + 1) * TOKENS], ACT.Identity, bias=qkb[:, 0, c:c + 1])

            def keys(m):
                act.wait_ge(s_k1, m + 1)
                for c in range(GROUPS):
                    ins = act_f(ks[:, c, :], ps[:, 0, c * TOKENS:(c + 1) * TOKENS], ACT.Identity, bias=qkb[:, 1, c:c + 1])
                ins.then_inc(s_qk, 1)

            def weighted(m):
                act.wait_ge(s_pv, m + 1)
                act_f(pvs[:].rearrange("p c t -> p (c t)"), ps[:, 7, 0:GROUPS * TOKENS], ACT.Copy).then_inc(s_pvs, 1)

            def att_x2(m):
                act.wait_ge(s_x2T, m + 1)
                act_f(x2T[:], ps[0:HALF, 3, 0:2 * TOKENS].rearrange("k (c t) -> k c t", c=2), ACT.Copy).then_inc(s_x2Te, 1)

            def logits(m):
                act.wait_ge(s_lgp, m + 1)
                act_f(lgT[:, bass.ds(m * TOKENS, TOKENS)], ps[0:EXPERTS, 3, 2 * TOKENS:3 * TOKENS], ACT.Copy).then_inc(s_lg, 1)

            def widen(m):
                act.wait_ge(s_rsum, m + 1)
                act_f(rwide[:].rearrange("t j c g d -> t (j c g) d"), bc(rsum[:].rearrange("t j c g -> t (j c g)"), PAD),
                      ACT.Copy).then_inc(s_rwide, 1)

            def att_slot(i, p, behind, last):
                if behind == 2:
                    att_x2(i - 2)
                if behind:
                    widen(i - 1)
                if behind == 2:
                    logits(i - 2)

                def weights(r, heads):
                    act.wait_ge(s_max, i * 4 + (r + 1))
                    for n in heads:
                        k = min(r, 2)
                        bank, at = (2 * k + n // 2, n % 2 * 3 * T) if k < 2 else (n, 0)
                        act_f(probs[:, k, n, 0, :], ps[0:T, bank, at:at + T], ACT.Exp, bias=sneg[:, k, n, 0:1])
                        ins = act_f(probs[:, k, n, 1:3, :].rearrange("t k s -> t (k s)"),
                                    ps[0:T, bank, at + T:at + 3 * T], ACT.Exp, bias=sneg[:, k, n, 1:2])
                    ins.then_inc(s_exp, 1)

                def turned(r):
                    act.wait_ge(s_pT, i * 3 + (r + 1))
                    act_f(probsT[:, r].rearrange("s (b g) k t -> s b (g k t)", b=2),
                          ps[0:T, 5:7, 0:6 * T], ACT.Copy).then_inc(s_pTe, 1)

                if not last:
                    enter_T(i + 1)
                weights(0, range(4))
                weights(1, range(4))
                turned(0)
                weights(2, range(2))
                turned(1)
                weights(3, range(2, 4))
                if not last:
                    queries(i + 1)
                turned(2)
                weighted(i)
                if not last:
                    keys(i + 1)

            enter_T(0, 5)
            queries(0)
            keys(0)
            run_att_slots(act, att_slot)
            widen(IMAGES - 1)
            for m in (IMAGES - 2, IMAGES - 1):
                att_x2(m)
                logits(m)

            act.wait_ge(s_pd, 1)
            act_f(pexp[:], pdiff[:], ACT.Exp).then_inc(s_pe, 1)

            def exp_slot(e, p, first, last):
                for f in range(FT):
                    if f == 0:
                        act.wait_ge(s_pj, e)
                    act.wait_ge(s_fc, e * FT + (f + 1))
                    act_f(hid[:, f, :], ps[:, 2 + (2 * p + f) % 4, 0:CAP], ACT.Gelu,
                          bias=fcb[:, bass.ds(e * FT + f, 1)]).then_inc(s_gelu, 1)

            run_slots(act, exp_slot)

        @block.gpsimd
        def _(pool):
            g = nc.gpsimd
            g.memset(ident[:], 0.0)
            g.memset(identb[:], 0.0)
            g.memset(r_le_t[:], 1.0)
            g.memset(r_gt_s[:], 1.0)
            g.memset(r_lt_t[:], 1.0)
            g.memset(causal[:], 1.0)
            g.memset(maskneg[:], 0.0)
            g.memset(restart[:], 1.0)
            g.memset(fill[:], 0.0)
            g.memset(onesb[:], 1.0)
            g.memset(onecol[:], 1.0)
            g.memset(minus_half[:], -0.5)
            g.memset(xpad[:, :, 0:TAPS - 1], 0.0)
            g.memset(vpad[:], 1.0)
            g.memset(wqk[:], 0.0)
            g.memset(projw[:], 0.0)
            g.memset(sumrow[:], 0.0)
            g.memset(qkb[:], 0.0).then_inc(s_padb, 1)
            pool.wait_ge(s_padb, 1)
            for m in (ident, identb):
                g.affine_select(out=m[:], in_=m[:], compare_op=ALU.not_equal, fill=1.0, base=0,
                                pattern=[[-1, 128]], channel_multiplier=1)
            g.affine_select(out=sumrow[:], in_=sumrow[:], compare_op=ALU.not_equal, fill=1.0, base=-AHEAD,
                            pattern=[[-PAD, 4]], channel_multiplier=1)
            g.affine_select(out=r_le_t[:], in_=r_le_t[:], compare_op=ALU.is_ge, fill=0.0, base=0,
                            pattern=[[1, T]], channel_multiplier=-1)
            g.affine_select(out=r_gt_s[:], in_=r_gt_s[:], compare_op=ALU.is_gt, fill=0.0, base=0,
                            pattern=[[-1, T]], channel_multiplier=1)
            g.affine_select(out=r_lt_t[:], in_=r_lt_t[:], compare_op=ALU.is_gt, fill=0.0, base=0,
                            pattern=[[1, 128]], channel_multiplier=-1)
            g.affine_select(out=causal[:, 0:3:2, :], in_=causal[:, 0:3:2, :], compare_op=ALU.is_ge, fill=0.0,
                            base=0, pattern=[[0, 2], [1, T]], channel_multiplier=-1)
            g.affine_select(out=maskneg[:, 0:3:2, :], in_=maskneg[:, 0:3:2, :], compare_op=ALU.is_ge, fill=-1e30,
                            base=0, pattern=[[0, 2], [-1, T]], channel_multiplier=1)
            g.affine_select(out=restart[:], in_=restart[:], compare_op=ALU.not_equal, fill=0.0,
                            base=0, pattern=[[0, EXPERTS], [1, 2 * RT]], channel_multiplier=0)
            for e in range(EXPERTS):
                g.memset(revw[:, :, e], float(EXPERTS - e))
            g.iota(fill[:, :, TOKCOL].bitcast(I32), pattern=[[CHUNK, 3]], base=NTOK, channel_multiplier=1
                   ).then_inc(s_const, 1)
            pool.wait_ge(s_const, 1)
            pool.wait_ge(s_absmax, 2)
            g.partition_all_reduce(absall[0:HALF, :], absmax[0:HALF, :], HALF, bass.bass_isa.ReduceOp.absmax
                                   ).then_inc(s_absall, 1)
            for e in range(EXPERTS):
                pool.dma_start(xslots[e * CAP:(e + 1) * CAP, :].rearrange("(c p) n -> p c n", p=CHUNK), fill[:]
                               ).then_inc(s_fillx, 16)
            for n in range(TILES // 4):
                pool.wait_ge(s_var, n + 1)
                four = slice(4 * n, 4 * n + 4)
                g.tensor_tensor(rstd_all[:, four], veps_all[:, four], minus_half[:], ALU.pow).then_inc(s_rstd, 1)
            pool.wait_ge(s_par, 16 * NPAR)
            g.tensor_tensor(wout[:], wout[:], bc(normw[:], D), ALU.mult)
            pool.wait_ge(s_part, 16 * NPART)
            scale = float(AHEAD) ** -0.5
            for k in range(2):
                for c in range(2):
                    src = wqkv[:, c, k * D:(k + 1) * D].rearrange("p (h d) -> p h d", d=AHEAD)
                    g.tensor_scalar(wqk[:, c, k, :, 0:AHEAD], src, 1.0 if k else scale, None, ALU.mult)
            g.tensor_scalar(qkb[:, 0, :], qkb[:, 0, :], scale, None, ALU.mult).then_inc(s_prep, 1)

            def pow_rms(m):
                pool.wait_ge(s_msq, m + 1)
                g.tensor_tensor(rms[:], msq[:], minus_half[:, 0:2], ALU.pow).then_inc(s_rms, 1)

            pool.wait_ge(s_as, 1)

            def ssm_slot(i, p, first, last):
                pool.wait_ge(s_seg, i)
                for k in range(3):
                    ins = g.tensor_tensor(amask[:, k], bc_at(bc_at(r_le_t[:], 1, HEADS), 1, 2),
                                          bc(asplit[:, k, bass.ds(i * 2, 2), :], T), ALU.mult)
                ins.then_inc(s_amask, 1)
                if not first:
                    pow_rms(i - 1)

            run_slots(pool, ssm_slot)
            def rstd_ln(i):
                for n in range(2):
                    pool.wait_ge(s_var1, i * 2 + (n + 1))
                    g.tensor_tensor(rstd[:], veps[:], minus_half[:, 0:2], ALU.pow).then_inc(s_rstd1, 1)

            def after_attention(m):
                pool.wait_ge(s_x1, m + 1)
                pool.wait_ge(s_based, m * 32 + 16)
                g.tensor_tensor(base[:], x1[:], imgs(h, m), ALU.add).then_inc(s_base, 1)
                pool.wait_ge(s_var2, m + 1)
                g.tensor_tensor(rstd[:], veps[:], minus_half[:, 0:2], ALU.pow).then_inc(s_rstd2, 1)

            rstd_ln(0)
            pow_rms(IMAGES - 1)
            g.iota(xd[:, :, TOKCOL].bitcast(I32), pattern=[[128, RT]], base=0, channel_multiplier=1).then_inc(s_tokcol, 1)

            def att_slot(i, p, behind, last):
                if not last:
                    rstd_ln(i + 1)
                if behind:
                    after_attention(i - 1)

            run_att_slots(pool, att_slot)
            after_attention(IMAGES - 1)

            pool.wait_ge(s_gate, 1)
            pool.wait_ge(s_slot, 1)
            pool.wait_ge(s_xd, 16)
            pool.wait_ge(s_tokcol, 1)
            pool.wait_ge(s_fillx, 16 * EXPERTS)
            for n in range(2 * RT):
                g.indirect_dma_start(out=xslots[:, :],
                                     out_offset=bass.IndirectOffsetOnAxis(ap=slot[:, n:n + 1], axis=0),
                                     in_=xd[:, n % RT, :], in_offset=None,
                                     bounds_check=SLOTS - 1, oob_is_err=False).then_inc(s_scat, 16)

            pool.wait_ge(s_based, 16 * (2 * IMAGES + 1))

            def exp_slot(e, p, first, last):
                pool.wait_ge(s_relay, e)
                pool.wait_ge(s_og, e + 1)
                pool.wait_ge(s_add, e * 48)
                g.tensor_tensor(sparep[:], onecol[0:1, :], onecol[0:1, :], ALU.mult).then_inc(s_relay, 1)
                for c in range(3):
                    g.indirect_dma_start(out=ysum[:, :],
                                         out_offset=bass.IndirectOffsetOnAxis(
                                             ap=yrow[:, p, c:c + 1], axis=0),
                                         in_=og[:, p, c, :], in_offset=None, compute_op=ALU.add).then_inc(s_add, 16)

            run_slots(pool, exp_slot)

        @block.vector
        def _(dve):
            v = nc.vector

            dve.wait_ge(s_wt, 16)
            v.tensor_reduce(absmax[0:HALF, 1:2], win_tok[:].rearrange("p j k -> p (j k)"), AX.X, ALU.max,
                            apply_absolute_value=True).then_inc(s_absmax, 1)
            dve.wait_ge(s_x, 16 * 4)
            v.tensor_reduce(absmax[0:HALF, 0:1], xin.rearrange("x c t -> x (c t)"), AX.X, ALU.max,
                            apply_absolute_value=True).then_inc(s_absmax, 1)
            dve.wait_ge(s_absall, 1)
            link = Chain(dve, s_a0, 0, 99)
            link(v.tensor_scalar(scales[0:HALF, :], absall[0:HALF, :], 1e-8, 1.0 / QMAX, ALU.max, ALU.mult))
            v.tensor_tensor(sxw[0:HALF, :], scales[0:HALF, 0:1], scales[0:HALF, 1:2], ALU.mult)
            link(v.reciprocal(inv[0:HALF, :], scales[0:HALF, :]))
            v.tensor_scalar(rndw[:], win_tok[:].rearrange("p j k -> p (j k)"), inv[0:HALF, 1:2], MAGIC, ALU.mult, ALU.add)
            for n in range(2):
                at = slice(n * NTOK // 2, (n + 1) * NTOK // 2)
                link(v.tensor_scalar(rnd[:, :, at], xin[:, :, at], inv[0:HALF, 0:1], MAGIC, ALU.mult, ALU.add))
                if n == 0:
                    v.tensor_scalar(rndw[:], rndw[:], MAGIC - QMAX, MAGIC + QMAX, ALU.max, ALU.min)
                v.tensor_scalar(rnd[:, :, at], rnd[:, :, at], MAGIC - QMAX, MAGIC + QMAX, ALU.max, ALU.min
                                ).then_inc(s_rnd, 1)

            def embed(b):
                dve.wait_ge(s_tok, b + 1)
                v.scalar_tensor_tensor(out=h[:, 2 * b:2 * b + 2, :],
                                       in0=ps[0:T, 5 + b % 2, 0:2 * D].rearrange("t (j d) -> t j d", j=2),
                                       scalar=sxw[0:T, :], in1=bc_at(tokb[:], 1, 2), op0=ALU.mult, op1=ALU.add
                                       ).then_inc(s_h, 1)

            def embedded_stats(b):
                dve.wait_ge(s_h, b + 1)
                for j in range(2 * b, 2 * b + 2):
                    ins = v.bn_stats(stats_all[:, j, :], h[:, j, :])
                return ins

            def spread_pair(n):
                for j in range(4 * n, 4 * n + 4):
                    ins = v.bn_aggr(mv_all[:, j, :], stats_all[:, j, :])
                link(ins)
                four = slice(4 * n, 4 * n + 4)
                v.tensor_scalar_add(veps_all[:, four], mv_all[:, four, 1], EPS).then_inc(s_var, 1)

            def normalise_pair(n):
                dve.wait_ge(s_rstd, n + 1)
                for j in range(4 * n, 4 * n + 4):
                    v.tensor_scalar(hn[:, j, :], h[:, j, :], mv_all[:, j, 0:1], rstd_all[:, j:j + 1],
                                    ALU.subtract, ALU.mult).then_inc(s_hn, 1)

            for b in range(IMAGES + 1):
                if b < IMAGES:
                    embed(b)
                if b:
                    ins = embedded_stats(b - 1)
                    if b % 2 == 0:
                        link(ins)
                        spread_pair(b // 2 - 1)
                        if b >= 4:
                            normalise_pair(b // 2 - 2)
            normalise_pair(IMAGES // 2 - 1)
            dve.wait_ge(s_dtp, 1)
            link(v.tensor_tensor(dpre[:], ps[0:T, 3, 0:TILES * HEADS].rearrange("t (j h) -> t j h", h=HEADS),
                                 bc_at(dtb[:], 1, TILES), ALU.add))
            link(v.tensor_scalar(dpos[:], dpre[:], 0.0, None, ALU.max))
            v.scalar_tensor_tensor(out=dabs[:], in0=dpos[:], scalar=2.0, in1=dpre[:], op0=ALU.mult, op1=ALU.subtract
                                   ).then_inc(s_dabs, 1)
            dve.wait_ge(s_dexp, 1)
            v.tensor_scalar_add(donep[:], dexp[:], 1.0).then_inc(s_donep, 1)
            dve.wait_ge(s_donep, 1)
            link(v.scalar_tensor_tensor(out=dlost[:], in0=donep[:], scalar=-1.0, in1=dexp[:],
                                        op0=ALU.add, op1=ALU.subtract))
            link(v.tensor_tensor(dpos[:], dpos[:], dlost[:], ALU.subtract))
            dve.wait_ge(s_dlog, 1)
            link(v.tensor_tensor(dt[:], dpos[:], dlog[:], ALU.add))
            dve.wait_ge(s_aexp, 1)
            link(v.scalar_tensor_tensor(out=amat[:], in0=dt[:], scalar=-1.0, in1=bc_at(aexp[:], 1, TILES),
                                        op0=ALU.mult, op1=ALU.mult))
            link(v.tensor_copy(asplit[:, 0], amat[:]))
            link(v.tensor_tensor(arest[:], amat[:], asplit[:, 0], ALU.subtract))
            link(v.tensor_copy(asplit[:, 1], arest[:]))
            link(v.tensor_tensor(arest[:], arest[:], asplit[:, 1], ALU.subtract))
            v.tensor_copy(asplit[:, 2], arest[:]).then_inc(s_as, 1)
            dve.wait_ge(s_par, 16 * NPAR)
            dve.wait_ge(s_const, 1)

            def gate_y(m, q):
                step = Chain(dve, s_y_step, m, 1)
                dve.wait_ge(s_y, m + 1)
                for c in range(3):
                    ins = v.scalar_tensor_tensor(out=yg[:, c, :], in0=xc[:, q, c, :], scalar=dskip[:, c:c + 1],
                                                 in1=ps[:, 3, c * TOKENS:(c + 1) * TOKENS], op0=ALU.mult, op1=ALU.add)
                step(ins)
                v.tensor_tensor(yg[:], yg[:], sz[:, q], ALU.mult).then_inc(s_yg, 1)

            def residual(m):
                dve.wait_ge(s_wo, m + 1)
                dve.wait_ge(s_rms, m + 1)
                for j in range(2):
                    ins = v.scalar_tensor_tensor(out=tile(h, m, j), in0=ps[0:T, 4, j * D:(j + 1) * D],
                                                 scalar=rms[:, j:j + 1], in1=tile(h, m, j), op0=ALU.mult, op1=ALU.add)
                ins.then_inc(s_h1, 1)

            def convolve(step, tiles):
                for k in range(TAPS - 1):
                    for c in tiles:
                        ins = v.scalar_tensor_tensor(out=conv[:, c, :], in0=xpad[:, c, k:k + TOKENS],
                                                     scalar=cw[:, c, k:k + 1], in1=conv[:, c, :],
                                                     op0=ALU.mult, op1=ALU.add)
                    if k < TAPS - 2:
                        step(ins)
                return ins

            def ssm_slot(i, p, first, last):
                step = Chain(dve, s_conv_step, i, 2 * (TAPS - 2))
                dve.wait_ge(s_padbc, i + 1)
                convolve(step, [NCH - 1]).then_inc(s_convbc, 1)
                if not first:
                    gate_y(i - 1, 1 - p)
                dve.wait_ge(s_padx, i + 1)
                convolve(step, range(NCH - 1)).then_inc(s_convx, 1)
                step.close()
                if not first:
                    residual(i - 1)
                dve.wait_ge(s_xsT, i + 1)
                for j in range(2):
                    ins = v.tensor_tensor(dtx[:, p, j], ps[0:T, 3 + j, 0:D_INNER].rearrange("t (h d) -> t h d", h=HEADS),
                                          bc(tile(dt, i, j), HEAD), ALU.mult)
                dve.wait_ge(s_cb, i + 1)
                v.tensor_tensor(cbm[:], ps[0:T, 0, TOKENS:TOKENS + 3 * T].rearrange("s (k t) -> s k t", k=3),
                                causal[:], ALU.mult).then_inc(s_cbm, 1)
                dve.wait_ge(s_cbm, i + 1)
                dve.wait_ge(s_decay, i + 1)
                v.tensor_tensor(mix[:, p], decay[:], bc_at(cbm[:], 2, HEADS), ALU.mult).then_inc(s_mix, 1)

            run_slots(dve, ssm_slot)
            def spread(step, src, s_var_):
                v.memset(spare[:], 0.0)
                v.bn_stats(stats[:, 0, :], src(0))
                step(v.bn_stats(stats[:, 1, :], src(1)))
                v.memset(spare[:], 0.0)
                v.bn_aggr(mv[:, 0, :], stats[:, 0, :])
                step(v.bn_aggr(mv[:, 1, :], stats[:, 1, :]))
                v.tensor_scalar_add(veps[:], mv[:, :, 1], EPS).then_inc(s_var_, 1)

            def normalise(src, dst, s_rstd_, count):
                dve.wait_ge(s_rstd_, count)
                for j in range(2):
                    ins = v.tensor_scalar(dst(j), src(j), mv[:, j, 0:1], rstd[:, j:j + 1], ALU.subtract, ALU.mult)
                return ins

            def enter(i, p, between=None, meanwhile=None):
                step = Chain(dve, s_ln_step, i, 5)
                spread(step, lambda j: tile(h, i, j), s_var1)
                if meanwhile:
                    meanwhile()
                step(normalise(lambda j: tile(h, i, j), lambda j: tile(u, i, j), s_rstd1, i * 2 + 1))
                if between:
                    between()
                spread(step, lambda j: tile(u, i, j), s_var1)
                normalise(lambda j: tile(u, i, j), lambda j: xh[:, p, j, :], s_rstd1, i * 2 + 2).then_inc(s_xh, 1)
                step.close()

            def maxima(i, r):
                step = Chain(dve, s_max_step, i * 4 + r, 1)
                dve.wait_ge(s_s, i * 4 + (r + 1))
                if r < 2:
                    sc = ps[0:T, 2 * r:2 * r + 2, 0:6 * T].rearrange("t b (c s) -> t b c s", c=2)
                    own, both = sc[:, :, :, 0:T], sc[:, :, :, T:3 * T]
                    top4, neg = smax[:, r].rearrange("t (b c) j -> t b c j", b=2), sneg[:, r]
                    flat = smax[:, r]
                else:
                    two = slice(2 * r - 4, 2 * r - 2)
                    own, both = ps[0:T, two, 0:T], ps[0:T, two, T:3 * T]
                    top4 = flat = smax[:, 2, two]
                    neg = sneg[:, 2, two]
                v.tensor_reduce(top4[..., 0], own, AX.X, ALU.max)
                step(v.tensor_reduce(top4[..., 1], both, AX.X, ALU.max))
                v.tensor_scalar(neg, flat, -1.0, None, ALU.mult).then_inc(s_max, 1)

            def sums(m):
                dve.wait_ge(s_sum, m + 1)
                v.reciprocal(rsum[:].rearrange("t j c g -> t (j c g)"), ps[0:T, 4, 0:2 * AHEADS]).then_inc(s_rsum, 1)

            def attended(m):
                dve.wait_ge(s_rT, m + 1)
                v.tensor_tensor(att[:].rearrange("p c t -> p (c t)"), pvs[:].rearrange("p c t -> p (c t)"),
                                ps[:, 4, 0:GROUPS * TOKENS], ALU.mult).then_inc(s_ao, 1)

            def after_attention(m, between=None):
                step = Chain(dve, s_x1_step, m, 5)
                dve.wait_ge(s_pr, m + 1)
                step(v.tensor_tensor(x1[:], ps[0:T, 4, 0:2 * D].rearrange("t (j d) -> t j d", j=2),
                                     bc_at(projb[:], 1, 2), ALU.add))
                v.tensor_tensor(x1[:], x1[:], imgs(u, m), ALU.add).then_inc(s_x1, 1)
                dve.wait_ge(s_x1, m + 1)
                if between:
                    between()
                spread(step, lambda j: x1[:, j, :], s_var2)
                step(normalise(lambda j: x1[:, j, :], lambda j: xh2[:, j, :], s_rstd2, m + 1))
                step(v.tensor_tensor(xh2[:], xh2[:], bc_at(ln2w[:], 1, 2), ALU.mult))
                dve.wait_ge(s_based, m * 32 + 16)
                v.tensor_tensor(x2[:], xh2[:], bc_at(ln2b[:], 1, 2), ALU.add).then_inc(s_x2, 1)
                step.close()

            def att_slot(i, p, behind, last):
                if last:
                    sums(i - 1)
                elif behind:
                    enter(i + 1, 1 - p, lambda: sums(i - 1))
                else:
                    enter(i + 1, 1 - p)
                if behind:
                    attended(i - 1)
                maxima(i, 0)
                maxima(i, 1)
                dve.wait_ge(s_v, i + 1)
                v.tensor_tensor(vpad[:, :, :, 0:AHEAD],
                                ps[0:T, 7, 0:2 * D].rearrange("t (j h d) -> t j h d", j=2, d=AHEAD),
                                bc_at(vb[:], 1, 2).rearrange("t j (h d) -> t j h d", d=AHEAD), ALU.add).then_inc(s_vpad, 1)


                def last_maxima():
                    maxima(i, 2)
                    maxima(i, 3)

                if behind:
                    after_attention(i - 1, last_maxima)
                else:
                    last_maxima()

            dve.wait_ge(s_prep, 1)
            dve.wait_ge(s_part, 16 * NPART)
            enter(0, 0, meanwhile=lambda: gate_y(IMAGES - 1, 1))
            residual(IMAGES - 1)
            run_att_slots(dve, att_slot)
            sums(IMAGES - 1)
            attended(IMAGES - 1)
            after_attention(IMAGES - 1)

            link = Chain(dve, s_r_step, 0, 99)
            dve.wait_ge(s_lgt, 1)
            link(v.tensor_copy(lg[:], ps[:, 2, 0:RT * EXPERTS].rearrange("t (j e) -> t j e", e=EXPERTS)))
            src = lg
            for k in range(2):
                link(v.tensor_reduce(top[:, k, :], src[:], AX.X, ALU.max))
                link(v.tensor_tensor(cand[:], src[:], bc(top[:, k, :], EXPERTS), ALU.is_equal))
                link(v.tensor_tensor(cand2[:], cand[:], revw[:], ALU.mult))
                link(v.tensor_reduce(pick[:, k, :], cand2[:], AX.X, ALU.max))
                link(v.tensor_tensor(hotb[:, k], revw[:], bc(pick[:, k, :], EXPERTS), ALU.is_equal))
                if k == 0:
                    link(v.scalar_tensor_tensor(out=lg2[:], in0=hotb[:, 0], scalar=-3e38, in1=lg[:],
                                                op0=ALU.mult, op1=ALU.add))
                    src = lg2
            v.tensor_tensor(pdiff[:], top[:, 1, :], top[:, 0, :], ALU.subtract).then_inc(s_pd, 1)
            dve.wait_ge(s_pre, 1)
            prev = ps[:, 0, 0:2 * RT * EXPERTS].rearrange("t (n e) -> t e n", e=EXPERTS)
            totv = ps[:, 1, 0:2 * RT * EXPERTS].rearrange("t (n e) -> t e n", e=EXPERTS)
            link(v.tensor_copy(tot[:], totv))
            link(v.tensor_tensor_scan(incl[:].rearrange("t e n -> t (e n)"), restart[:],
                                      tot[:].rearrange("t e n -> t (e n)"), 0.0, ALU.mult, ALU.add))
            link(v.tensor_tensor(before[:], incl[:], tot[:], ALU.subtract))
            link(v.tensor_tensor(before[:], before[:], prev, ALU.add))
            link(v.tensor_tensor(rankm[:], before[:].rearrange("t e n -> t n e"),
                                 hotb[:].rearrange("t k j e -> t (k j) e"), ALU.mult))
            link(v.tensor_reduce(rank[:], rankm[:], AX.X, ALU.add))
            v.tensor_scalar(late[:], rank[:], float(CAP), OUT_OF_RANGE, ALU.is_ge, ALU.mult)
            link(v.scalar_tensor_tensor(out=slotf[:], in0=pick[:].rearrange("t k j -> t (k j)"), scalar=-float(CAP),
                                        in1=rank[:], op0=ALU.mult, op1=ALU.add))
            link(v.scalar_tensor_tensor(out=slotf[:], in0=slotf[:], scalar=float(EXPERTS * CAP), in1=late[:],
                                        op0=ALU.add, op1=ALU.add))
            v.tensor_copy(slot[:], slotf[:]).then_inc(s_slot, 1)
            dve.wait_ge(s_pe, 1)
            link(v.tensor_scalar_add(psum1[:], pexp[:], 1.0))
            link(v.reciprocal(p1[:], psum1[:]))
            link(v.tensor_tensor(p2[:], p1[:], pexp[:], ALU.mult))
            v.tensor_tensor(g1[:], hotb[:, 0], bc(p1[:], EXPERTS), ALU.mult)
            link(v.tensor_tensor(g2[:], hotb[:, 1], bc(p2[:], EXPERTS), ALU.mult))
            v.tensor_tensor(xd[:, :, GATE0:GATE0 + EXPERTS], g1[:], g2[:], ALU.add).then_inc(s_gate, 1)

            def rows_out(e, p):
                dve.wait_ge(s_et, e + 1)
                for c in range(2):
                    ins = v.tensor_copy(xsT[:, p, c, :], ps[0:HALF, c, 0:CAP])
                ins.then_inc(s_ete, 1)

            rows_out(0, 0)
            metaf = meta[:].rearrange("s c n -> s (c n)")
            rows = meta[:, :, EXPERTS].bitcast(I32)
            dve.wait_ge(s_meta, 16)
            dve.wait_ge(s_moeb, 16)

            def exp_slot(e, p, first, last):
                if not last:
                    rows_out(e + 1, 1 - p)
                dve.wait_ge(s_og, e)
                dve.wait_ge(s_pj, e + 1)
                bias = pjb[:, bass.ds(e * D, D)]
                v.tensor_tensor(ob[:, 0:2, :], ps[0:CHUNK, 6, 0:2 * D].rearrange("s (c d) -> s c d", c=2),
                                bc_at(bias, 1, 2), ALU.add)
                v.tensor_tensor(ob[:, 2, :], ps[0:CHUNK, 7, 0:D], bias, ALU.add).then_inc(s_ob, 1)
                dve.wait_ge(s_ob, e + 1)
                dve.wait_ge(s_relay, e)
                v.tensor_copy(yrow[:, p, :], rows[:, bass.ds(e * 3, 3)])
                for c in range(3):
                    gate = metaf[:, bass.ds((e * 3 + c) * (EXPERTS + 1) + e, 1)]
                    ins = v.tensor_scalar(og[:, p, c, :], ob[:, c, :], gate, None, ALU.mult)
                ins.then_inc(s_og, 1)

            run_slots(dve, exp_slot)

        @block.tensor
        def _(pe):
            mm, tr = nc.tensor.matmul, nc.tensor.transpose
            pe.wait_ge(s_const, 1)

            for b in range(IMAGES):
                pe.wait_ge(s_q, 1 + b // 4)
                if b >= 2:
                    pe.wait_ge(s_h, b - 1)
                for j in range(2):
                    at = b * TOKENS + j * T
                    for c in range(2):
                        ins = mm(ps[0:T, 5 + b % 2, j * D:(j + 1) * D], xqT[:, c, at:at + T], wqT[:, c, :],
                                 start=c == 0, stop=c == 1)
                ins.then_inc(s_tok, 1)
            pe.wait_ge(s_par, 16 * NPAR)

            def time_steps(b):
                pe.wait_ge(s_hnTe, b + 1)
                for j in range(2 * b, 2 * b + 2):
                    for c in range(2):
                        ins = mm(ps[0:T, 3, j * HEADS:(j + 1) * HEADS], hnT[:, c, j * T:(j + 1) * T],
                                 win[:, c, D_PROJ - HEADS:D_PROJ], start=c == 0, stop=c == 1)
                return ins

            for b in range(IMAGES):
                pe.wait_ge(s_hn, 2 * b + 2)
                if b >= 2:
                    pe.wait_ge(s_hnTe, b - 1)
                for c in range(2):
                    for j in range(2):
                        at = c * TOKENS + j * T
                        ins = tr(ps[0:HALF, b % 2, at:at + T], hn[:, 2 * b + j, c * HALF:(c + 1) * HALF], ident[0:T, 0:T])
                ins.then_inc(s_hnT, 1)
                if b:
                    time_steps(b - 1)
            time_steps(IMAGES - 1).then_inc(s_dtp, 1)

            def project(done, bank, n, c0, m):
                for c in range(n):
                    w = (c0 + c) * 128
                    for k in range(2):
                        ins = mm(ps[:, bank, c * TOKENS:(c + 1) * TOKENS], win[:, k, w:w + 128],
                                 hnT[:, k, bass.ds(m * TOKENS, TOKENS)], start=k == 0, stop=k == 1)
                ins.then_inc(done, 1)

            def project_x(m):
                project(s_px, 1, 3, 3, m)

            def project_bc(m):
                project(s_pbc, 0, 1, 6, m)

            def scan(m, q):
                pe.wait_ge(s_mix, m + 1)
                for hd in range(HEADS):
                    r = slice(64 * (hd % 2), 64 * (hd % 2) + 64)
                    at = (hd // 2) * TOKENS
                    mm(ps[r, 3, at:at + TOKENS], dtx[:, q, 0, hd, :], mix[:, q, 0:2, hd, :], start=True, stop=False)
                    ins = mm(ps[r, 3, at + T:at + TOKENS], dtx[:, q, 1, hd, :], mix[:, q, 2, hd, :], start=False, stop=True)
                ins.then_inc(s_y, 1)

            def project_y(m):
                pe.wait_ge(s_yg, m + 1)
                for j in range(2):
                    for c in range(3):
                        ins = mm(ps[0:T, 4, j * D:(j + 1) * D], yg[:, c, j * T:(j + 1) * T], wout[:, c, :],
                                 start=c == 0, stop=c == 2)
                    if j == 0:
                        pe.wait_ge(s_ysq, m + 1)
                        for k in range(2):
                            for c in range(3):
                                ins = mm(ps[0:T, 3, 432 + k:433 + k], ysq[:, c, k * T:(k + 1) * T], onecol[:, :],
                                         start=c == 0, stop=c == 2)
                        ins.then_inc(s_ssq, 1)
                ins.then_inc(s_wo, 1)

            def ssm_slot(i, p, first, last):
                if not first:
                    scan(i - 1, 1 - p)
                    pe.wait_ge(s_z, i)
                project(s_pz, 2, 3, 0, i)
                if not first:
                    project_y(i - 1)
                pe.wait_ge(s_amask, i + 1)
                if not first:
                    pe.wait_ge(s_decay, i)
                for k in range(3):
                    mm(ps[0:T, 5, 0:HEADS * T], r_gt_s[:], amask[:, k, 0], start=k == 0, stop=k == 2)
                for k in range(3):
                    ins = mm(ps[0:T, 6, 0:HEADS * T], r_gt_s[:], amask[:, k, 1], start=k == 0, stop=k == 2)
                ins.then_inc(s_seg_own, 1)
                pe.wait_ge(s_xc, i + 1)
                if not first:
                    pe.wait_ge(s_h1, i)
                for j in range(2):
                    for c in range(3):
                        ins = tr(ps[0:T, 3 + j, c * 128:(c + 1) * 128], xc[:, p, c, j * T:(j + 1) * T], ident[:])
                ins.then_inc(s_xsT, 1)
                for k in range(3):
                    mm(ps[0:T, 7, 0:HEADS * T], r_gt_s[:],
                       amask[:, k, 0, :, T - 1:T].to_broadcast([T, HEADS, T]), start=k == 0, stop=False)
                for k in range(3):
                    ins = mm(ps[0:T, 7, 0:HEADS * T], onesb[0:T, 0:T], amask[:, k, 1], start=False, stop=k == 2)
                ins.then_inc(s_seg, 1)
                pe.wait_ge(s_cT, (i + 1) * 16)
                mm(ps[0:T, 0, TOKENS:2 * TOKENS], xc[0:STATE, p, 3, 0:T], cT[:, :], start=True, stop=True)
                mm(ps[0:T, 0, 2 * TOKENS:2 * TOKENS + T], xc[0:STATE, p, 3, T:TOKENS], cT[:, T:TOKENS],
                   start=True, stop=True).then_inc(s_cb, 1)
                if not last:
                    project_x(i + 1)
                    pe.wait_ge(s_cbm, i + 1)
                    project_bc(i + 1)

            project_x(0)
            project_bc(0)
            run_slots(pe, ssm_slot)
            scan(IMAGES - 1, 1)
            project_y(IMAGES - 1)

            pe.wait_ge(s_prep, 1)
            pe.wait_ge(s_part, 16 * NPART)
            pe.wait_ge(s_decay, IMAGES)

            def weight_sums(m):
                pe.wait_ge(s_pvs, m + 1)
                for j in range(2):
                    for c in range(GROUPS):
                        at = (j * GROUPS + c) * 4
                        ins = mm(ps[0:T, 4, at:at + 4], pvs[:, c, j * T:(j + 1) * T], sumrow[:], start=True, stop=True)
                ins.then_inc(s_sum, 1)

            def reciprocals_T(m):
                pe.wait_ge(s_rwide, m + 1)
                for c in range(GROUPS):
                    for j in range(2):
                        at = c * TOKENS + j * T
                        ins = tr(ps[:, 4, at:at + T], rwide[:, j, c].rearrange("t g d -> t (g d)"), ident[0:T, 0:T])
                ins.then_inc(s_rT, 1)

            def att_project(m):
                pe.wait_ge(s_ao, m + 1)
                for j in range(2):
                    for c in range(GROUPS):
                        ins = mm(ps[0:T, 4, j * D:(j + 1) * D], att[:, c, j * T:(j + 1) * T], projw[:, c, :],
                                 start=c == 0, stop=c == GROUPS - 1)
                ins.then_inc(s_pr, 1)

            def enter_T(m, p, bank=4):
                pe.wait_ge(s_xh, m + 1)
                for c in range(2):
                    for j in range(2):
                        at = c * TOKENS + j * T
                        ins = tr(ps[0:HALF, bank, at:at + T], xh[:, p, j, c * HALF:(c + 1) * HALF], ident[0:T, 0:T])
                ins.then_inc(s_xhT, 1)

            def router_T(m):
                pe.wait_ge(s_x2, m + 1)
                for c in range(2):
                    for j in range(2):
                        at = c * TOKENS + j * T
                        ins = tr(ps[0:HALF, 3, at:at + T], x2[:, j, c * HALF:(c + 1) * HALF], ident[0:T, 0:T])
                ins.then_inc(s_x2T, 1)

            def router(m):
                pe.wait_ge(s_x2Te, m + 1)
                for c in range(2):
                    ins = mm(ps[0:EXPERTS, 3, 2 * TOKENS:3 * TOKENS], wg[:, c, :], x2T[:, c, :], start=c == 0, stop=c == 1)
                ins.then_inc(s_lgp, 1)

            rounds = [[(2 * r + n // 2, n % 2) for n in range(4)] for r in range(2)] + [[(n, 2) for n in range(4)]]
            parts = rounds[:2] + [rounds[2][:2], rounds[2][2:]]

            def project_qk(k, bank):
                for c in range(GROUPS):
                    for f in range(2):
                        w = wqk[:, f, k, 4 * c:4 * c + 4, :].rearrange("p h d -> p (h d)")
                        ins = mm(ps[:, bank, c * TOKENS:(c + 1) * TOKENS], w, xT[:, f, :], start=f == 0, stop=f == 1)
                return ins

            def queries(m):
                pe.wait_ge(s_xT, m + 1)
                project_qk(0, 4).then_inc(s_q1, 1)

            def keys(m):
                project_qk(1, 0).then_inc(s_k1, 1)

            def att_slot(i, p, behind, last):
                if behind == 2:
                    pe.wait_ge(s_exp, i * 4)
                    router_T(i - 2)
                if behind:
                    weight_sums(i - 1)
                for j in range(2):
                    for f in range(2):
                        ins = mm(ps[0:T, 7, j * D:(j + 1) * D], xT[:, f, j * T:(j + 1) * T], wqkv[:, f, 2 * D:3 * D],
                                 start=f == 0, stop=f == 1)
                ins.then_inc(s_v, 1)
                if behind == 2:
                    router(i - 2)
                if behind:
                    reciprocals_T(i - 1)

                def scores(r):
                    heads = 2 if r < 2 else 1
                    for bank in sorted({g for g, c in parts[r]}):
                        blocks = ps[0:T, bank, 0:heads * 3 * T].rearrange("t (c k s) -> t c k s", c=heads, k=3)
                        mm(blocks[:, :, 0:3:2, :], identb[0:T, 0:T], bc_at(maskneg[:, 0:3:2, :], 1, heads),
                           start=True, stop=False)
                    for g, c in sorted(parts[r], key=lambda head: head[1]):
                        quad = slice(PAD * g, PAD * g + PAD)
                        at = c * 3 * T if r < 2 else 0
                        mm(ps[0:T, g, at:at + T], qs[quad, c, 0:T], ks[quad, c, 0:T], start=False, stop=False)
                        mm(ps[0:T, g, at + T:at + 2 * T], qs[quad, c, T:TOKENS], ks[quad, c, 0:T], start=False, stop=False)
                        ins = mm(ps[0:T, g, at + 2 * T:at + 3 * T], qs[quad, c, T:TOKENS], ks[quad, c, T:TOKENS],
                                 start=False, stop=heads == 1 or c == 1)
                    ins.then_inc(s_s, 1)

                def turn(r):
                    pe.wait_ge(s_exp, i * 4 + (r + 1 if r < 2 else 4))
                    if r:
                        pe.wait_ge(s_pTe, i * 3 + r)
                    for n in range(4):
                        for k in range(3):
                            at = ((n % 2) * 3 + k) * T
                            ins = tr(ps[0:T, 5 + n // 2, at:at + T], probs[:, r, n, k, :], ident[0:T, 0:T])
                    ins.then_inc(s_pT, 1)

                def weigh(r):
                    pe.wait_ge(s_pTe, i * 3 + (r + 1))
                    for g, c in sorted(rounds[r], key=lambda head: head[1]):
                        n = rounds[r].index((g, c))
                        quad = slice(PAD * g, PAD * g + PAD)
                        at = c * TOKENS
                        mm(ps[quad, 7, at:at + TOKENS], vpad[:, 0, 4 * c + g, :],
                           probsT[:, r, n, 0:2, :].rearrange("s k t -> s (k t)"), start=True, stop=False)
                        ins = mm(ps[quad, 7, at + T:at + TOKENS], vpad[:, 1, 4 * c + g, :], probsT[:, r, n, 2, :],
                                 start=False, stop=True)
                    if r == 2:
                        ins.then_inc(s_pv, 1)

                pe.wait_ge(s_qk, i + 1)
                if behind:
                    pe.wait_ge(s_exp, i * 4)
                scores(0)
                if not last:
                    if behind:
                        pe.wait_ge(s_ao, i)
                    enter_T(i + 1, 1 - p)
                if behind == 2:
                    pe.wait_ge(s_lg, i - 1)
                scores(1)
                if behind:
                    if not last:
                        pe.wait_ge(s_xT, i + 2)
                    att_project(i - 1)
                    pe.wait_ge(s_pTe, i * 3)
                turn(0)
                scores(2)
                pe.wait_ge(s_exp, i * 4 + 2)
                scores(3)
                turn(1)
                pe.wait_ge(s_vpad, i + 1)
                weigh(0)
                if not last:
                    if behind:
                        pe.wait_ge(s_x1_step, i * 5 - 4)
                    queries(i + 1)
                weigh(1)
                turn(2)
                if not last:
                    pe.wait_ge(s_exp, i * 4 + 3)
                    keys(i + 1)
                weigh(2)

            enter_T(0, 0, 5)
            pe.wait_ge(s_h1, IMAGES)
            queries(0)
            keys(0)
            run_att_slots(pe, att_slot)
            weight_sums(IMAGES - 1)
            reciprocals_T(IMAGES - 1)
            pe.wait_ge(s_exp, IMAGES * 4)
            router_T(IMAGES - 2)
            router(IMAGES - 2)
            att_project(IMAGES - 1)
            pe.wait_ge(s_lg, IMAGES - 1)
            router_T(IMAGES - 1)
            router(IMAGES - 1)

            pe.wait_ge(s_lg, IMAGES)
            for j in range(RT):
                ins = tr(ps[:, 2, j * EXPERTS:(j + 1) * EXPERTS], lgT[:, j * 128:(j + 1) * 128], ident[0:EXPERTS, 0:EXPERTS])
            ins.then_inc(s_lgt, 1)
            pe.wait_ge(s_pd, 1)
            hot = hotb[:].rearrange("t k j e -> t (k j e)")
            mm(ps[:, 0, 0:2 * RT * EXPERTS], r_lt_t[:], hot, start=True, stop=True)
            mm(ps[:, 1, 0:2 * RT * EXPERTS], onesb[:], hot, start=True, stop=True).then_inc(s_pre, 1)

            def rows_in(e, p, n):
                pe.wait_ge(s_ex[p], n * 16)
                for c in range(2):
                    for k in range(3):
                        ins = tr(ps[0:HALF, c, k * CHUNK:(k + 1) * CHUNK], xs[:, p, k, c * HALF:(c + 1) * HALF],
                                 ident[0:CHUNK, 0:CHUNK])
                ins.then_inc(s_et, 1)

            pe.wait_ge(s_slot, 1)
            rows_in(0, 0, 1)

            def exp_slot(e, p, first, last):
                half = 1 if first else 4 if last else None
                n = half if half else (e + (1 if p else 2)) // 2
                pe.wait_ge(s_ew[p], n * 32)
                pe.wait_ge(s_ete, e + 1)
                for f in range(FT):
                    if not first or f > 3:
                        pe.wait_ge(s_gelu, e * FT + (f - 3))
                    for c in range(2):
                        ins = mm(ps[:, 2 + (2 * p + f) % 4, 0:CAP], fcw[:, p, c, f * 128:(f + 1) * 128], xsT[:, p, c, :],
                                 start=c == 0, stop=c == 1)
                    ins.then_inc(s_fc, 1)
                if not last:
                    rows_in(e + 1, 1 - p, 1 if first else (e + (3 if p else 2)) // 2)
                pe.wait_ge(s_gelu, e * FT + FT)
                pe.wait_ge(s_ob, e)
                for k in range(3):
                    for f in range(FT):
                        ins = mm(ps[0:CHUNK, 6 + k // 2, (k % 2) * D:(k % 2) * D + D],
                                 hid[:, f, k * CHUNK:(k + 1) * CHUNK], pjw[:, p, f, :], start=f == 0, stop=f == FT - 1)
                ins.then_inc(s_pj, 1)

            run_slots(pe, exp_slot)


def _layouts(v):
    import numpy as np

    g = {n: np.asarray(x) for n, x in v.items()}
    x, w = g.pop("x"), g.pop("L0_tok_w")
    g["patches"] = x.reshape(IMAGES, CHANNELS, GRID, PATCH, GRID, PATCH).transpose(1, 3, 5, 0, 2, 4).reshape(D, NTOK)
    g["patch_w"] = w.reshape(D, D).T
    g["conv_b"] = g.pop("L0_attn_conv_b").reshape(NCH, 128).T
    g["norm_w"] = g.pop("L0_attn_norm_w").reshape(3, 128).T
    g["d_skip"] = np.repeat(g.pop("L0_attn_D").reshape(3, 2).T, HEAD, axis=0)
    g["ln1_w"] = g.pop("L0_ffn_ln1_w").reshape(2, HALF).T
    g["ln1_b"] = g.pop("L0_ffn_ln1_b").reshape(2, HALF).T
    g["qk_b"] = g["L0_ffn_attn_qkv_b"][:2 * D].reshape(2, GROUPS, 4, AHEAD).transpose(2, 3, 0, 1)
    g["fc_b"] = g.pop("L0_ffn_exp_fc_b").reshape(EXPERTS * FT, 128).T
    return g


_INS = ["x", "L0_tok_w", "L0_tok_b", "L0_attn_W_in", "L0_attn_conv_w", "L0_attn_conv_b", "L0_attn_dt_bias",
        "L0_attn_A_log", "L0_attn_D", "L0_attn_norm_w", "L0_attn_W_out", "L0_ffn_ln1_w", "L0_ffn_ln1_b",
        "L0_ffn_ln2_w", "L0_ffn_ln2_b", "L0_ffn_attn_qkv_w", "L0_ffn_attn_qkv_b", "L0_ffn_attn_proj_w",
        "L0_ffn_attn_proj_b", "L0_ffn_w_g", "L0_ffn_exp_fc_w", "L0_ffn_exp_fc_b", "L0_ffn_exp_proj_w",
        "L0_ffn_exp_proj_b"]
_OUTS = [((IMAGES, TOKENS, D), "float32")]


def kernel(**inputs):
    import numpy as _np
    import concourse.bacc as _bacc
    from concourse import mybir as _mybir
    from concourse.bass_utils import run_bass_kernel_spmd as _run

    nc = _bacc.Bacc("TRN2", target_bir_lowering=False, num_devices=1)
    arrays, aps = {}, {}
    for name, x in _layouts({n: inputs[n] for n in _INS}).items():
        x = _np.ascontiguousarray(x)
        arrays[f"in_{name}_dram"] = x
        aps[name] = nc.dram_tensor(f"in_{name}_dram", x.shape, _mybir.dt.from_np(x.dtype), kind="ExternalInput").ap()
    shape, dtype = _OUTS[0]
    out = nc.dram_tensor("out_0_dram", shape, _mybir.dt.from_np(_np.dtype(dtype)), kind="ExternalOutput").ap()
    tower(nc, aps, out)
    r = _run(nc, [arrays], core_ids=[0])
    return r.results[0]["out_0_dram"]
```
